# Optimizing a Trainium2 kernel written in Bass

```python
import numpy as np
import jax
import jax.numpy as jnp

def _softmax(x, axis=-1):
    return jax.nn.softmax(x, axis=axis)

def _gelu(x):
    return jax.nn.gelu(x, approximate=True)

def _silu(x):
    return jax.nn.silu(x)

def _sigmoid(x):
    return jax.nn.sigmoid(x)

def _layernorm(x, axis=-1, eps=1e-05):
    m = jnp.mean(x, axis=axis, keepdims=True)
    v = jnp.var(x, axis=axis, keepdims=True)
    return (x - m) / jnp.sqrt(v + eps)

def _scatter_add(tgt, idx, src, axis=0):
    return tgt.at[idx].add(src)

def _segment_sum(src, seg, n):
    return jax.ops.segment_sum(src, seg, n)
kernel_name = 'mk_decoder_preln_d1_seqx_r4_fae97a'

def setup_inputs(seed: int=0):
    np.random.seed(seed)
    _w = jnp.asarray

    def _rec_inputs():
        import jax
        import jax.numpy as jnp
        _rk = jax.random.key(seed)
        x = -0.0003929 + 0.9999 * jax.random.normal(jax.random.fold_in(_rk, 1), (32, 112, 256), jnp.float32)
        _lenS = 112 - jax.random.randint(jax.random.fold_in(_rk, 7), (32,), 0, max(1, 112 // 4) + 1, jnp.int32)
        _lenS2 = 375 - jax.random.randint(jax.random.fold_in(_rk, 8), (32,), 0, max(1, 375 // 4) + 1, jnp.int32)
        _ctx_1024P = jax.random.normal(jax.random.fold_in(_rk, 11), (32, 16, 256), jnp.float32)
        _ctx_1024c = jax.random.dirichlet(jax.random.fold_in(_rk, 511), 0.3 * jnp.ones((16,), jnp.float32), (32, 375))
        _ctx_1024t = jnp.einsum('bsk,bkd->bsd', _ctx_1024c, _ctx_1024P)
        _ctx_1024t = _ctx_1024t * jax.lax.rsqrt(jnp.mean(jnp.square(_ctx_1024t)) + 1e-12) * 0.953939
        ctx_1024 = -1.39393e-06 + 0.999914 * (_ctx_1024t + 0.3 * jax.random.normal(jax.random.fold_in(_rk, 611), (32, 375, 256), jnp.float32))
        return (x, ctx_1024)
    x, ctx_1024 = _rec_inputs()

    def _L0_attn_setup():
        import jax, jax.numpy as jnp
        import numpy as np
        NUM_HEADS = 1
        LN_EPS = 1e-05
        key = jax.random.key(seed)
        ks = jax.random.split(key, 4)
        B, L, D = (8, 1024, 256)
        x = jax.random.normal(ks[0], (B, L, D), dtype=jnp.float32)
        qkv_w = jax.random.normal(ks[1], (3 * D, D), dtype=jnp.float32) * np.float32(np.sqrt(1.0 / D))
        qkv_b = jnp.zeros((3 * D,), dtype=jnp.float32)
        proj_w = jax.random.normal(ks[2], (D, D), dtype=jnp.float32) * np.float32(np.sqrt(1.0 / D))
        proj_b = jnp.zeros((D,), dtype=jnp.float32)
        return {'x': x, 'norm_w': jnp.ones((D,), dtype=jnp.float32), 'norm_b': jnp.zeros((D,), dtype=jnp.float32), 'qkv_w': qkv_w, 'qkv_b': qkv_b, 'proj_w': proj_w, 'proj_b': proj_b}
    _L0_attn_all = _L0_attn_setup()
    _L0_attn_in = {k: v for k, v in _L0_attn_all.items() if k in ('norm_w', 'norm_b', 'qkv_w', 'qkv_b', 'proj_w', 'proj_b')}
    del _L0_attn_all

    def _L0_xattn_setup():
        import jax, jax.numpy as jnp
        import numpy as np
        B, C_LEN, Q_LEN, D = (8, 512, 128, 256)
        key = jax.random.key(seed)
        ks = jax.random.split(key, 10)
        scale = 1.0 / np.sqrt(D)
        return {'c': jax.random.normal(ks[0], (B, C_LEN, D), dtype=jnp.float32), 'q': jax.random.normal(ks[1], (B, Q_LEN, D), dtype=jnp.float32), 'w_cq': jax.random.normal(ks[2], (D,), dtype=jnp.float32) * scale, 'b_cq': jax.random.normal(ks[3], (), dtype=jnp.float32) * scale, 'w_c': jax.random.normal(ks[4], (D,), dtype=jnp.float32) * scale, 'b_c': jax.random.normal(ks[5], (), dtype=jnp.float32) * scale, 'w_q': jax.random.normal(ks[6], (D,), dtype=jnp.float32) * scale, 'b_q': jax.random.normal(ks[7], (), dtype=jnp.float32) * scale, 'W_l': jax.random.normal(ks[8], (D, 4 * D), dtype=jnp.float32) * (1.0 / np.sqrt(4 * D)), 'b_l': jax.random.normal(ks[9], (D,), dtype=jnp.float32) * (1.0 / np.sqrt(4 * D))}
    _L0_xattn_all = _L0_xattn_setup()
    _L0_xattn_in = {k: v for k, v in _L0_xattn_all.items() if k in ('w_cq', 'b_cq', 'w_c', 'b_c', 'w_q', 'b_q', 'W_l', 'b_l')}
    del _L0_xattn_all

    def _L0_ffn_setup():
        import jax, jax.numpy as jnp
        import numpy as np
        E, H, I = (8, 256, 128)
        NG, TKG, TOPK = (4, 2, 4)
        SCALE = 2.5

        def _mlp(x, wg, wu, wd):
            return jax.nn.silu(x @ wg) * (x @ wu) @ wd
        key = jax.random.key(seed)
        ks = jax.random.split(key, 8)
        s = 0.02
        return {'hidden_states': jax.random.normal(ks[0], (32, 64, H), jnp.float32), 'gate_w': jax.random.normal(ks[1], (E, H), jnp.float32) * np.float32(np.sqrt(2.0 / H)), 'correction_bias': jnp.zeros((E,), jnp.float32), 'Wg': jax.random.normal(ks[2], (E, H, I), jnp.float32) * s, 'Wu': jax.random.normal(ks[3], (E, H, I), jnp.float32) * s, 'Wd': jax.random.normal(ks[4], (E, I, H), jnp.float32) * s, 'Wg_s': jax.random.normal(ks[5], (H, I), jnp.float32) * s, 'Wu_s': jax.random.normal(ks[6], (H, I), jnp.float32) * s, 'Wd_s': jax.random.normal(ks[7], (I, H), jnp.float32) * s}
    _L0_ffn_all = _L0_ffn_setup()
    _L0_ffn_in = {k: v for k, v in _L0_ffn_all.items() if k in ('gate_w', 'correction_bias', 'Wg', 'Wu', 'Wd', 'Wg_s', 'Wu_s', 'Wd_s')}
    del _L0_ffn_all
    return {'x': x, 'ctx_1024': ctx_1024, 'L0_attn_norm_w': _L0_attn_in['norm_w'], 'L0_attn_norm_b': _L0_attn_in['norm_b'], 'L0_attn_qkv_w': _L0_attn_in['qkv_w'], 'L0_attn_qkv_b': _L0_attn_in['qkv_b'], 'L0_attn_proj_w': _L0_attn_in['proj_w'], 'L0_attn_proj_b': _L0_attn_in['proj_b'], 'L0_xattn_w_cq': _L0_xattn_in['w_cq'], 'L0_xattn_b_cq': _L0_xattn_in['b_cq'], 'L0_xattn_w_c': _L0_xattn_in['w_c'], 'L0_xattn_b_c': _L0_xattn_in['b_c'], 'L0_xattn_w_q': _L0_xattn_in['w_q'], 'L0_xattn_b_q': _L0_xattn_in['b_q'], 'L0_xattn_W_l': _L0_xattn_in['W_l'], 'L0_xattn_b_l': _L0_xattn_in['b_l'], 'L0_ffn_gate_w': _L0_ffn_in['gate_w'], 'L0_ffn_correction_bias': _L0_ffn_in['correction_bias'], 'L0_ffn_Wg': _L0_ffn_in['Wg'], 'L0_ffn_Wu': _L0_ffn_in['Wu'], 'L0_ffn_Wd': _L0_ffn_in['Wd'], 'L0_ffn_Wg_s': _L0_ffn_in['Wg_s'], 'L0_ffn_Wu_s': _L0_ffn_in['Wu_s'], 'L0_ffn_Wd_s': _L0_ffn_in['Wd_s']}

def reference(x, ctx_1024, L0_attn_norm_w, L0_attn_norm_b, L0_attn_qkv_w, L0_attn_qkv_b, L0_attn_proj_w, L0_attn_proj_b, L0_xattn_w_cq, L0_xattn_b_cq, L0_xattn_w_c, L0_xattn_b_c, L0_xattn_w_q, L0_xattn_b_q, L0_xattn_W_l, L0_xattn_b_l, L0_ffn_gate_w, L0_ffn_correction_bias, L0_ffn_Wg, L0_ffn_Wu, L0_ffn_Wd, L0_ffn_Wg_s, L0_ffn_Wu_s, L0_ffn_Wd_s):
    import jax
    import jax.numpy as jnp

    def _L0_attn_ref(x, norm_w, norm_b, qkv_w, qkv_b, proj_w, proj_b):
        import jax, jax.numpy as jnp
        import numpy as np
        NUM_HEADS = 1
        LN_EPS = 1e-05
        B, L, D = x.shape
        H = NUM_HEADS
        mu = jnp.mean(x, axis=-1, keepdims=True)
        var = jnp.mean(jnp.square(x - mu), axis=-1, keepdims=True)
        h = (x - mu) / jnp.sqrt(var + LN_EPS) * norm_w + norm_b
        qkv = h @ qkv_w.T + qkv_b
        qkv = qkv.reshape(B * H, L // H, 3, D)
        q, k, v = (qkv[..., 0, :], qkv[..., 1, :], qkv[..., 2, :])
        scale = np.float32(1.0 / np.sqrt(L // H))
        w = jax.nn.softmax(jnp.einsum('ncq,nck->nqk', q, k * scale), axis=2)
        a = jnp.einsum('nqk,nck->ncq', w, v)
        a = a.reshape(B, L, D)
        return a @ proj_w.T + proj_b + x

    def _L0_xattn_ref(c, q, w_cq, b_cq, w_c, b_c, w_q, b_q, W_l, b_l):
        import jax, jax.numpy as jnp
        import numpy as np
        B, C_LEN, Q_LEN, D = (8, 512, 128, 256)
        cq = jnp.einsum('bcd,bqd,d->bcq', c, q, w_cq) + b_cq
        s = (c @ w_c + b_c)[:, :, None] + (q @ w_q + b_q)[:, None, :] + cq
        a = jax.nn.softmax(s, axis=2)
        c2q_att = jnp.einsum('bcq,bqd->bcd', a, q)
        b_att = jax.nn.softmax(jnp.max(s, axis=2), axis=1)
        q2c_att = jnp.einsum('bc,bcd->bd', b_att, c)[:, None, :]
        x = jnp.concatenate([c, c2q_att, c * c2q_att, c * q2c_att], axis=-1)
        z = x @ W_l.T + b_l
        return z

    def _L0_ffn_ref(hidden_states, gate_w, correction_bias, Wg, Wu, Wd, Wg_s, Wu_s, Wd_s):
        import jax, jax.numpy as jnp
        import numpy as np
        E, H, I = (8, 256, 128)
        NG, TKG, TOPK = (4, 2, 4)
        SCALE = 2.5

        def _mlp(x, wg, wu, wd):
            return jax.nn.silu(x @ wg) * (x @ wu) @ wd
        B, T, _ = hidden_states.shape
        x = hidden_states.reshape(-1, H)
        N = x.shape[0]
        logits = x @ gate_w.T
        scores = jax.nn.sigmoid(logits)
        scores_c = scores + correction_bias
        grp = scores_c.reshape(N, NG, E // NG)
        group_scores = jnp.sum(jax.lax.top_k(grp, 2)[0], axis=-1)
        grp_idx = jax.lax.top_k(group_scores, TKG)[1]
        group_mask = jnp.zeros_like(group_scores).at[jnp.arange(N)[:, None], grp_idx].set(1.0)
        score_mask = jnp.repeat(group_mask, E // NG, axis=-1) > 0.5
        scores_for_choice = jnp.where(score_mask, scores_c, 0.0)
        topk_idx = jax.lax.top_k(scores_for_choice, TOPK)[1]
        topk_w = jnp.take_along_axis(scores, topk_idx, axis=-1)
        topk_w = topk_w / (jnp.sum(topk_w, axis=-1, keepdims=True) + 1e-20)
        topk_w = topk_w * SCALE
        cw = jnp.sum(jax.nn.one_hot(topk_idx, E, dtype=topk_w.dtype) * topk_w[..., None], axis=1)
        g = jnp.einsum('nh,ehi->eni', x, Wg)
        u = jnp.einsum('nh,ehi->eni', x, Wu)
        y = jnp.einsum('eni,eih->enh', jax.nn.silu(g) * u, Wd)
        routed = jnp.einsum('enh,ne->nh', y, cw)
        out = routed + _mlp(x, Wg_s, Wu_s, Wd_s)
        return out.reshape(B, T, H)
    x = x + _L0_attn_ref(_layernorm(x, axis=-1), L0_attn_norm_w, L0_attn_norm_b, L0_attn_qkv_w, L0_attn_qkv_b, L0_attn_proj_w, L0_attn_proj_b)
    x = x + _L0_xattn_ref(_layernorm(x, axis=-1), ctx_1024, L0_xattn_w_cq, L0_xattn_b_cq, L0_xattn_w_c, L0_xattn_b_c, L0_xattn_w_q, L0_xattn_b_q, L0_xattn_W_l, L0_xattn_b_l)
    x = x + _L0_ffn_ref(_layernorm(x, axis=-1), L0_ffn_gate_w, L0_ffn_correction_bias, L0_ffn_Wg, L0_ffn_Wu, L0_ffn_Wd, L0_ffn_Wg_s, L0_ffn_Wu_s, L0_ffn_Wd_s)
    return x

_drawn_inputs = setup_inputs


def setup_inputs(seed=0):
    import zlib

    import numpy as np

    out = dict(_drawn_inputs(seed))
    spreads = {'L0_attn_norm_w': (1.0, 0.2),
     'L0_attn_norm_b': (0.0, 0.325),
     'L0_attn_qkv_b': (0.0, 0.343),
     'L0_attn_proj_b': (0.0, 0.1),
     'L0_ffn_correction_bias': (0.0, 0.8)}
    factors = {'L0_xattn_b_l': 3.718,
     'L0_ffn_gate_w': 8.0,
     'L0_ffn_Wg': 7.582,
     'L0_ffn_Wu': 7.509,
     'L0_ffn_Wd': 7.505,
     'L0_ffn_Wg_s': 8.0,
     'L0_ffn_Wu_s': 8.0,
     'L0_ffn_Wd_s': 8.0}
    for name, (base, spread) in spreads.items():
        noise = np.random.default_rng([zlib.crc32(name.encode()), seed]).standard_normal(out[name].shape)
        drawn = base * np.exp(spread * noise) if base else spread * noise
        out[name] = jnp.asarray(drawn.astype(out[name].dtype))
    for name, factor in factors.items():
        out[name] = (out[name] * factor).astype(out[name].dtype)
    return out
```

```python
from contextlib import ExitStack

import numpy as np

import concourse.bass as bass
from concourse import mybir

F32 = mybir.dt.float32
F32R = mybir.dt.float32r
ALU = mybir.AluOpType
ACT = mybir.ActivationFunctionType
AX = mybir.AxisListType.X

P = 128
STREAMS = 4
LN_EPS = 1e-5
NEXP = 8
EXPERT_SCALE = 2.5
ROUTE_TINY = 1e-20
FFN_TOKENS = 512
FFN_TILES = FFN_TOKENS // P


def is_first(g):
    return isinstance(g, int) and g == 0


def f32(ap):
    return ap.bitcast(F32)


def decoder_layer(nc, x, ctx, ctx_t, norm_w, norm_b, qkv_wt, qk_b, v_b, proj_wt, proj_b, w_cq, b_cq, w_c, b_c,
                  w_q, b_q, wl_t, b_l, gate_t, corr, wg, wu, wd, wg_s, wu_s, wd_s, ident_in, tri8_in,
                  tri4_in, diag_in, out):
    B, L, D = x.shape
    S = ctx.shape[1]
    KB = D // P
    I = wg.shape[2]
    G = STREAMS
    NGRP = B // G
    SB = 125
    NSB = S // SB
    SP_ = S + S % 2
    TOK = G * L
    ATT_SCALE = float(1.0 / np.sqrt(L))
    NT = B * L
    NG2 = NT // FFN_TOKENS
    NE = NEXP + 1
    assert D == 256 and I == P and NSB * SB == S and NG2 * FFN_TOKENS == NT and NG2 % 2 == 1

    x2_dram = nc.dram_tensor("x2_scratch", (NT, D), F32, kind="Internal").ap()
    cw_dram = nc.dram_tensor("cw_scratch", (2, NEXP, FFN_TOKENS), F32, kind="Internal").ap()

    def mm3(pe, dst, a_hi, a_lo, b_hi, b_lo, first, last, **kw):
        pe.matmul(dst, a_lo, b_hi, start=first, stop=False, **kw)
        pe.matmul(dst, a_hi, b_lo, start=False, stop=False, **kw)
        return pe.matmul(dst, a_hi, b_hi, start=False, stop=last, **kw)

    outer = ExitStack()
    with outer:
        bank = [outer.enter_context(nc.psum_tensor(f"bank{n}", [P, 512], F32)) for n in range(8)]
        ident = outer.enter_context(nc.sbuf_tensor("ident", [P, P], F32))
        held = outer.enter_context(nc.sbuf_tensor("held", [P, 1 + STREAMS], F32))
        x2_st = outer.enter_context(nc.semaphore("x2_stored"))

        with ExitStack() as c1:
            def sb(name, shape, dt=F32):
                return c1.enter_context(nc.sbuf_tensor(name, shape, dt))

            def sem(name):
                return c1.enter_context(nc.semaphore(name))

            v_bank = bank[4:6]
            m_bank = bank[6]

            ctxf = sb("ctxf", [P, G, NSB, D])
            tmp_all = sb("tmp", [P, G, 512])
            staging = ctxf[:, :, :, :].rearrange("p g b d -> p (g b d)")
            wqkv_f = staging[:, 0:3 * KB * D].rearrange("p (k n) -> p k n", k=KB)
            wp_f = staging[:, 3 * KB * D:4 * KB * D].rearrange("p (k n) -> p k n", k=KB)
            wl_f = tmp_all[:, :, :].rearrange("p g (k n) -> p (g k) n", n=D)
            wqkv_hi, wqkv_lo = sb("wqkv_hi", [P, KB, 3 * D], F32R), sb("wqkv_lo", [P, KB, 3 * D], F32R)
            wp_hi, wp_lo = sb("wp_hi", [P, KB, D], F32R), sb("wp_lo", [P, KB, D], F32R)
            wl_hi, wl_lo = sb("wl_hi", [P, 4 * KB, D], F32R), sb("wl_lo", [P, 4 * KB, D], F32R)
            nw, nb = sb("nw", [P, KB]), sb("nb", [P, KB])
            nb_wide = sb("nb_wide", [P, KB, L])
            qk_bias, qk_bias0 = sb("qk_bias", [L, 2 * D]), sb("qk_bias0", [L, 2 * D])
            v_bias, v_bias0 = sb("v_bias", [P, KB]), sb("v_bias0", [P, KB])
            pb_wide, bl_wide, wc_wide = sb("pb_wide", [L, D]), sb("bl_wide", [L, D]), sb("wc_wide", [L, D])
            wcq, wq = sb("wcq", [P, KB]), sb("wq", [P, KB])
            b3, b_sum = sb("b3", [L, 3]), sb("b_sum", [L, 1])
            diag = sb("diag", [L, G, G])
            mhalf, eps, one, mone, pheld = (sb(n, [L, G]) for n in ("mhalf", "eps", "one", "mone", "pheld"))

            xt = sb("xt", [L, G, D])
            st1, mv1 = sb("st1", [L, G, 6]), sb("mv1", [L, G, 2])
            ln1 = sb("ln1", [L, 10, G])
            hh = sb("hh", [L, G, D])
            res = sb("res", [L, G, D])
            h_hi, h_lo = sb("h_hi", [P, KB, TOK], F32R), sb("h_lo", [P, KB, TOK], F32R)
            v_hi, v_lo = sb("v_hi", [P, KB, TOK], F32R), sb("v_lo", [P, KB, TOK], F32R)
            op_hi = [sb(f"op_hi{j}", [P, 512], F32R) for j in range(G)]
            op_lo = [sb(f"op_lo{j}", [P, 512], F32R) for j in range(G)]
            tmp = [tmp_all[:, j, :] for j in range(G)]
            smx, ssum, sinv = sb("smx", [P, G, 2]), sb("ssum", [P, G, 2]), sb("sinv", [P, G, 2])
            x1 = sb("x1", [L, G, D])
            st2, mv2, r2a, r2 = sb("st2", [L, G, 6]), sb("mv2", [L, G, 2]), sb("r2a", [L, G]), sb("r2", [L, G])
            c = sb("c", [L, G, D])
            cwc, rdot = sb("cwc", [L, D]), sb("rdot", [L, G])
            ct = sb("ct", [P, G, KB, L])
            c_hi, c_lo = sb("c_hi", [P, G, KB, L], F32R), sb("c_lo", [P, G, KB, L], F32R)
            ctw = sb("ctw", [P, G, KB, L])
            cw_hi, cw_lo = sb("cw_hi", [P, G, KB, L], F32R), sb("cw_lo", [P, G, KB, L], F32R)
            ctxtf = sb("ctxtf", [P, G, KB, S])
            ctx_hi, ctx_lo = sb("ctx_hi", [SB, G, NSB, D], F32R), sb("ctx_lo", [SB, G, NSB, D], F32R)
            ctxt_hi, ctxt_lo = sb("ctxt_hi", [P, G, KB, SP_], F32R), sb("ctxt_lo", [P, G, KB, SP_], F32R)
            smx2, ssum2, sinv2 = sb("smx2", [L, G]), sb("ssum2", [L, G]), sb("sinv2", [L, G])
            m4 = sb("m4", [L, G])
            mneg, msum, minv = sb("mneg", [G, 1]), sb("msum", [G, 1]), sb("minv", [G, 1])
            mexp, mrow = sb("mexp", [G, L]), sb("mrow", [G, L])
            b4 = sb("b4", [L, G])
            bm = sb("bm", [L, G, G])
            q2c_row, q2c = sb("q2c_row", [G, D]), sb("q2c", [P, KB, G])
            x4 = ctw
            x4_hi, x4_lo = cw_hi, cw_lo

            w_in, x_in = sem("weights_in"), sem("x_in")
            cx_in = [sem(f"context{j}_in") for j in range(G)]
            wide = sem("nb_widened")
            w_split, bias_mm, bias_ok = sem("weights_split"), sem("bias_product"), sem("bias_ready")
            consts = sem("constants_set")
            st1_ok, mv1_ok, ln1_step = sem("ln1_stats"), sem("ln1_moments"), sem("ln1_scalars")
            hh_ok, res0_ok, res_ok = sem("hh_ready"), sem("residual_scaled"), sem("residual_ready")
            t_h, h_hi_ok, h_lo_ok = sem("h_transposed"), sem("h_hi_ready"), sem("h_lo_ready")
            qk_mm, qk_f_ok, qk_hi_ok, qk_lo_ok = sem("qk_product"), sem("qk_biased"), sem("qk_hi_ready"), sem("qk_lo_ready")
            v_mm, v_hi_ok, v_lo_ok = sem("v_product"), sem("v_hi_ready"), sem("v_lo_ready")
            sc_mm, smx_ok, exp_ok, sinv_ok = sem("scores_product"), sem("scores_max"), sem("scores_exp"), sem("scores_inv_sum")
            w_f_ok, w_hi_ok, w_lo_ok = sem("probs_scaled"), sem("probs_hi_ready"), sem("probs_lo_ready")
            g_mm, g_hi_ok, g_lo_ok = sem("probs_proj_product"), sem("probs_proj_hi"), sem("probs_proj_lo")
            ao_mm, x1_ok, st2_ok, mv2_ok = sem("attention_out"), sem("x1_ready"), sem("ln2_stats"), sem("ln2_moments")
            r2a_ok, r2_ok, c_ok, x1b_ok = sem("ln2_var_eps"), sem("ln2_rstd"), sem("c_ready"), sem("x1_biased")
            rdot_ok = sem("row_term_ready")
            t_c, ct_ok, c_hi_ok, c_lo_ok = sem("c_transposed"), sem("ct_ready"), sem("c_hi_ready"), sem("c_lo_ready")
            ctw_ok, cw_hi_ok, cw_lo_ok = sem("c_weighted"), sem("cw_hi_ready"), sem("cw_lo_ready")
            cx_hi_ok, cx_lo_ok = sem("context_hi_ready"), sem("context_lo_ready")
            s_mm, smx2_ok, exp2_ok, sinv2_ok, a_f_ok = sem("similarity"), sem("sim_max"), sem("sim_exp"), sem("sim_inv_sum"), sem("sim_probs")
            m4_ok = sem("row_max_ready")
            t_a, a_hi_ok, a_lo_ok = sem("a_transposed"), sem("a_hi_ready"), sem("a_lo_ready")
            c2q_mm, c2q_ok, x3_ok = sem("c2q_product"), sem("c2q_copied"), sem("c_c2q_ready")
            t_x, x_hi_ok, x_lo_ok = sem("x23_transposed"), sem("x23_hi_ready"), sem("x23_lo_ready")
            t_m, mneg_ok, mexp_ok, minv_ok, mrow_ok = sem("m_transposed"), sem("m_max"), sem("m_exp"), sem("m_inv_sum"), sem("b_att_rows")
            t_b, b4_ok, bm_ok, q2c_mm, q2cr_ok = sem("b_att_transposed"), sem("b_att_columns"), sem("b_att_masked"), sem("q2c_product"), sem("q2c_rows")
            t_q, q2c_ok, x4_ok, x4_hi_ok, x4_lo_ok = sem("q2c_transposed"), sem("q2c_ready"), sem("x4_ready"), sem("x4_hi_ready"), sem("x4_lo_ready")
            z_mm, x2_ok = sem("z_product"), sem("x2_ready")
            smx_raw, smx2_raw, b_sum_ok = sem("scores_max_raw"), sem("sim_max_raw"), sem("b_sum_ready")

            NSETUP = 17
            x_tiles = x.rearrange("b t d -> t b d")
            x2_tiles = x2_dram.rearrange("(b t) d -> t b d", t=L)
            LN1_STEPS = 10

            block = c1.enter_context(nc.Block())

            @block.sync
            def _(sp):
                sp.dma_start(xt[:, :, :], x_tiles[:, 0:G, :]).then_inc(x_in, 16)
                sp.dma_start(ident[:, :], ident_in).then_inc(w_in, 16)
                sp.dma_start(nw[:, :], norm_w).then_inc(w_in, 16)
                sp.dma_start(nb[:, :], norm_b).then_inc(w_in, 16)
                sp.dma_start(wqkv_f[:, :, :], qkv_wt.rearrange("(k p) n -> p k n", p=P)).then_inc(w_in, 16)
                sp.dma_start(qk_bias0[:, :], qk_b.partition_broadcast(L)).then_inc(w_in, 16)
                sp.dma_start(v_bias0[:, :], v_b).then_inc(w_in, 16)
                sp.dma_start(wp_f[:, :, :], proj_wt.rearrange("(k p) n -> p k n", p=P)).then_inc(w_in, 16)
                sp.dma_start(wl_f[:, :, :], wl_t.rearrange("(k p) n -> p k n", p=P)).then_inc(w_in, 16)
                sp.dma_start(pb_wide[:, :], proj_b.partition_broadcast(L)).then_inc(w_in, 16)
                sp.dma_start(bl_wide[:, :], b_l.partition_broadcast(L)).then_inc(w_in, 16)
                sp.dma_start(wc_wide[:, :], w_c.partition_broadcast(L)).then_inc(w_in, 16)
                sp.dma_start(wcq[:, :], w_cq).then_inc(w_in, 16)
                sp.dma_start(wq[:, :], w_q).then_inc(w_in, 16)
                sp.dma_start(diag[:, :, :], diag_in.partition_broadcast(L)).then_inc(w_in, 16)
                for n, b in enumerate((b_cq, b_c, b_q)):
                    sp.dma_start(b3[:, n:n + 1], b.partition_broadcast(L)).then_inc(w_in, 16)

                def load_context(batch, j):
                    sp.dma_start(ctxtf[:, j, :, :], ctx_t[bass.ds(batch + j, 1)].rearrange("o (k p) s -> p (o k) s", p=P)).then_inc(cx_in[j], 16)
                    sp.dma_start(ctxf[0:SB, j, :, :], ctx[bass.ds(batch + j, 1)].rearrange("o (k p) d -> p (o k) d", p=SB)).then_inc(cx_in[j], 16)

                def group(i, last):
                    batch = sp.snap(G * i)
                    if not last:
                        sp.wait_ge(hh_ok, G * (i + 1))
                        sp.wait_ge(res0_ok, G * (i + 1))
                        sp.wait_ge(w_in, 16)
                        sp.dma_start(xt[:, :, :], x_tiles[:, bass.ds(batch + G, G), :]).then_inc(x_in, 16)
                        for j in range(G):
                            sp.wait_ge(cx_lo_ok, G * i + j + 1)
                            sp.wait_ge(w_in, 16)
                            load_context(batch + G, j)
                    sp.wait_ge(x2_ok, G * (i + 1))
                    sp.wait_ge(w_in, 16)
                    sp.dma_start(x2_tiles[:, bass.ds(batch, G), :], x1[:, :, :]).then_inc(x2_st, 16)

                sp.wait_ge(w_split, 2 * (KB + 2))
                sp.wait_ge(bias_mm, 1)
                for j in range(G):
                    load_context(0, j)
                with sp.Fori(0, NGRP - 1) as i:
                    group(i, False)
                group(NGRP - 1, True)
                sp.wait_ge(x2_st, 16 * (NGRP + 1))

            @block.tensor
            def _(pe):
                pe.wait_ge(wide, 1)
                for k in range(KB):
                    pe.matmul(m_bank[0:L, :], nb_wide[:, k, :], wqkv_f[:, k, 0:2 * D], start=(k == 0), stop=(k == KB - 1))
                for half in range(KB):
                    for k in range(KB):
                        last = pe.matmul(v_bank[0][:, half:half + 1], wqkv_f[:, k, 2 * D + half * P:2 * D + (half + 1) * P],
                                         nb[:, k:k + 1], start=(k == 0), stop=(k == KB - 1))
                last.then_inc(bias_mm, 1)
                pe.wait_ge(bias_ok, 2)
                pe.wait_ge(w_split, 2 * (KB + 2))

                def turn_h(g):
                    for j in range(G):
                        if not is_first(g):
                            pe.wait_ge(x2_ok, G * (g - 1) + j + 1)
                        pe.wait_ge(hh_ok, G * g + j + 1)
                        for k in range(KB):
                            t = pe.transpose(bank[j][:, k * L:(k + 1) * L], hh[:, j, k * P:(k + 1) * P], ident[0:L, 0:L])
                        t.then_inc(t_h, 1)

                def group(i, last_group):
                    ev = [G * i + j + 1 for j in range(G)]
                    for j in range(G):
                        pe.wait_ge(h_lo_ok, ev[j])
                        for k in range(KB):
                            t = slice(j * L, (j + 1) * L)
                            last = mm3(pe, bank[j][0:L, :], h_hi[:, k, t], h_lo[:, k, t], wqkv_hi[:, k, 0:2 * D],
                                       wqkv_lo[:, k, 0:2 * D], k == 0, k == KB - 1)
                        last.then_inc(qk_mm, 1)
                    for half in range(KB):
                        n = slice(2 * D + half * P, 2 * D + (half + 1) * P)
                        for k in range(KB):
                            last = mm3(pe, v_bank[half][:, 0:TOK], wqkv_hi[:, k, n], wqkv_lo[:, k, n], h_hi[:, k, :], h_lo[:, k, :],
                                       k == 0, k == KB - 1)
                        last.then_inc(v_mm, 1)
                    for j in range(G):
                        pe.wait_ge(qk_lo_ok, ev[j])
                        for half in range(KB):
                            q = slice(half * P, (half + 1) * P)
                            last = mm3(pe, bank[j][:, half * D:(half + 1) * D], op_hi[j][0:L, q], op_lo[j][0:L, q],
                                       op_hi[j][0:L, D:2 * D], op_lo[j][0:L, D:2 * D], True, True)
                        last.then_inc(sc_mm, 1)
                    for j in range(G):
                        pe.wait_ge(w_lo_ok, ev[j])
                        for half in range(KB):
                            for q in range(KB):
                                n = slice(q * D + half * P, q * D + (half + 1) * P)
                                last = mm3(pe, bank[j][:, half * D:(half + 1) * D], op_hi[j][:, n], op_lo[j][:, n],
                                           wp_hi[:, q, :], wp_lo[:, q, :], q == 0, q == KB - 1)
                        last.then_inc(g_mm, 1)
                    pe.wait_ge(v_lo_ok, KB * (i + 1))
                    for j in range(G):
                        pe.wait_ge(g_lo_ok, ev[j])
                        t = slice(j * L, (j + 1) * L)
                        for k in range(KB):
                            n = slice(k * D, (k + 1) * D)
                            last = mm3(pe, bank[j][0:L, 0:D], v_hi[:, k, t], v_lo[:, k, t], op_hi[j][:, n], op_lo[j][:, n],
                                       k == 0, k == KB - 1)
                        last.then_inc(ao_mm, 1)
                    for j in range(G):
                        pe.wait_ge(c_ok, ev[j])
                        for k in range(KB):
                            last = pe.transpose(bank[j][:, k * L:(k + 1) * L], c[:, j, k * P:(k + 1) * P], ident[0:L, 0:L])
                        last.then_inc(t_c, 1)
                    for j in range(G):
                        pe.wait_ge(cw_lo_ok, ev[j])
                        pe.wait_ge(c_lo_ok, ev[j])
                        pe.wait_ge(cx_lo_ok, ev[j])
                        for k in range(KB):
                            last = mm3(pe, bank[j][0:L, 0:SP_], cw_hi[:, j, k, :], cw_lo[:, j, k, :], ctxt_hi[:, j, k, :],
                                       ctxt_lo[:, j, k, :], k == 0, k == KB - 1)
                        last.then_inc(s_mm, 1)
                    for j in range(G):
                        pe.wait_ge(a_f_ok, ev[j])
                        for b in range(NSB):
                            last = pe.transpose(bank[j][0:SB, b * L:(b + 1) * L], tmp[j][0:L, b * SB:(b + 1) * SB], ident[0:L, 0:L])
                        last.then_inc(t_a, 1)
                    pe.wait_ge(m4_ok, G * (i + 1))
                    pe.transpose(m_bank[0:G, 0:L], m4[:, :], ident[0:L, 0:L]).then_inc(t_m, 1)
                    for j in range(G):
                        pe.wait_ge(a_lo_ok, ev[j])
                        for b in range(NSB):
                            t = slice(b * L, (b + 1) * L)
                            last = mm3(pe, bank[j][0:L, 0:D], op_hi[j][0:SB, t], op_lo[j][0:SB, t], ctx_hi[:, j, b, :],
                                       ctx_lo[:, j, b, :], b == 0, b == NSB - 1)
                        last.then_inc(c2q_mm, 1)
                    for j in range(2):
                        if j == 0:
                            pe.wait_ge(mrow_ok, i + 1)
                        pe.wait_ge(x3_ok, ev[j])
                        for k in range(2 * KB):
                            last = pe.transpose(bank[j][:, k * L:(k + 1) * L], tmp[j][0:L, k * P:(k + 1) * P], ident[0:L, 0:L])
                        last.then_inc(t_x, 1)
                        if j == 0:
                            pe.transpose(m_bank[0:L, P:P + G], mrow[:, :], ident[0:G, 0:G]).then_inc(t_b, 1)
                    pe.wait_ge(bm_ok, i + 1)
                    for j in range(G):
                        last = pe.matmul(m_bank[0:G, D:2 * D], bm[:, j, :], c[:, j, :], start=(j == 0), stop=(j == G - 1))
                    last.then_inc(q2c_mm, 1)
                    for j in range(2, G):
                        pe.wait_ge(x3_ok, ev[j])
                        for k in range(2 * KB):
                            last = pe.transpose(bank[j][:, k * L:(k + 1) * L], tmp[j][0:L, k * P:(k + 1) * P], ident[0:L, 0:L])
                        last.then_inc(t_x, 1)
                    for j in range(G):
                        pe.wait_ge(x_lo_ok, ev[j])
                        if j == 0:
                            pe.wait_ge(q2cr_ok, i + 1)
                        zb = bank[j][0:L, 0:D]
                        for k in range(KB):
                            mm3(pe, zb, c_hi[:, j, k, :], c_lo[:, j, k, :], wl_hi[:, k, :], wl_lo[:, k, :], k == 0, False)
                        if j == 0:
                            for k in range(KB):
                                last = pe.transpose(m_bank[:, k * G:(k + 1) * G], q2c_row[:, k * P:(k + 1) * P], ident[0:G, 0:G])
                            last.then_inc(t_q, 1)
                        for k in range(2 * KB):
                            t = slice(k * L, (k + 1) * L)
                            mm3(pe, zb, op_hi[j][:, t], op_lo[j][:, t], wl_hi[:, KB + k, :], wl_lo[:, KB + k, :], False, False)
                    pe.wait_ge(x4_lo_ok, i + 1)
                    for j in range(G):
                        zb = bank[j][0:L, 0:D]
                        for k in range(KB):
                            last = mm3(pe, zb, x4_hi[:, j, k, :], x4_lo[:, j, k, :], wl_hi[:, 3 * KB + k, :],
                                       wl_lo[:, 3 * KB + k, :], False, k == KB - 1)
                        last.then_inc(z_mm, 1)
                    if not last_group:
                        turn_h(i + 1)

                turn_h(0)
                with pe.Fori(0, NGRP - 1) as i:
                    group(i, False)
                group(NGRP - 1, True)

            @block.scalar
            def _(act):
                def residual(g):
                    act.wait_ge(x_in, 16 * (g + 1))
                    act.wait_ge(ln1_step, LN1_STEPS * (g + 1))
                    if not is_first(g):
                        act.wait_ge(x1_ok, G * g)
                    for j in range(G):
                        act.activation(res[:, j, :], xt[:, j, :], ACT.Identity, bias=ln1[:, 9, j:j + 1],
                                       scale=ln1[:, 7, j:j + 1]).then_inc(res0_ok, 1)

                def context_hi(i, j):
                    act.wait_ge(cx_in[j], 32 * (i + 1))
                    act.activation(ctxt_hi[:, j, :, 0:S], ctxtf[:, j, :, :], ACT.Copy)
                    act.activation(ctx_hi[:, j, :, :], ctxf[0:SB, j, :, :], ACT.Copy).then_inc(cx_hi_ok, 1)

                def group(i, last):
                    ev = [G * i + j + 1 for j in range(G)]
                    for j in range(G):
                        act.wait_ge(t_h, ev[j])
                        act.activation(h_hi[:, :, j * L:(j + 1) * L], bank[j][:, 0:KB * L].rearrange("p (k t) -> p k t", k=KB),
                                       ACT.Copy).then_inc(h_hi_ok, 1)
                    context_hi(i, 0)
                    for j in range(G):
                        act.wait_ge(qk_f_ok, ev[j])
                        act.activation(op_hi[j][0:L, :], tmp[j][0:L, :], ACT.Copy).then_inc(qk_hi_ok, 1)
                    for half in range(KB):
                        act.wait_ge(v_mm, KB * i + half + 1)
                        act.activation(v_hi[:, half, :], v_bank[half][:, 0:TOK], ACT.Identity,
                                       bias=v_bias[:, half:half + 1]).then_inc(v_hi_ok, 1)
                    context_hi(i, 1)
                    for j in range(G):
                        act.wait_ge(smx_ok, ev[j])
                        for half in range(KB):
                            n = slice(half * D, (half + 1) * D)
                            e = act.activation(tmp[j][:, n], bank[j][:, n], ACT.Exp, bias=smx[:, j, half:half + 1], scale=ATT_SCALE,
                                               accum_out=ssum[:, j, half:half + 1])
                        e.then_inc(exp_ok, 1)
                    for j in range(G):
                        act.wait_ge(w_f_ok, ev[j])
                        act.activation(op_hi[j][:, :], tmp[j][:, :], ACT.Copy).then_inc(w_hi_ok, 1)
                    context_hi(i, 2)
                    for j in range(G):
                        act.wait_ge(g_mm, ev[j])
                        act.activation(op_hi[j][:, :], bank[j][:, :], ACT.Copy).then_inc(g_hi_ok, 1)
                    context_hi(i, 3)
                    for j in range(G):
                        act.wait_ge(t_c, ev[j])
                        tc = bank[j][:, 0:KB * L].rearrange("p (k t) -> p k t", k=KB)
                        act.activation(ct[:, j, :, :], tc, ACT.Copy).then_inc(ct_ok, 1)
                        act.activation(c_hi[:, j, :, :], tc, ACT.Copy).then_inc(c_hi_ok, 1)
                    for j in range(G):
                        act.wait_ge(ctw_ok, ev[j])
                        act.activation(cw_hi[:, j, :, :], ctw[:, j, :, :], ACT.Copy).then_inc(cw_hi_ok, 1)
                    for j in range(G):
                        act.wait_ge(smx2_ok, ev[j])
                        act.activation(tmp[j][0:L, 0:S], bank[j][0:L, 0:S], ACT.Exp, bias=smx2[:, j:j + 1],
                                       accum_out=ssum2[:, j:j + 1]).then_inc(exp2_ok, 1)
                    for j in range(G):
                        act.wait_ge(t_a, ev[j])
                        act.activation(op_hi[j][0:SB, 0:NSB * L], bank[j][0:SB, 0:NSB * L], ACT.Copy).then_inc(a_hi_ok, 1)
                    act.wait_ge(mneg_ok, i + 1)
                    act.activation(mexp[:, :], m_bank[0:G, 0:L], ACT.Exp, bias=mneg[:, :], accum_out=msum[:, :]).then_inc(mexp_ok, 1)
                    for j in range(G):
                        act.wait_ge(c2q_mm, ev[j])
                        act.activation(tmp[j][0:L, 0:D], bank[j][0:L, 0:D], ACT.Copy).then_inc(c2q_ok, 1)
                    for j in range(G):
                        act.wait_ge(t_x, ev[j])
                        act.activation(op_hi[j][:, 0:2 * KB * L], bank[j][:, 0:2 * KB * L], ACT.Copy).then_inc(x_hi_ok, 1)
                    act.wait_ge(x4_ok, i + 1)
                    act.activation(x4_hi[:, :, :, :], x4[:, :, :, :], ACT.Copy).then_inc(x4_hi_ok, 1)
                    if not last:
                        residual(i + 1)

                residual(0)
                act.wait_ge(bias_ok, 2)
                with act.Fori(0, NGRP - 1) as i:
                    group(i, False)
                group(NGRP - 1, True)

            @block.gpsimd
            def _(pool):
                def ln1_scalars(g):
                    pool.wait_ge(mv1_ok, G * (g + 1))
                    if not is_first(g):
                        pool.wait_ge(res0_ok, G * g)
                        pool.wait_ge(hh_ok, G * g)
                    mean, var = mv1[:, :, 0], mv1[:, :, 1]
                    row = [ln1[:, n, :] for n in range(10)]
                    done = [0]

                    def step(ins):
                        done[0] += 1
                        ins.then_inc(ln1_step, 1)
                        if done[0] < LN1_STEPS:
                            pool.wait_ge(ln1_step, LN1_STEPS * g + done[0])

                    step(pool.tensor_tensor(row[0], var, eps[:, :], ALU.add))
                    step(pool.tensor_tensor(row[1], row[0], mhalf[:, :], ALU.pow))
                    step(pool.tensor_tensor(row[2], var, row[1], ALU.mult))
                    step(pool.tensor_tensor(row[3], row[2], row[1], ALU.mult))
                    step(pool.tensor_tensor(row[4], row[3], eps[:, :], ALU.add))
                    step(pool.tensor_tensor(row[5], row[4], mhalf[:, :], ALU.pow))
                    step(pool.tensor_tensor(row[6], row[5], row[1], ALU.mult))
                    step(pool.tensor_tensor(row[7], row[1], one[:, :], ALU.add))
                    step(pool.tensor_tensor(row[8], mean, row[1], ALU.mult))
                    step(pool.tensor_tensor(row[9], row[8], mone[:, :], ALU.mult))

                def residual_bias(g):
                    for j in range(G):
                        pool.wait_ge(res0_ok, G * g + j + 1)
                        pool.tensor_tensor(res[:, j, :], res[:, j, :], pb_wide[:, :], ALU.add).then_inc(res_ok, 1)

                def context_lo(i, j):
                    pool.wait_ge(cx_hi_ok, G * i + j + 1)
                    pool.tensor_tensor(ctxt_lo[:, j, :, 0:S], ctxtf[:, j, :, :], f32(ctxt_hi[:, j, :, 0:S]), ALU.subtract)
                    pool.tensor_tensor(ctx_lo[:, j, :, :], ctxf[0:SB, j, :, :], f32(ctx_hi[:, j, :, :]), ALU.subtract).then_inc(cx_lo_ok, 1)

                def group(i, last):
                    ev = [G * i + j + 1 for j in range(G)]
                    for j in range(G):
                        pool.wait_ge(qk_hi_ok, ev[j])
                        pool.tensor_tensor(op_lo[j][0:L, :], tmp[j][0:L, :], f32(op_hi[j][0:L, :]), ALU.subtract).then_inc(qk_lo_ok, 1)
                    context_lo(i, 0)
                    context_lo(i, 1)
                    context_lo(i, 2)
                    context_lo(i, 3)
                    if not last:
                        ln1_scalars(i + 1)
                    for j in range(G):
                        pool.wait_ge(mv2_ok, ev[j])
                        pool.tensor_tensor(r2a[:, j:j + 1], mv2[:, j, 1:2], eps[:, j:j + 1], ALU.add).then_inc(r2a_ok, 1)
                        pool.wait_ge(r2a_ok, ev[j])
                        pool.tensor_tensor(r2[:, j:j + 1], r2a[:, j:j + 1], mhalf[:, j:j + 1], ALU.pow).then_inc(r2_ok, 1)
                    for j in range(G):
                        pool.wait_ge(ct_ok, ev[j])
                        pool.tensor_tensor(pheld[:, j:j + 1], one[:, 0:1], one[:, 0:1], ALU.add)
                        for k in range(KB):
                            w = pool.tensor_scalar(ctw[:, j, k, :], ct[:, j, k, :], wcq[:, k:k + 1], wq[:, k:k + 1], ALU.mult, ALU.add)
                        w.then_inc(ctw_ok, 1)
                    for j in range(G):
                        pool.wait_ge(c_ok, ev[j])
                        pool.tensor_tensor(x1[:, j, :], x1[:, j, :], bl_wide[:, :], ALU.add).then_inc(x1b_ok, 1)
                    if not last:
                        residual_bias(i + 1)

                pool.wait_ge(w_in, 16 * (NSETUP))
                pool.wait_ge(consts, 6)
                ln1_scalars(0)
                residual_bias(0)
                with pool.Fori(0, NGRP - 1) as i:
                    group(i, False)
                group(NGRP - 1, True)

            @block.vector
            def _(dve):
                def ln1_moments(g):
                    dve.wait_ge(x_in, 16 * (g + 1))
                    if not is_first(g):
                        dve.wait_ge(ln1_step, LN1_STEPS * g)
                    for j in range(G):
                        dve.bn_stats(st1[:, j, :], xt[:, j, :]).then_inc(st1_ok, 1)
                    dve.wait_ge(st1_ok, G * (g + 1))
                    dve.tensor_copy(held[0:L, 0:1], mhalf[:, 0:1])
                    for j in range(G):
                        dve.bn_aggr(mv1[:, j, :], st1[:, j, :]).then_inc(mv1_ok, 1)

                def normalise_h(g):
                    dve.wait_ge(ln1_step, LN1_STEPS * (g + 1))
                    if not is_first(g):
                        dve.wait_ge(t_h, G * g)
                    for j in range(G):
                        dve.tensor_scalar(hh[:, j, :], xt[:, j, :], mv1[:, j, 0:1], ln1[:, 6, j:j + 1], ALU.subtract,
                                          ALU.mult).then_inc(hh_ok, 1)

                def group(i, last):
                    ev = [G * i + j + 1 for j in range(G)]
                    for j in range(G):
                        dve.wait_ge(h_hi_ok, ev[j])
                        t = slice(j * L, (j + 1) * L)
                        dve.tensor_tensor(h_lo[:, :, t], bank[j][:, 0:KB * L].rearrange("p (k t) -> p k t", k=KB),
                                          f32(h_hi[:, :, t]), ALU.subtract).then_inc(h_lo_ok, 1)
                    for j in range(G):
                        dve.wait_ge(qk_mm, ev[j])
                        dve.tensor_tensor(tmp[j][0:L, :], bank[j][0:L, :], qk_bias[:, :], ALU.add).then_inc(qk_f_ok, 1)
                    for half in range(KB):
                        dve.wait_ge(v_hi_ok, KB * i + half + 1)
                        dve.scalar_tensor_tensor(v_lo[:, half, :], v_bank[half][:, 0:TOK], v_bias[:, half:half + 1],
                                                 f32(v_hi[:, half, :]), ALU.add, ALU.subtract).then_inc(v_lo_ok, 1)
                    for j in range(G):
                        dve.wait_ge(sc_mm, ev[j])
                        dve.reduce_max(ssum[:, j, :], bank[j][:, :].rearrange("p (h k) -> p h k", h=KB), AX).then_inc(smx_raw, 1)
                        dve.wait_ge(smx_raw, ev[j])
                        dve.tensor_scalar(smx[:, j, :], ssum[:, j, :], -ATT_SCALE, None, ALU.mult).then_inc(smx_ok, 1)
                    for j in range(G):
                        dve.wait_ge(exp_ok, ev[j])
                        dve.reciprocal(sinv[:, j, :], ssum[:, j, :]).then_inc(sinv_ok, 1)
                        dve.wait_ge(sinv_ok, ev[j])
                        for half in range(KB):
                            n = slice(half * D, (half + 1) * D)
                            w = dve.tensor_scalar(tmp[j][:, n], tmp[j][:, n], sinv[:, j, half:half + 1], None, ALU.mult)
                        w.then_inc(w_f_ok, 1)
                    for j in range(G):
                        dve.wait_ge(w_hi_ok, ev[j])
                        dve.tensor_tensor(op_lo[j][:, :], tmp[j][:, :], f32(op_hi[j][:, :]), ALU.subtract).then_inc(w_lo_ok, 1)
                    if not last:
                        ln1_moments(i + 1)
                    for j in range(G):
                        dve.wait_ge(g_hi_ok, ev[j])
                        dve.tensor_tensor(op_lo[j][:, :], bank[j][:, :], f32(op_hi[j][:, :]), ALU.subtract).then_inc(g_lo_ok, 1)
                    dve.wait_ge(res_ok, G * (i + 1))
                    dve.wait_ge(x2_st, 16 * (i + 1))
                    for j in range(G):
                        dve.wait_ge(ao_mm, ev[j])
                        dve.tensor_tensor(x1[:, j, :], bank[j][0:L, 0:D], res[:, j, :], ALU.add).then_inc(x1_ok, 1)
                        dve.wait_ge(x1_ok, ev[j])
                        dve.bn_stats(st2[:, j, :], x1[:, j, :]).then_inc(st2_ok, 1)
                        dve.wait_ge(st2_ok, ev[j])
                        dve.tensor_copy(held[0:L, 1 + j:2 + j], mhalf[:, 0:1])
                        dve.bn_aggr(mv2[:, j, :], st2[:, j, :]).then_inc(mv2_ok, 1)
                    for j in range(G):
                        dve.wait_ge(r2_ok, ev[j])
                        dve.wait_ge(mv2_ok, ev[j])
                        dve.tensor_scalar(c[:, j, :], x1[:, j, :], mv2[:, j, 0:1], r2[:, j:j + 1], ALU.subtract, ALU.mult).then_inc(c_ok, 1)
                    for j in range(G):
                        dve.wait_ge(c_hi_ok, ev[j])
                        dve.tensor_tensor(c_lo[:, j, :, :], bank[j][:, 0:KB * L].rearrange("p (k t) -> p k t", k=KB),
                                          f32(c_hi[:, j, :, :]), ALU.subtract).then_inc(c_lo_ok, 1)
                        dve.wait_ge(c_ok, ev[j])
                        if j:
                            dve.wait_ge(rdot_ok, ev[j - 1])
                        dve.scalar_tensor_tensor(cwc[:, :], c[:, j, :], 1.0, wc_wide[:, :], ALU.mult, ALU.mult,
                                                 accum_out=rdot[:, j:j + 1]).then_inc(rdot_ok, 1)
                    for j in range(G):
                        dve.wait_ge(cw_hi_ok, ev[j])
                        dve.tensor_tensor(cw_lo[:, j, :, :], ctw[:, j, :, :], f32(cw_hi[:, j, :, :]), ALU.subtract).then_inc(cw_lo_ok, 1)
                    for j in range(G):
                        dve.wait_ge(s_mm, ev[j])
                        dve.reduce_max(ssum2[:, j:j + 1], bank[j][0:L, 0:S], AX).then_inc(smx2_raw, 1)
                        dve.wait_ge(smx2_raw, ev[j])
                        dve.scalar_tensor_tensor(m4[:, j:j + 1], ssum2[:, j:j + 1], b_sum[:, 0:1], rdot[:, j:j + 1], ALU.add,
                                                 ALU.add).then_inc(m4_ok, 1)
                        dve.tensor_scalar(smx2[:, j:j + 1], ssum2[:, j:j + 1], -1.0, None, ALU.mult).then_inc(smx2_ok, 1)
                    for j in range(G):
                        dve.wait_ge(exp2_ok, ev[j])
                        dve.reciprocal(sinv2[:, j:j + 1], ssum2[:, j:j + 1]).then_inc(sinv2_ok, 1)
                        dve.wait_ge(sinv2_ok, ev[j])
                        dve.tensor_scalar(tmp[j][0:L, 0:S], tmp[j][0:L, 0:S], sinv2[:, j:j + 1], None, ALU.mult).then_inc(a_f_ok, 1)
                    dve.wait_ge(t_m, i + 1)
                    dve.reduce_max(mneg[:, :], m_bank[0:G, 0:L], AX, negate=True).then_inc(mneg_ok, 1)
                    for j in range(G):
                        dve.wait_ge(a_hi_ok, ev[j])
                        dve.tensor_tensor(op_lo[j][0:SB, 0:NSB * L], bank[j][0:SB, 0:NSB * L], f32(op_hi[j][0:SB, 0:NSB * L]),
                                          ALU.subtract).then_inc(a_lo_ok, 1)
                    dve.wait_ge(mexp_ok, i + 1)
                    dve.reciprocal(minv[:, :], msum[:, :]).then_inc(minv_ok, 1)
                    dve.wait_ge(minv_ok, i + 1)
                    dve.tensor_scalar(mrow[:, :], mexp[:, :], minv[:, 0:1], None, ALU.mult).then_inc(mrow_ok, 1)
                    for j in range(G):
                        dve.wait_ge(c2q_ok, ev[j])
                        dve.tensor_tensor(tmp[j][0:L, D:2 * D], tmp[j][0:L, 0:D], c[:, j, :], ALU.mult).then_inc(x3_ok, 1)
                        if j == 1:
                            dve.wait_ge(t_b, i + 1)
                            dve.tensor_copy(b4[:, :], m_bank[0:L, P:P + G]).then_inc(b4_ok, 1)
                            dve.wait_ge(b4_ok, i + 1)
                            dve.tensor_tensor(bm[:, :, :], diag[:, :, :], b4[:, :].unsqueeze(2).to_broadcast([L, G, G]),
                                              ALU.mult).then_inc(bm_ok, 1)
                    for j in range(G):
                        dve.wait_ge(x_hi_ok, ev[j])
                        dve.tensor_tensor(op_lo[j][:, 0:2 * KB * L], bank[j][:, 0:2 * KB * L], f32(op_hi[j][:, 0:2 * KB * L]),
                                          ALU.subtract).then_inc(x_lo_ok, 1)
                        if j == 1:
                            dve.wait_ge(q2c_mm, i + 1)
                            dve.tensor_copy(q2c_row[:, :], m_bank[0:G, D:2 * D]).then_inc(q2cr_ok, 1)
                    dve.wait_ge(t_q, i + 1)
                    dve.tensor_copy(q2c[:, :, :], m_bank[:, 0:KB * G].rearrange("p (k g) -> p k g", k=KB)).then_inc(q2c_ok, 1)
                    dve.wait_ge(q2c_ok, i + 1)
                    for k in range(KB):
                        w = dve.tensor_tensor(x4[:, :, k, :], ct[:, :, k, :], q2c[:, k, :].unsqueeze(2).to_broadcast([P, G, L]), ALU.mult)
                    w.then_inc(x4_ok, 1)
                    dve.wait_ge(x4_hi_ok, i + 1)
                    dve.tensor_tensor(x4_lo[:, :, :, :], x4[:, :, :, :], f32(x4_hi[:, :, :, :]), ALU.subtract).then_inc(x4_lo_ok, 1)
                    if not last:
                        normalise_h(i + 1)
                    for j in range(G):
                        dve.wait_ge(z_mm, ev[j])
                        dve.wait_ge(x1b_ok, ev[j])
                        dve.tensor_tensor(x1[:, j, :], bank[j][0:L, 0:D], x1[:, j, :], ALU.add).then_inc(x2_ok, 1)

                dve.memset(mhalf[:, :], -0.5).then_inc(consts, 1)
                dve.memset(eps[:, :], LN_EPS).then_inc(consts, 1)
                dve.memset(one[:, :], 1.0).then_inc(consts, 1)
                dve.memset(mone[:, :], -1.0).then_inc(consts, 1)
                dve.memset(held[:, 0:1], 0.0).then_inc(x2_st, 16)
                dve.wait_ge(x2_st, 16)
                dve.memset(f32(ctxt_hi[:, :, :, S:SP_]), 0.0).then_inc(consts, 1)
                dve.memset(f32(ctxt_lo[:, :, :, S:SP_]), 0.0).then_inc(consts, 1)
                dve.wait_ge(consts, 6)
                ln1_moments(0)
                dve.wait_ge(w_in, 16 * (NSETUP))
                dve.tensor_copy(nb_wide[:, :, :], nb[:, :].unsqueeze(2).to_broadcast([P, KB, L])).then_inc(wide, 1)
                normalise_h(0)
                for k in range(KB):
                    dve.tensor_scalar(wqkv_hi[:, k, :], wqkv_f[:, k, :], nw[:, k:k + 1], None, ALU.mult).then_inc(w_split, 1)
                dve.tensor_copy(wp_hi[:, :, :], wp_f[:, :, :]).then_inc(w_split, 1)
                dve.tensor_copy(wl_hi[:, :, :], wl_f[:, :, :]).then_inc(w_split, 1)
                dve.wait_ge(w_split, KB + 2)
                for k in range(KB):
                    dve.scalar_tensor_tensor(wqkv_lo[:, k, :], wqkv_f[:, k, :], nw[:, k:k + 1], f32(wqkv_hi[:, k, :]), ALU.mult,
                                             ALU.subtract).then_inc(w_split, 1)
                dve.tensor_tensor(wp_lo[:, :, :], wp_f[:, :, :], f32(wp_hi[:, :, :]), ALU.subtract).then_inc(w_split, 1)
                dve.tensor_tensor(wl_lo[:, :, :], wl_f[:, :, :], f32(wl_hi[:, :, :]), ALU.subtract).then_inc(w_split, 1)
                dve.reduce_sum(b_sum[:, :], b3[:, :], AX).then_inc(b_sum_ok, 1)
                dve.wait_ge(b_sum_ok, 1)
                dve.wait_ge(bias_mm, 1)
                dve.tensor_tensor(qk_bias[:, :], m_bank[0:L, :], qk_bias0[:, :], ALU.add).then_inc(bias_ok, 1)
                dve.tensor_tensor(v_bias[:, :], v_bank[0][:, 0:KB], v_bias0[:, :], ALU.add).then_inc(bias_ok, 1)
                dve.wait_ge(bias_ok, 2)
                with dve.Fori(0, NGRP - 1) as i:
                    group(i, False)
                group(NGRP - 1, True)

        with ExitStack() as c2:
            def sb(name, shape, dt=F32):
                return c2.enter_context(nc.sbuf_tensor(name, shape, dt))

            def sem(name):
                return c2.enter_context(nc.semaphore(name))

            T = FFN_TILES
            g_bank, u_bank, y_bank, h_bank = bank[0:2], bank[2:4], bank[4:6], bank[6:8]
            ORDER = [NEXP] + list(range(NEXP))

            wgu_f = sb("wgu_f", [P, NE, 2, KB, I])
            wd_f = sb("wd_f", [P, NE, D])
            wgu_hi, wgu_lo = sb("wgu_hi", [P, NE, 2, KB, I], F32R), sb("wgu_lo", [P, NE, 2, KB, I], F32R)
            wd_hi, wd_lo = sb("wd_hi", [P, NE, D], F32R), sb("wd_lo", [P, NE, D], F32R)
            gate_f = sb("gate_f", [P, KB, NEXP])
            gate = sb("gate", [P, KB, 2 * NEXP], F32R)
            corr_w = sb("corr_w", [P, NEXP])
            tri8, tri4 = sb("tri8", [P, 8, 8]), sb("tri4", [P, 4, 4])
            mhalf2, eps2 = sb("mhalf2", [P, T]), sb("eps2", [P, T])

            x2t = [sb(f"x2t{p}", [P, T, D]) for p in range(2)]
            st3, mv3, r3a, r3 = sb("st3", [P, T, 6]), sb("mv3", [P, T, 2]), sb("r3a", [P, T]), sb("r3", [P, T])
            h3 = sb("h3", [P, T, D])
            h3_hi = [sb(f"h3_hi{p}", [P, KB, FFN_TOKENS], F32R) for p in range(2)]
            h3_lo = [sb(f"h3_lo{p}", [P, KB, FFN_TOKENS], F32R) for p in range(2)]
            lgt = sb("lgt", [2 * NEXP, FFN_TOKENS])
            lg2 = sb("lg2", [P, T, 2 * NEXP])
            lg, den, score, scorec, choice, wsel, cw = (sb(n, [P, T, NEXP]) for n in ("lg", "den", "score", "scorec", "choice", "wsel", "cw"))
            gsum, grank, gmask = (sb(n, [P, T, 4]) for n in ("gsum", "grank", "gmask"))
            g_gt, g_eq = sb("g_gt", [P, T, 4, 4]), sb("g_eq", [P, T, 4, 4])
            e_gt, e_eq = sb("e_gt", [P, T, 8, 8]), sb("e_eq", [P, T, 8, 8])
            erank, wsum, winv = sb("erank", [P, T, NEXP]), sb("wsum", [P, T]), sb("winv", [P, T])
            cwt = sb("cwt", [NEXP, FFN_TOKENS])
            cw_wide = [sb(f"cw_wide{p}", [P, NEXP, FFN_TOKENS]) for p in range(2)]
            sg = [sb(f"sg{b}", [P, FFN_TOKENS]) for b in range(2)]
            af = [sb(f"af{b}", [P, FFN_TOKENS]) for b in range(2)]
            a_hi = [sb(f"a_hi{b}", [P, FFN_TOKENS], F32R) for b in range(2)]
            a_lo = [sb(f"a_lo{b}", [P, FFN_TOKENS], F32R) for b in range(2)]

            wk_in = sem("routing_constants_in")
            wx_in = [sem(f"expert{e}_in") for e in range(NE)]
            x2_in = [sem(f"x2_{p}_in") for p in range(2)]
            out_st = sem("out_stored")
            w_hi_ok, w_lo_ok, gate_hi_ok, gate_ok, half_ok = sem("expert_hi"), sem("expert_lo"), sem("gate_hi"), sem("gate_ready"), sem("mhalf_set")
            st3_ok, mv3_ok, r3a_ok, r3_ok, h3_ok = sem("ln3_stats"), sem("ln3_moments"), sem("ln3_var_eps"), sem("ln3_rstd"), sem("h3_ready")
            t_h3, h3_hi_ok, h3_lo_ok = sem("h3_transposed"), sem("h3_hi_ready"), sem("h3_lo_ready")
            lg_mm, lgt_ok, t_lg, lg2_ok, lg_ok, eneg_ok = sem("logits_product"), sem("logits_copied"), sem("logits_transposed"), sem("logits_halves"), sem("logits_ready"), sem("logits_exp")
            route = sem("routing_step")
            t_cw, cwt_ok, cw_st, cw_in = sem("cw_transposed"), sem("cw_copied"), sem("cw_stored"), sem("cw_in")
            gu_mm, sg_ok, sgw_ok, af_ok, a_hi_ok, a_lo_ok = sem("gate_up_product"), sem("silu_ready"), sem("silu_weighted"), sem("act_ready"), sem("act_hi"), sem("act_lo")
            y_mm, out_ok = sem("down_product"), sem("out_ready")

            x2_g = x2_dram.rearrange("(t p) d -> p t d", p=P)
            out_g = out.rearrange("b l d -> (b l) d").rearrange("(t p) d -> p t d", p=P)
            ROUTE_STEPS = 23

            block = c2.enter_context(nc.Block())

            @block.sync
            def _(sp):
                def load_x2(g, p):
                    sp.dma_start(x2t[p][:, :, :], x2_g[:, bass.ds(T * g, T), :]).then_inc(x2_in[p], 16)

                def spread_cw(g, p):
                    sp.wait_ge(cwt_ok, g + 1)
                    sp.dma_start(cw_dram[p], cwt[:, :]).then_inc(cw_st, 16)
                    sp.wait_ge(cw_st, 16 * (g + 1))
                    sp.dma_start(cw_wide[p][:, :, :], cw_dram[p].partition_broadcast(P)).then_inc(cw_in, 16)

                def store(g, p):
                    sp.wait_ge(out_ok, 2 * (g + 1))
                    sp.wait_ge(wk_in, 64)
                    sp.dma_start(out_g[:, bass.ds(T * g, T), :], x2t[p][:, :, :]).then_inc(out_st, 16)

                load_x2(0, 0)
                load_x2(1, 1)
                sp.dma_start(corr_w[:, :], corr.partition_broadcast(P)).then_inc(wk_in, 16)
                sp.dma_start(tri8[:, :, :], tri8_in.partition_broadcast(P)).then_inc(wk_in, 16)
                sp.dma_start(tri4[:, :, :], tri4_in.partition_broadcast(P)).then_inc(wk_in, 16)
                sp.dma_start(gate_f[:, :, :], gate_t.rearrange("(k p) n -> p k n", p=P)).then_inc(wk_in, 16)
                for e in ORDER:
                    for half, (w, ws) in enumerate(((wg, wg_s), (wu, wu_s))):
                        src = ws if e == NEXP else w[e]
                        sp.dma_start(wgu_f[:, e, half, :, :], src.rearrange("(k p) n -> p k n", p=P)).then_inc(wx_in[e], 16)
                    sp.dma_start(wd_f[:, e, :], wd_s if e == NEXP else wd[e]).then_inc(wx_in[e], 16)
                spread_cw(0, 0)

                def group(g, p, more):
                    spread_cw(g + 1, 1 - p)
                    store(g, p)
                    if more:
                        sp.wait_ge(out_st, 16 * (g + 1))
                        sp.wait_ge(wk_in, 64)
                        load_x2(g + 2, p)

                with sp.Fori(0, NG2 // 2 - 1) as it:
                    group(2 * it, 0, True)
                    group(2 * it + 1, 1, True)
                group(NG2 - 3, 0, True)
                group(NG2 - 2, 1, False)
                store(NG2 - 1, 0)
                sp.wait_ge(out_st, 16 * NG2)

            @block.tensor
            def _(pe):
                def turn_h3(g):
                    pe.wait_ge(h3_ok, T * (g + 1))
                    for k in range(KB):
                        for t in range(T):
                            last = pe.transpose(h_bank[k][:, t * P:(t + 1) * P], h3[:, t, k * P:(k + 1) * P], ident[:, :])
                        last.then_inc(t_h3, 1)

                def logits(g, p):
                    pe.wait_ge(h3_lo_ok, KB * (g + 1))
                    for k in range(KB):
                        pe.matmul(h_bank[0][0:2 * NEXP, :], gate[:, k, :], h3_lo[p][:, k, :], start=(k == 0), stop=False)
                        last = pe.matmul(h_bank[0][0:2 * NEXP, :], gate[:, k, :], h3_hi[p][:, k, :], start=False, stop=(k == KB - 1))
                    last.then_inc(lg_mm, 1)

                def turn_logits(g):
                    for t in range(T):
                        last = pe.transpose(h_bank[1][:, t * 2 * NEXP:(t + 1) * 2 * NEXP], lgt[:, t * P:(t + 1) * P],
                                            ident[0:2 * NEXP, 0:2 * NEXP])
                    last.then_inc(t_lg, 1)

                def turn_cw(g):
                    pe.wait_ge(route, ROUTE_STEPS * (g + 1))
                    for t in range(T):
                        last = pe.transpose(h_bank[0][0:NEXP, t * P:(t + 1) * P], cw[:, t, :], ident[:, :])
                    last.then_inc(t_cw, 1)

                def gate_up(g, p, n):
                    e, b = ORDER[n], (p + n) % 2
                    if n >= 2:
                        pe.wait_ge(af_ok, NE * g + n - 1)
                    if is_first(g):
                        pe.wait_ge(w_lo_ok, n + 1)
                    for half, dst in enumerate((g_bank[b], u_bank[b])):
                        for k in range(KB):
                            last = mm3(pe, dst[:, :], wgu_hi[:, e, half, k, :], wgu_lo[:, e, half, k, :], h3_hi[p][:, k, :],
                                       h3_lo[p][:, k, :], k == 0, k == KB - 1)
                        last.then_inc(gu_mm, 1)

                def down(g, p, n):
                    e, b = ORDER[n], (p + n) % 2
                    pe.wait_ge(a_lo_ok, NE * g + n + 1)
                    if n == 0 and not is_first(g):
                        pe.wait_ge(out_ok, 2 * g)
                    for t in range(T):
                        s = slice(t * P, (t + 1) * P)
                        last = mm3(pe, y_bank[t // 2][:, (t % 2) * D:(t % 2 + 1) * D], a_hi[b][:, s], a_lo[b][:, s], wd_hi[:, e, :],
                                   wd_lo[:, e, :], n == 0 and t % 2 == 0, n == NE - 1, skip_group_check=True)
                    if n == NE - 1:
                        last.then_inc(y_mm, 1)

                def group(g, p, last):
                    gate_up(g, p, 0)
                    for n in range(1, NE):
                        if n == 3 and not last:
                            pe.wait_ge(lgt_ok, g + 2)
                        gate_up(g, p, n)
                        down(g, p, n - 1)
                        if not last:
                            if n == 1:
                                turn_h3(g + 1)
                            if n == 2:
                                logits(g + 1, 1 - p)
                            if n == 3:
                                turn_logits(g + 1)
                            if n == 5:
                                turn_cw(g + 1)
                    down(g, p, NE - 1)

                turn_h3(0)
                pe.wait_ge(gate_ok, 1)
                logits(0, 0)
                pe.wait_ge(lgt_ok, 1)
                turn_logits(0)
                turn_cw(0)
                group(0, 0, False)
                with pe.Fori(0, NG2 // 2 - 1) as it:
                    group(2 * it + 1, 1, False)
                    group(2 * it + 2, 0, False)
                group(NG2 - 2, 1, False)
                group(NG2 - 1, 0, True)

            @block.scalar
            def _(act):
                def h3_high(g, p):
                    for k in range(KB):
                        act.wait_ge(t_h3, KB * g + k + 1)
                        act.activation(h3_hi[p][:, k, :], h_bank[k][:, :], ACT.Copy).then_inc(h3_hi_ok, 1)

                def copy_logits(g):
                    act.wait_ge(lg_mm, g + 1)
                    act.activation(lgt[:, :], h_bank[0][0:2 * NEXP, :], ACT.Copy).then_inc(lgt_ok, 1)

                def exp_logits(g):
                    act.wait_ge(lg_ok, g + 1)
                    act.activation(den[:, :, :], lg[:, :, :], ACT.Exp, scale=-1.0).then_inc(eneg_ok, 1)

                def copy_cw(g):
                    act.wait_ge(t_cw, g + 1)
                    if not is_first(g):
                        act.wait_ge(cw_st, 16 * g)
                    act.activation(cwt[:, :], h_bank[0][0:NEXP, :], ACT.Copy).then_inc(cwt_ok, 1)

                def expert(g, p, n):
                    b = (p + n) % 2
                    act.wait_ge(gu_mm, 2 * (NE * g + n) + 1)
                    act.activation(sg[b][:, :], g_bank[b][:, :], ACT.Silu).then_inc(sg_ok, 1)

                def act_high(g, p, n):
                    b = (p + n) % 2
                    act.wait_ge(af_ok, NE * g + n + 1)
                    act.activation(a_hi[b][:, :], af[b][:, :], ACT.Copy).then_inc(a_hi_ok, 1)

                def group(g, p, last):
                    expert(g, p, 0)
                    for n in range(1, NE):
                        expert(g, p, n)
                        act_high(g, p, n - 1)
                        if not last:
                            if n == 1:
                                h3_high(g + 1, 1 - p)
                            if n == 2:
                                copy_logits(g + 1)
                            if n == 3:
                                exp_logits(g + 1)
                            if n == 5:
                                copy_cw(g + 1)
                    act_high(g, p, NE - 1)

                h3_high(0, 0)
                copy_logits(0)
                exp_logits(0)
                copy_cw(0)
                with act.Fori(0, NG2 // 2) as it:
                    group(2 * it, 0, False)
                    group(2 * it + 1, 1, False)
                group(NG2 - 1, 0, True)

            @block.gpsimd
            def _(pool):
                def rstd(g):
                    pool.wait_ge(mv3_ok, T * (g + 1))
                    if not is_first(g):
                        pool.wait_ge(h3_ok, T * g)
                    pool.tensor_tensor(r3a[:, :], mv3[:, :, 1], eps2[:, :], ALU.add).then_inc(r3a_ok, 1)
                    pool.wait_ge(r3a_ok, g + 1)
                    pool.tensor_tensor(r3[:, :], r3a[:, :], mhalf2[:, :], ALU.pow).then_inc(r3_ok, 1)

                def expert(g, p, n):
                    b = (p + n) % 2
                    pool.wait_ge(sg_ok, NE * g + n + 1)
                    if n == 1:
                        pool.wait_ge(cw_in, 16 * (g + 1))
                    pool.tensor_tensor(sg[b][:, :], sg[b][:, :], cw_wide[p][:, ORDER[n], :], ALU.mult).then_inc(sgw_ok, 1)

                def group(g, p, last):
                    if not last:
                        rstd(g + 1)
                    for n in range(1, NE):
                        expert(g, p, n)

                pool.wait_ge(half_ok, 2)
                rstd(0)
                with pool.Fori(0, NG2 // 2) as it:
                    group(2 * it, 0, False)
                    group(2 * it + 1, 1, False)
                group(NG2 - 1, 0, True)

            @block.vector
            def _(dve):
                def moments(g, p, nth):
                    dve.wait_ge(x2_in[p], 16 * nth)
                    if not is_first(g):
                        dve.wait_ge(r3_ok, g)
                    for t in range(T):
                        dve.bn_stats(st3[:, t, :], x2t[p][:, t, :]).then_inc(st3_ok, 1)
                    dve.wait_ge(st3_ok, T * (g + 1))
                    dve.tensor_copy(held[:, 0:1], mhalf2[:, 0:1])
                    for t in range(T):
                        dve.bn_aggr(mv3[:, t, :], st3[:, t, :]).then_inc(mv3_ok, 1)

                def normalise(g, p):
                    dve.wait_ge(r3_ok, g + 1)
                    dve.wait_ge(mv3_ok, T * (g + 1))
                    if not is_first(g):
                        dve.wait_ge(t_h3, KB * g)
                    for t in range(T):
                        dve.tensor_scalar(h3[:, t, :], x2t[p][:, t, :], mv3[:, t, 0:1], r3[:, t:t + 1], ALU.subtract,
                                          ALU.mult).then_inc(h3_ok, 1)

                def h3_low(g, p):
                    for k in range(KB):
                        dve.wait_ge(h3_hi_ok, KB * g + k + 1)
                        dve.tensor_tensor(h3_lo[p][:, k, :], h_bank[k][:, :], f32(h3_hi[p][:, k, :]), ALU.subtract).then_inc(h3_lo_ok, 1)

                def sum_logits(g):
                    dve.wait_ge(t_lg, g + 1)
                    dve.tensor_copy(lg2[:, :, :], h_bank[1][:, 0:T * 2 * NEXP].rearrange("p (t n) -> p t n", t=T)).then_inc(lg2_ok, 1)
                    dve.wait_ge(lg2_ok, g + 1)
                    dve.tensor_tensor(lg[:, :, :], lg2[:, :, 0:NEXP], lg2[:, :, NEXP:2 * NEXP], ALU.add).then_inc(lg_ok, 1)

                def routing(g):
                    done = [0]

                    def step(ins):
                        done[0] += 1
                        ins.then_inc(route, 1)
                        dve.wait_ge(route, ROUTE_STEPS * g + done[0])

                    def pairs(a, n, axis):
                        return a.unsqueeze(axis).to_broadcast([P, T, n, n])

                    dve.wait_ge(eneg_ok, g + 1)
                    if not is_first(g):
                        dve.wait_ge(t_cw, g)
                    step(dve.tensor_scalar(den[:, :, :], den[:, :, :], 1.0, None, ALU.add))
                    step(dve.reciprocal(score[:, :, :], den[:, :, :]))
                    step(dve.tensor_tensor(scorec[:, :, :], score[:, :, :], corr_w[:, :].unsqueeze(1).to_broadcast([P, T, NEXP]), ALU.add))
                    halves = scorec[:, :, :].rearrange("p t (a b) -> p t a b", b=2)
                    step(dve.tensor_tensor(gsum[:, :, :], halves[:, :, :, 0], halves[:, :, :, 1], ALU.add))
                    mine, other = pairs(gsum[:, :, :], 4, 3), pairs(gsum[:, :, :], 4, 2)
                    step(dve.tensor_tensor(g_gt[:, :, :, :], other, mine, ALU.is_gt))
                    step(dve.tensor_tensor(g_eq[:, :, :, :], other, mine, ALU.is_equal))
                    step(dve.tensor_tensor(g_eq[:, :, :, :], g_eq[:, :, :, :], tri4[:, :, :].unsqueeze(1).to_broadcast([P, T, 4, 4]), ALU.mult))
                    step(dve.tensor_tensor(g_gt[:, :, :, :], g_gt[:, :, :, :], g_eq[:, :, :, :], ALU.add))
                    step(dve.reduce_sum(grank[:, :, :], g_gt[:, :, :, :], AX))
                    step(dve.tensor_scalar(gmask[:, :, :], grank[:, :, :], 2.0, None, ALU.is_lt))
                    step(dve.tensor_tensor(choice[:, :, :].rearrange("p t (a b) -> p t a b", b=2), halves,
                                           gmask[:, :, :].unsqueeze(3).to_broadcast([P, T, 4, 2]), ALU.mult))
                    mine, other = pairs(choice[:, :, :], 8, 3), pairs(choice[:, :, :], 8, 2)
                    step(dve.tensor_tensor(e_gt[:, :, :, :], other, mine, ALU.is_gt))
                    step(dve.tensor_tensor(e_eq[:, :, :, :], other, mine, ALU.is_equal))
                    step(dve.tensor_tensor(e_eq[:, :, :, :], e_eq[:, :, :, :], tri8[:, :, :].unsqueeze(1).to_broadcast([P, T, 8, 8]), ALU.mult))
                    step(dve.tensor_tensor(e_gt[:, :, :, :], e_gt[:, :, :, :], e_eq[:, :, :, :], ALU.add))
                    step(dve.reduce_sum(erank[:, :, :], e_gt[:, :, :, :], AX))
                    step(dve.tensor_scalar(erank[:, :, :], erank[:, :, :], 4.0, None, ALU.is_lt))
                    step(dve.tensor_tensor(wsel[:, :, :], score[:, :, :], erank[:, :, :], ALU.mult))
                    step(dve.reduce_sum(wsum[:, :], wsel[:, :, :], AX))
                    step(dve.tensor_scalar(wsum[:, :], wsum[:, :], ROUTE_TINY, None, ALU.add))
                    step(dve.reciprocal(winv[:, :], wsum[:, :]))
                    step(dve.tensor_tensor(wsel[:, :, :], wsel[:, :, :], winv[:, :].unsqueeze(2).to_broadcast([P, T, NEXP]), ALU.mult))
                    step(dve.tensor_scalar(cw[:, :, :], wsel[:, :, :], EXPERT_SCALE, None, ALU.mult))
                    assert done[0] == ROUTE_STEPS

                def product(g, p, n):
                    b = (p + n) % 2
                    dve.wait_ge(gu_mm, 2 * (NE * g + n) + 2)
                    if n == 0:
                        dve.wait_ge(sg_ok, NE * g + 1)
                    else:
                        dve.wait_ge(sgw_ok, NEXP * g + n)
                    dve.tensor_tensor(af[b][:, :], u_bank[b][:, :], sg[b][:, :], ALU.mult).then_inc(af_ok, 1)

                def act_low(g, p, n):
                    b = (p + n) % 2
                    dve.wait_ge(a_hi_ok, NE * g + n + 1)
                    dve.tensor_tensor(a_lo[b][:, :], af[b][:, :], f32(a_hi[b][:, :]), ALU.subtract).then_inc(a_lo_ok, 1)

                def finish(g, p):
                    dve.wait_ge(y_mm, g + 1)
                    for q in range(2):
                        x2q = x2t[p][:, 2 * q:2 * q + 2, :]
                        dve.tensor_tensor(x2q, y_bank[q][:, :].rearrange("p (t d) -> p t d", t=2), x2q, ALU.add).then_inc(out_ok, 1)

                def group(g, p, nth, last):
                    if not last:
                        moments(g + 1, 1 - p, nth)
                    product(g, p, 0)
                    if not last:
                        normalise(g + 1, 1 - p)
                    for n in range(1, NE):
                        product(g, p, n)
                        act_low(g, p, n - 1)
                        if not last:
                            if n == 1:
                                h3_low(g + 1, 1 - p)
                            if n == 3:
                                sum_logits(g + 1)
                            if n == 4:
                                routing(g + 1)
                    act_low(g, p, NE - 1)
                    finish(g, p)

                def split_expert(e):
                    dve.wait_ge(wx_in[e], 48)
                    dve.tensor_copy(wgu_hi[:, e, :, :, :], wgu_f[:, e, :, :, :])
                    dve.tensor_copy(wd_hi[:, e, :], wd_f[:, e, :]).then_inc(w_hi_ok, 1)
                    dve.wait_ge(w_hi_ok, ORDER.index(e) + 1)
                    dve.tensor_tensor(wgu_lo[:, e, :, :, :], wgu_f[:, e, :, :, :], f32(wgu_hi[:, e, :, :, :]), ALU.subtract)
                    dve.tensor_tensor(wd_lo[:, e, :], wd_f[:, e, :], f32(wd_hi[:, e, :]), ALU.subtract).then_inc(w_lo_ok, 1)

                dve.memset(mhalf2[:, :], -0.5).then_inc(half_ok, 1)
                dve.memset(eps2[:, :], LN_EPS).then_inc(half_ok, 1)
                dve.wait_ge(half_ok, 2)
                moments(0, 0, 1)
                dve.wait_ge(wk_in, 64)
                dve.tensor_copy(gate[:, :, 0:NEXP], gate_f[:, :, :]).then_inc(gate_hi_ok, 1)
                dve.wait_ge(gate_hi_ok, 1)
                dve.tensor_tensor(gate[:, :, NEXP:2 * NEXP], gate_f[:, :, :], f32(gate[:, :, 0:NEXP]), ALU.subtract).then_inc(gate_ok, 1)
                normalise(0, 0)
                split_expert(ORDER[0])
                h3_low(0, 0)
                split_expert(ORDER[1])
                sum_logits(0)
                routing(0)
                for e in ORDER[2:]:
                    split_expert(e)
                with dve.Fori(0, NG2 // 2) as it:
                    group(2 * it, 0, it + 1, False)
                    group(2 * it + 1, 1, it + 2, False)
                group(NG2 - 1, 0, None, True)


def kernel(**inputs):
    import concourse.bacc as bacc
    from concourse.bass_utils import run_bass_kernel_spmd

    a = {k: np.asarray(v) for k, v in inputs.items()}
    D = a["x"].shape[2]
    att, xat, ffn = (lambda n, p=p: a[f"L0_{p}_{n}"] for p in ("attn", "xattn", "ffn"))

    def columns(v):
        return v.reshape(-1, P).T

    arrays = {
        "x": a["x"], "ctx": a["ctx_1024"], "ctx_t": a["ctx_1024"].transpose(0, 2, 1),
        "norm_w": columns(att("norm_w")), "norm_b": columns(att("norm_b")), "qkv_wt": att("qkv_w").T,
        "qk_b": att("qkv_b")[:2 * D], "v_b": columns(att("qkv_b")[2 * D:]),
        "proj_wt": att("proj_w").T, "proj_b": att("proj_b"),
        "w_cq": columns(xat("w_cq")), "b_cq": xat("b_cq").reshape(1), "w_c": xat("w_c"), "b_c": xat("b_c").reshape(1),
        "w_q": columns(xat("w_q")), "b_q": xat("b_q").reshape(1), "wl_t": xat("W_l").T, "b_l": xat("b_l"),
        "gate_t": ffn("gate_w").T, "corr": ffn("correction_bias"), "wg": ffn("Wg"), "wu": ffn("Wu"), "wd": ffn("Wd"),
        "wg_s": ffn("Wg_s"), "wu_s": ffn("Wu_s"), "wd_s": ffn("Wd_s"),
        "ident_in": np.eye(P, dtype=np.float32), "tri8_in": np.tri(8, 8, -1, dtype=np.float32),
        "tri4_in": np.tri(4, 4, -1, dtype=np.float32), "diag_in": np.eye(STREAMS, dtype=np.float32),
    }
    nc = bacc.Bacc("TRN2", target_bir_lowering=False, num_devices=1)
    arrays = {k: np.ascontiguousarray(v) for k, v in arrays.items()}
    aps = {k: nc.dram_tensor(f"in_{k}", v.shape, mybir.dt.from_np(v.dtype), kind="ExternalInput").ap() for k, v in arrays.items()}
    out = nc.dram_tensor("out_dram", a["x"].shape, F32, kind="ExternalOutput").ap()
    decoder_layer(nc, **aps, out=out)
    r = run_bass_kernel_spmd(nc, [{f"in_{k}": v for k, v in arrays.items()}], core_ids=[0])
    return r.results[0]["out_dram"]
```

```python
from contextlib import ExitStack

import numpy as np

import concourse.bass as bass
from concourse import mybir

F32 = mybir.dt.float32
F32R = mybir.dt.float32r
ALU = mybir.AluOpType
ACT = mybir.ActivationFunctionType
AX = mybir.AxisListType.X

P = 128
STREAMS = 4
LN_EPS = 1e-5
NEXP = 8
EXPERT_SCALE = 2.5
ROUTE_TINY = 1e-20
FFN_TOKENS = 512
FFN_TILES = FFN_TOKENS // P


def is_first(g):
    return isinstance(g, int) and g == 0


def f32(ap):
    return ap.bitcast(F32)


def decoder_layer(nc, x, ctx, ctx_t, norm_w, norm_b, qkv_wt, qk_b, v_b, proj_wt, proj_b, w_cq, b_cq, w_c, b_c,
                  w_q, b_q, wl_t, b_l, gate_t, corr, wg, wu, wd, wg_s, wu_s, wd_s, ident_in, tri8_in,
                  tri4_in, diag_in, out):
    B, L, D = x.shape
    S = ctx.shape[1]
    KB = D // P
    I = wg.shape[2]
    G = STREAMS
    NGRP = B // G
    SB = 125
    NSB = S // SB
    SP_ = S + S % 2
    TOK = G * L
    PAIRS = G // 2
    ATT_SCALE = float(1.0 / np.sqrt(L))
    NT = B * L
    NG2 = NT // FFN_TOKENS
    NE = NEXP + 1
    assert D == 256 and I == P and NSB * SB == S and NG2 * FFN_TOKENS == NT and NG2 % 2 == 1

    x2_dram = nc.dram_tensor("x2_scratch", (NT, D), F32, kind="Internal").ap()
    cw_dram = nc.dram_tensor("cw_scratch", (2, NEXP, FFN_TOKENS), F32, kind="Internal").ap()

    def mm3(pe, dst, a_hi, a_lo, b_hi, b_lo, first, last, **kw):
        pe.matmul(dst, a_lo, b_hi, start=first, stop=False, **kw)
        pe.matmul(dst, a_hi, b_lo, start=False, stop=False, **kw)
        return pe.matmul(dst, a_hi, b_hi, start=False, stop=last, **kw)

    outer = ExitStack()
    with outer:
        bank = [outer.enter_context(nc.psum_tensor(f"bank{n}", [P, 512], F32)) for n in range(8)]
        ident = outer.enter_context(nc.sbuf_tensor("ident", [P, P], F32))
        held = outer.enter_context(nc.sbuf_tensor("held", [P, 1 + STREAMS], F32))
        x2_st = outer.enter_context(nc.semaphore("x2_stored"))

        with ExitStack() as c1:
            def sb(name, shape, dt=F32):
                return c1.enter_context(nc.sbuf_tensor(name, shape, dt))

            def sem(name):
                return c1.enter_context(nc.semaphore(name))

            v_bank = bank[4:6]
            z_bank = bank[4:6]
            m_bank = bank[6]

            ctxf = sb("ctxf", [P, G, NSB, D])
            tmp_all = sb("tmp", [P, G, 512])
            staging = ctxf[:, :, :, :].rearrange("p g b d -> p (g b d)")
            wqkv_f = staging[:, 0:3 * KB * D].rearrange("p (k n) -> p k n", k=KB)
            wp_f = staging[:, 3 * KB * D:4 * KB * D].rearrange("p (k n) -> p k n", k=KB)
            wl_f = tmp_all[:, :, :].rearrange("p g (k n) -> p (g k) n", n=D)
            wqkv_hi, wqkv_lo = sb("wqkv_hi", [P, KB, 3 * D], F32R), sb("wqkv_lo", [P, KB, 3 * D], F32R)
            wp_hi, wp_lo = sb("wp_hi", [P, KB, D], F32R), sb("wp_lo", [P, KB, D], F32R)
            wl_hi, wl_lo = sb("wl_hi", [P, 4 * KB, D], F32R), sb("wl_lo", [P, 4 * KB, D], F32R)
            nw, nb = sb("nw", [P, KB]), sb("nb", [P, KB])
            nb_wide = sb("nb_wide", [P, KB, L])
            qk_bias, qk_bias0 = sb("qk_bias", [L, 2 * D]), sb("qk_bias0", [L, 2 * D])
            v_bias, v_bias0 = sb("v_bias", [P, KB]), sb("v_bias0", [P, KB])
            pb_wide, bl_wide, wc_wide = sb("pb_wide", [L, D]), sb("bl_wide", [L, D]), sb("wc_wide", [L, D])
            wcq, wq = sb("wcq", [P, KB]), sb("wq", [P, KB])
            b3, b_sum = sb("b3", [L, 3]), sb("b_sum", [L, 1])
            diag = sb("diag", [L, G, G])
            mhalf, eps, one, mone, pheld = (sb(n, [L, G]) for n in ("mhalf", "eps", "one", "mone", "pheld"))

            xt = sb("xt", [L, G, D])
            st1, mv1 = sb("st1", [L, G, 6]), sb("mv1", [L, G, 2])
            ln1 = sb("ln1", [L, 10, G])
            hh = sb("hh", [L, G, D])
            res = sb("res", [L, G, D])
            h_hi, h_lo = sb("h_hi", [P, KB, TOK], F32R), sb("h_lo", [P, KB, TOK], F32R)
            v_hi, v_lo = sb("v_hi", [P, KB, TOK], F32R), sb("v_lo", [P, KB, TOK], F32R)
            op_hi = [sb(f"op_hi{j}", [P, 512], F32R) for j in range(G)]
            op_lo = [sb(f"op_lo{j}", [P, 512], F32R) for j in range(G)]
            tmp = [tmp_all[:, j, :] for j in range(G)]
            smx, ssum, sinv = sb("smx", [P, G, 2]), sb("ssum", [P, G, 2]), sb("sinv", [P, G, 2])
            x1 = sb("x1", [L, G, D])
            st2, mv2, r2a, r2 = sb("st2", [L, G, 6]), sb("mv2", [L, G, 2]), sb("r2a", [L, G]), sb("r2", [L, G])
            c = sb("c", [L, G, D])
            cwc, rdot = sb("cwc", [L, D]), sb("rdot", [L, G])
            ct = sb("ct", [P, G, KB, L])
            c_hi, c_lo = sb("c_hi", [P, G, KB, L], F32R), sb("c_lo", [P, G, KB, L], F32R)
            ctw = sb("ctw", [P, G, KB, L])
            cw_hi, cw_lo = sb("cw_hi", [P, G, KB, L], F32R), sb("cw_lo", [P, G, KB, L], F32R)
            ctxtf = sb("ctxtf", [P, G, KB, S])
            ctx_hi, ctx_lo = sb("ctx_hi", [SB, G, NSB, D], F32R), sb("ctx_lo", [SB, G, NSB, D], F32R)
            ctxt_hi, ctxt_lo = sb("ctxt_hi", [P, G, KB, SP_], F32R), sb("ctxt_lo", [P, G, KB, SP_], F32R)
            smx2, ssum2, sinv2 = sb("smx2", [L, G]), sb("ssum2", [L, G]), sb("sinv2", [L, G])
            m4 = sb("m4", [L, G])
            mneg, msum, minv = sb("mneg", [G, 1]), sb("msum", [G, 1]), sb("minv", [G, 1])
            mexp, mrow = sb("mexp", [G, L]), sb("mrow", [G, L])
            b4 = sb("b4", [L, G])
            bm = sb("bm", [L, G, G])
            q2c_row, q2c = sb("q2c_row", [G, D]), sb("q2c", [P, KB, G])
            x4 = ctw
            x4_hi, x4_lo = cw_hi, cw_lo

            w_in, x_in = sem("weights_in"), sem("x_in")
            cx_in = [sem(f"context{j}_in") for j in range(G)]
            wide = sem("nb_widened")
            w_split, bias_mm, bias_ok = sem("weights_split"), sem("bias_product"), sem("bias_ready")
            consts = sem("constants_set")
            st1_ok, mv1_ok, ln1_step = sem("ln1_stats"), sem("ln1_moments"), sem("ln1_scalars")
            hh_ok, res0_ok, res_ok = sem("hh_ready"), sem("residual_scaled"), sem("residual_ready")
            t_h, h_hi_ok, h_lo_ok = sem("h_transposed"), sem("h_hi_ready"), sem("h_lo_ready")
            qk_mm, qk_f_ok, qk_hi_ok, qk_lo_ok = sem("qk_product"), sem("qk_biased"), sem("qk_hi_ready"), sem("qk_lo_ready")
            v_mm, v_hi_ok, v_lo_ok = sem("v_product"), sem("v_hi_ready"), sem("v_lo_ready")
            sc_mm, smx_ok, exp_ok, sinv_ok = sem("scores_product"), sem("scores_max"), sem("scores_exp"), sem("scores_inv_sum")
            w_hi_ok, w_lo_ok = sem("probs_hi_ready"), sem("probs_lo_ready")
            g_mm, g_hi_ok, g_lo_ok = sem("probs_proj_product"), sem("probs_proj_hi"), sem("probs_proj_lo")
            ao_mm, x1_ok, st2_ok, mv2_ok = sem("attention_out"), sem("x1_ready"), sem("ln2_stats"), sem("ln2_moments")
            r2a_ok, r2_ok, c_ok, x1b_ok = sem("ln2_var_eps"), sem("ln2_rstd"), sem("c_ready"), sem("x1_biased")
            rdot_ok = sem("row_term_ready")
            t_c, ct_ok, c_hi_ok, c_lo_ok = sem("c_transposed"), sem("ct_ready"), sem("c_hi_ready"), sem("c_lo_ready")
            ctw_ok, cw_hi_ok, cw_lo_ok = sem("c_weighted"), sem("cw_hi_ready"), sem("cw_lo_ready")
            cx_hi_ok, cx_lo_ok = sem("context_hi_ready"), sem("context_lo_ready")
            s_mm, smx2_ok, exp2_ok, sinv2_ok = sem("similarity"), sem("sim_max"), sem("sim_exp"), sem("sim_inv_sum")
            m4_ok = sem("row_max_ready")
            t_a, a_hi_ok, a_lo_ok = sem("a_transposed"), sem("a_hi_ready"), sem("a_lo_ready")
            c2q_mm, c2q_ok, x3_ok = sem("c2q_product"), sem("c2q_copied"), sem("c_c2q_ready")
            t_x, x_hi_ok, x_lo_ok = sem("x23_transposed"), sem("x23_hi_ready"), sem("x23_lo_ready")
            t_m, mneg_ok, mexp_ok, minv_ok, mrow_ok = sem("m_transposed"), sem("m_max"), sem("m_exp"), sem("m_inv_sum"), sem("b_att_rows")
            t_b, b4_ok, bm_ok, q2c_mm, q2cr_ok = sem("b_att_transposed"), sem("b_att_columns"), sem("b_att_masked"), sem("q2c_product"), sem("q2c_rows")
            t_q, q2c_ok, x4_ok, x4_hi_ok, x4_lo_ok = sem("q2c_transposed"), sem("q2c_ready"), sem("x4_ready"), sem("x4_hi_ready"), sem("x4_lo_ready")
            z_mm, x2_ok = sem("z_product"), sem("x2_ready")
            smx_raw, b_sum_ok = sem("scores_max_raw"), sem("b_sum_ready")

            NSETUP = 17
            x_tiles = x.rearrange("b t d -> t b d")
            x2_tiles = x2_dram.rearrange("(b t) d -> t b d", t=L)
            LN1_STEPS = 10

            block = c1.enter_context(nc.Block())

            @block.sync
            def _(sp):
                sp.dma_start(xt[:, :, :], x_tiles[:, 0:G, :]).then_inc(x_in, 16)
                sp.dma_start(ident[:, :], ident_in).then_inc(w_in, 16)
                sp.dma_start(nw[:, :], norm_w).then_inc(w_in, 16)
                sp.dma_start(nb[:, :], norm_b).then_inc(w_in, 16)
                sp.dma_start(wqkv_f[:, :, :], qkv_wt.rearrange("(k p) n -> p k n", p=P)).then_inc(w_in, 16)
                sp.dma_start(qk_bias0[:, :], qk_b.partition_broadcast(L)).then_inc(w_in, 16)
                sp.dma_start(v_bias0[:, :], v_b).then_inc(w_in, 16)
                sp.dma_start(wp_f[:, :, :], proj_wt.rearrange("(k p) n -> p k n", p=P)).then_inc(w_in, 16)
                sp.dma_start(wl_f[:, :, :], wl_t.rearrange("(k p) n -> p k n", p=P)).then_inc(w_in, 16)
                sp.dma_start(pb_wide[:, :], proj_b.partition_broadcast(L)).then_inc(w_in, 16)
                sp.dma_start(bl_wide[:, :], b_l.partition_broadcast(L)).then_inc(w_in, 16)
                sp.dma_start(wc_wide[:, :], w_c.partition_broadcast(L)).then_inc(w_in, 16)
                sp.dma_start(wcq[:, :], w_cq).then_inc(w_in, 16)
                sp.dma_start(wq[:, :], w_q).then_inc(w_in, 16)
                sp.dma_start(diag[:, :, :], diag_in.partition_broadcast(L)).then_inc(w_in, 16)
                for n, b in enumerate((b_cq, b_c, b_q)):
                    sp.dma_start(b3[:, n:n + 1], b.partition_broadcast(L)).then_inc(w_in, 16)

                def load_context(batch, j):
                    sp.dma_start(ctxtf[:, j, :, :], ctx_t[bass.ds(batch + j, 1)].rearrange("o (k p) s -> p (o k) s", p=P)).then_inc(cx_in[j], 16)
                    sp.dma_start(ctxf[0:SB, j, :, :], ctx[bass.ds(batch + j, 1)].rearrange("o (k p) d -> p (o k) d", p=SB)).then_inc(cx_in[j], 16)

                def group(i, last):
                    batch = sp.snap(G * i)
                    if not last:
                        sp.wait_ge(hh_ok, G * (i + 1))
                        sp.wait_ge(res0_ok, G * (i + 1))
                        sp.wait_ge(w_in, 16)
                        sp.dma_start(xt[:, :, :], x_tiles[:, bass.ds(batch + G, G), :]).then_inc(x_in, 16)
                        for j in range(G):
                            sp.wait_ge(cx_lo_ok, G * i + j + 1)
                            sp.wait_ge(w_in, 16)
                            load_context(batch + G, j)
                    sp.wait_ge(x2_ok, PAIRS * (i + 2))
                    sp.wait_ge(w_in, 16)
                    sp.dma_start(x2_tiles[:, bass.ds(batch, G), :], x1[:, :, :]).then_inc(x2_st, 16)

                sp.wait_ge(w_split, 2 * (KB + 2))
                sp.wait_ge(bias_mm, 1)
                for j in range(G):
                    load_context(0, j)
                with sp.Fori(0, NGRP - 1) as i:
                    group(i, False)
                group(NGRP - 1, True)
                sp.wait_ge(x2_st, 16 * (NGRP + 1))

            @block.tensor
            def _(pe):
                pe.wait_ge(wide, 1)
                for k in range(KB):
                    pe.matmul(m_bank[0:L, :], nb_wide[:, k, :], wqkv_f[:, k, 0:2 * D], start=(k == 0), stop=(k == KB - 1))
                for half in range(KB):
                    for k in range(KB):
                        last = pe.matmul(v_bank[0][:, half:half + 1], wqkv_f[:, k, 2 * D + half * P:2 * D + (half + 1) * P],
                                         nb[:, k:k + 1], start=(k == 0), stop=(k == KB - 1))
                last.then_inc(bias_mm, 1)
                pe.wait_ge(bias_ok, 2)
                pe.wait_ge(w_split, 2 * (KB + 2))

                def turn_h(g):
                    for j in range(G):
                        pe.wait_ge(hh_ok, G * g + j + 1)
                        for k in range(KB):
                            t = pe.transpose(bank[j][:, k * L:(k + 1) * L], hh[:, j, k * P:(k + 1) * P], ident[0:L, 0:L])
                        t.then_inc(t_h, 1)

                def z_of(j):
                    return z_bank[j // 2][0:L, (j % 2) * D:(j % 2 + 1) * D]

                def group(i, last_group):
                    ev = [G * i + j + 1 for j in range(G)]
                    for j in range(G):
                        pe.wait_ge(h_lo_ok, ev[j])
                        for k in range(KB):
                            t = slice(j * L, (j + 1) * L)
                            last = mm3(pe, bank[j][0:L, :], h_hi[:, k, t], h_lo[:, k, t], wqkv_hi[:, k, 0:2 * D],
                                       wqkv_lo[:, k, 0:2 * D], k == 0, k == KB - 1)
                        last.then_inc(qk_mm, 1)

                    def scores(j):
                        pe.wait_ge(qk_lo_ok, ev[j])
                        for half in range(KB):
                            q = slice(half * P, (half + 1) * P)
                            last = mm3(pe, bank[j][:, half * D:(half + 1) * D], op_hi[j][0:L, q], op_lo[j][0:L, q],
                                       op_hi[j][0:L, D:2 * D], op_lo[j][0:L, D:2 * D], True, True)
                        last.then_inc(sc_mm, 1)

                    def v_product(half):
                        n = slice(2 * D + half * P, 2 * D + (half + 1) * P)
                        for k in range(KB):
                            last = mm3(pe, v_bank[half][:, 0:TOK], wqkv_hi[:, k, n], wqkv_lo[:, k, n], h_hi[:, k, :], h_lo[:, k, :],
                                       k == 0, k == KB - 1)
                        last.then_inc(v_mm, 1)

                    scores(0)
                    pe.wait_ge(x2_ok, PAIRS * (i + 1))
                    v_product(0)
                    scores(1)
                    scores(2)
                    v_product(1)
                    scores(3)
                    for j in range(G):
                        pe.wait_ge(w_lo_ok, ev[j])
                        for half in range(KB):
                            for q in range(KB):
                                n = slice(q * D + half * P, q * D + (half + 1) * P)
                                last = mm3(pe, bank[j][:, half * D:(half + 1) * D], op_hi[j][:, n], op_lo[j][:, n],
                                           wp_hi[:, q, :], wp_lo[:, q, :], q == 0, q == KB - 1)
                        last.then_inc(g_mm, 1)
                    pe.wait_ge(v_lo_ok, KB * (i + 1))
                    for j in range(G):
                        pe.wait_ge(g_lo_ok, ev[j])
                        t = slice(j * L, (j + 1) * L)
                        for k in range(KB):
                            n = slice(k * D, (k + 1) * D)
                            last = mm3(pe, bank[j][0:L, 0:D], v_hi[:, k, t], v_lo[:, k, t], op_hi[j][:, n], op_lo[j][:, n],
                                       k == 0, k == KB - 1)
                        last.then_inc(ao_mm, 1)
                    for j in range(G):
                        pe.wait_ge(c_ok, ev[j])
                        for k in range(KB):
                            last = pe.transpose(bank[j][:, k * L:(k + 1) * L], c[:, j, k * P:(k + 1) * P], ident[0:L, 0:L])
                        last.then_inc(t_c, 1)

                    def z_c(j):
                        for k in range(KB):
                            mm3(pe, z_of(j), c_hi[:, j, k, :], c_lo[:, j, k, :], wl_hi[:, k, :], wl_lo[:, k, :],
                                k == 0 and j % 2 == 0, False, skip_group_check=True)

                    for j in range(2):
                        pe.wait_ge(c_lo_ok, ev[j])
                        z_c(j)
                    for j in range(G):
                        pe.wait_ge(cw_lo_ok, ev[j])
                        pe.wait_ge(c_lo_ok, ev[j])
                        pe.wait_ge(cx_lo_ok, ev[j])
                        for k in range(KB):
                            last = mm3(pe, bank[j][0:L, 0:SP_], cw_hi[:, j, k, :], cw_lo[:, j, k, :], ctxt_hi[:, j, k, :],
                                       ctxt_lo[:, j, k, :], k == 0, k == KB - 1)
                        last.then_inc(s_mm, 1)
                    for j in range(2, G):
                        z_c(j)
                    for j in range(G):
                        pe.wait_ge(exp2_ok, ev[j])
                        for b in range(NSB):
                            last = pe.transpose(bank[j][0:SB, b * L:(b + 1) * L], tmp[j][0:L, b * SB:(b + 1) * SB], ident[0:L, 0:L])
                        last.then_inc(t_a, 1)
                    pe.wait_ge(m4_ok, G * (i + 1))
                    pe.transpose(m_bank[0:G, 0:L], m4[:, :], ident[0:L, 0:L]).then_inc(t_m, 1)
                    for j in range(G):
                        pe.wait_ge(a_lo_ok, ev[j])
                        for b in range(NSB):
                            t = slice(b * L, (b + 1) * L)
                            last = mm3(pe, bank[j][0:L, 0:D], op_hi[j][0:SB, t], op_lo[j][0:SB, t], ctx_hi[:, j, b, :],
                                       ctx_lo[:, j, b, :], b == 0, b == NSB - 1)
                        last.then_inc(c2q_mm, 1)
                    for j in range(2):
                        if j == 0:
                            pe.wait_ge(mrow_ok, i + 1)
                        pe.wait_ge(x3_ok, ev[j])
                        for k in range(2 * KB):
                            last = pe.transpose(bank[j][:, k * L:(k + 1) * L], tmp[j][0:L, k * P:(k + 1) * P], ident[0:L, 0:L])
                        last.then_inc(t_x, 1)
                        if j == 0:
                            pe.transpose(m_bank[0:L, P:P + G], mrow[:, :], ident[0:G, 0:G]).then_inc(t_b, 1)
                    pe.wait_ge(bm_ok, i + 1)
                    for j in range(G):
                        last = pe.matmul(m_bank[0:G, D:2 * D], bm[:, j, :], c[:, j, :], start=(j == 0), stop=(j == G - 1))
                    last.then_inc(q2c_mm, 1)
                    for j in range(2, G):
                        pe.wait_ge(x3_ok, ev[j])
                        for k in range(2 * KB):
                            last = pe.transpose(bank[j][:, k * L:(k + 1) * L], tmp[j][0:L, k * P:(k + 1) * P], ident[0:L, 0:L])
                        last.then_inc(t_x, 1)
                    for j in range(G):
                        pe.wait_ge(x_lo_ok, ev[j])
                        if j == 0:
                            pe.wait_ge(q2cr_ok, i + 1)
                        for k in range(2 * KB):
                            t = slice(k * L, (k + 1) * L)
                            mm3(pe, z_of(j), op_hi[j][:, t], op_lo[j][:, t], wl_hi[:, KB + k, :], wl_lo[:, KB + k, :], False, False,
                                skip_group_check=True)
                            if j == 0 and k == 0:
                                for h in range(KB):
                                    last = pe.transpose(m_bank[:, h * G:(h + 1) * G], q2c_row[:, h * P:(h + 1) * P], ident[0:G, 0:G])
                                last.then_inc(t_q, 1)
                    if not last_group:
                        turn_h(i + 1)
                    pe.wait_ge(x4_lo_ok, i + 1)
                    for j in range(G):
                        for k in range(KB):
                            last = mm3(pe, z_of(j), x4_hi[:, j, k, :], x4_lo[:, j, k, :], wl_hi[:, 3 * KB + k, :],
                                       wl_lo[:, 3 * KB + k, :], False, k == KB - 1, skip_group_check=True)
                        if j % 2:
                            last.then_inc(z_mm, 1)

                turn_h(0)
                with pe.Fori(0, NGRP - 1) as i:
                    group(i, False)
                group(NGRP - 1, True)

            @block.scalar
            def _(act):
                def residual(g):
                    act.wait_ge(x_in, 16 * (g + 1))
                    act.wait_ge(ln1_step, LN1_STEPS * (g + 1))
                    if not is_first(g):
                        act.wait_ge(x1_ok, G * g)
                    for j in range(G):
                        act.activation(res[:, j, :], xt[:, j, :], ACT.Identity, bias=ln1[:, 9, j:j + 1],
                                       scale=ln1[:, 7, j:j + 1]).then_inc(res0_ok, 1)

                def context_hi(i, j):
                    act.wait_ge(cx_in[j], 32 * (i + 1))
                    act.activation(ctxt_hi[:, j, :, 0:S], ctxtf[:, j, :, :], ACT.Copy)
                    act.activation(ctx_hi[:, j, :, :], ctxf[0:SB, j, :, :], ACT.Copy).then_inc(cx_hi_ok, 1)

                def h_high(g):
                    for j in range(G):
                        act.wait_ge(t_h, G * g + j + 1)
                        act.activation(h_hi[:, :, j * L:(j + 1) * L], bank[j][:, 0:KB * L].rearrange("p (k t) -> p k t", k=KB),
                                       ACT.Copy).then_inc(h_hi_ok, 1)

                def group(i, last):
                    ev = [G * i + j + 1 for j in range(G)]

                    def qk_high(j):
                        act.wait_ge(qk_f_ok, ev[j])
                        act.activation(op_hi[j][0:L, :], tmp[j][0:L, :], ACT.Copy).then_inc(qk_hi_ok, 1)

                    def exps(j):
                        act.wait_ge(smx_ok, ev[j])
                        for half in range(KB):
                            n = slice(half * D, (half + 1) * D)
                            e = act.activation(tmp[j][:, n], bank[j][:, n], ACT.Exp, bias=smx[:, j, half:half + 1], scale=ATT_SCALE,
                                               accum_out=ssum[:, j, half:half + 1])
                        e.then_inc(exp_ok, 1)

                    def probs_high(j):
                        act.wait_ge(sinv_ok, ev[j])
                        for half in range(KB):
                            n = slice(half * D, (half + 1) * D)
                            w = act.activation(op_hi[j][:, n], tmp[j][:, n], ACT.Copy, scale=sinv[:, j, half:half + 1])
                        w.then_inc(w_hi_ok, 1)

                    qk_high(0)
                    qk_high(1)
                    context_hi(i, 3)
                    qk_high(2)
                    qk_high(3)
                    exps(0)
                    probs_high(0)
                    exps(1)
                    exps(2)
                    probs_high(1)
                    exps(3)
                    probs_high(2)
                    probs_high(3)
                    for half in range(KB):
                        act.wait_ge(v_mm, KB * i + half + 1)
                        act.activation(v_hi[:, half, :], v_bank[half][:, 0:TOK], ACT.Identity,
                                       bias=v_bias[:, half:half + 1]).then_inc(v_hi_ok, 1)
                    for j in range(G):
                        act.wait_ge(g_mm, ev[j])
                        act.activation(op_hi[j][:, :], bank[j][:, :], ACT.Copy).then_inc(g_hi_ok, 1)
                    for j in range(G):
                        act.wait_ge(t_c, ev[j])
                        tc = bank[j][:, 0:KB * L].rearrange("p (k t) -> p k t", k=KB)
                        act.activation(ct[:, j, :, :], tc, ACT.Copy).then_inc(ct_ok, 1)
                        act.activation(c_hi[:, j, :, :], tc, ACT.Copy).then_inc(c_hi_ok, 1)
                    for j in range(G):
                        act.wait_ge(ctw_ok, ev[j])
                        act.activation(cw_hi[:, j, :, :], ctw[:, j, :, :], ACT.Copy).then_inc(cw_hi_ok, 1)
                    for j in range(G):
                        act.wait_ge(smx2_ok, ev[j])
                        act.activation(tmp[j][0:L, 0:S], bank[j][0:L, 0:S], ACT.Exp, bias=smx2[:, j:j + 1],
                                       accum_out=ssum2[:, j:j + 1]).then_inc(exp2_ok, 1)
                    for j in range(G):
                        act.wait_ge(t_a, ev[j])
                        act.activation(op_hi[j][0:SB, 0:NSB * L], bank[j][0:SB, 0:NSB * L], ACT.Copy).then_inc(a_hi_ok, 1)
                    act.wait_ge(mneg_ok, i + 1)
                    act.activation(mexp[:, :], m_bank[0:G, 0:L], ACT.Exp, bias=mneg[:, :], accum_out=msum[:, :]).then_inc(mexp_ok, 1)
                    for j in range(G):
                        act.wait_ge(c2q_mm, ev[j])
                        act.wait_ge(sinv2_ok, ev[j])
                        act.activation(tmp[j][0:L, 0:D], bank[j][0:L, 0:D], ACT.Copy, scale=sinv2[:, j:j + 1]).then_inc(c2q_ok, 1)
                    for j in range(G):
                        act.wait_ge(t_x, ev[j])
                        act.activation(op_hi[j][:, 0:2 * KB * L], bank[j][:, 0:2 * KB * L], ACT.Copy).then_inc(x_hi_ok, 1)
                    if not last:
                        context_hi(i + 1, 0)
                    act.wait_ge(x4_ok, i + 1)
                    act.activation(x4_hi[:, :, :, :], x4[:, :, :, :], ACT.Copy).then_inc(x4_hi_ok, 1)
                    if not last:
                        h_high(i + 1)
                        context_hi(i + 1, 1)
                        context_hi(i + 1, 2)
                        residual(i + 1)

                residual(0)
                h_high(0)
                act.wait_ge(bias_ok, 2)
                for j in range(3):
                    context_hi(0, j)
                with act.Fori(0, NGRP - 1) as i:
                    group(i, False)
                group(NGRP - 1, True)

            @block.gpsimd
            def _(pool):
                def ln1_scalars(g):
                    pool.wait_ge(mv1_ok, G * (g + 1))
                    if not is_first(g):
                        pool.wait_ge(res0_ok, G * g)
                        pool.wait_ge(hh_ok, G * g)
                    mean, var = mv1[:, :, 0], mv1[:, :, 1]
                    row = [ln1[:, n, :] for n in range(10)]
                    done = [0]

                    def step(ins):
                        done[0] += 1
                        ins.then_inc(ln1_step, 1)
                        if done[0] < LN1_STEPS:
                            pool.wait_ge(ln1_step, LN1_STEPS * g + done[0])

                    step(pool.tensor_tensor(row[0], var, eps[:, :], ALU.add))
                    step(pool.tensor_tensor(row[1], row[0], mhalf[:, :], ALU.pow))
                    step(pool.tensor_tensor(row[2], var, row[1], ALU.mult))
                    step(pool.tensor_tensor(row[3], row[2], row[1], ALU.mult))
                    step(pool.tensor_tensor(row[4], row[3], eps[:, :], ALU.add))
                    step(pool.tensor_tensor(row[5], row[4], mhalf[:, :], ALU.pow))
                    step(pool.tensor_tensor(row[6], row[5], row[1], ALU.mult))
                    step(pool.tensor_tensor(row[7], row[1], one[:, :], ALU.add))
                    step(pool.tensor_tensor(row[8], mean, row[1], ALU.mult))
                    step(pool.tensor_tensor(row[9], row[8], mone[:, :], ALU.mult))

                def residual_bias(g):
                    for j in range(G):
                        pool.wait_ge(res0_ok, G * g + j + 1)
                        pool.tensor_tensor(res[:, j, :], res[:, j, :], pb_wide[:, :], ALU.add).then_inc(res_ok, 1)

                def context_lo(i, j):
                    pool.wait_ge(cx_hi_ok, G * i + j + 1)
                    pool.tensor_tensor(ctxt_lo[:, j, :, 0:S], ctxtf[:, j, :, :], f32(ctxt_hi[:, j, :, 0:S]), ALU.subtract)
                    pool.tensor_tensor(ctx_lo[:, j, :, :], ctxf[0:SB, j, :, :], f32(ctx_hi[:, j, :, :]), ALU.subtract).then_inc(cx_lo_ok, 1)

                def group(i, last):
                    ev = [G * i + j + 1 for j in range(G)]
                    for j in range(G):
                        pool.wait_ge(qk_hi_ok, ev[j])
                        pool.tensor_tensor(op_lo[j][0:L, :], tmp[j][0:L, :], f32(op_hi[j][0:L, :]), ALU.subtract).then_inc(qk_lo_ok, 1)
                    context_lo(i, 2)
                    residual_bias(i)
                    context_lo(i, 3)
                    for j in range(G):
                        pool.wait_ge(mv2_ok, ev[j])
                        pool.tensor_tensor(r2a[:, j:j + 1], mv2[:, j, 1:2], eps[:, j:j + 1], ALU.add).then_inc(r2a_ok, 1)
                        pool.wait_ge(r2a_ok, ev[j])
                        pool.tensor_tensor(r2[:, j:j + 1], r2a[:, j:j + 1], mhalf[:, j:j + 1], ALU.pow).then_inc(r2_ok, 1)
                    for j in range(G):
                        pool.wait_ge(ct_ok, ev[j])
                        pool.tensor_tensor(pheld[:, j:j + 1], one[:, 0:1], one[:, 0:1], ALU.add)
                        for k in range(KB):
                            w = pool.tensor_scalar(ctw[:, j, k, :], ct[:, j, k, :], wcq[:, k:k + 1], wq[:, k:k + 1], ALU.mult, ALU.add)
                        w.then_inc(ctw_ok, 1)
                    for j in range(G):
                        pool.wait_ge(c_ok, ev[j])
                        pool.tensor_tensor(x1[:, j, :], x1[:, j, :], bl_wide[:, :], ALU.add).then_inc(x1b_ok, 1)
                    if not last:
                        ln1_scalars(i + 1)
                        context_lo(i + 1, 0)
                        context_lo(i + 1, 1)

                pool.wait_ge(w_in, 16 * (NSETUP))
                pool.wait_ge(consts, 6)
                ln1_scalars(0)
                context_lo(0, 0)
                context_lo(0, 1)
                with pool.Fori(0, NGRP - 1) as i:
                    group(i, False)
                group(NGRP - 1, True)

            @block.vector
            def _(dve):
                def ln1_moments(g):
                    dve.wait_ge(x_in, 16 * (g + 1))
                    if not is_first(g):
                        dve.wait_ge(ln1_step, LN1_STEPS * g)
                    for j in range(G):
                        dve.bn_stats(st1[:, j, :], xt[:, j, :]).then_inc(st1_ok, 1)
                    dve.wait_ge(st1_ok, G * (g + 1))
                    dve.tensor_copy(held[0:L, 0:1], mhalf[:, 0:1])
                    for j in range(G):
                        dve.bn_aggr(mv1[:, j, :], st1[:, j, :]).then_inc(mv1_ok, 1)

                def normalise_h(g):
                    dve.wait_ge(ln1_step, LN1_STEPS * (g + 1))
                    if not is_first(g):
                        dve.wait_ge(t_h, G * g)
                    for j in range(G):
                        dve.tensor_scalar(hh[:, j, :], xt[:, j, :], mv1[:, j, 0:1], ln1[:, 6, j:j + 1], ALU.subtract,
                                          ALU.mult).then_inc(hh_ok, 1)

                def h_low(g):
                    for j in range(G):
                        dve.wait_ge(h_hi_ok, G * g + j + 1)
                        t = slice(j * L, (j + 1) * L)
                        dve.tensor_tensor(h_lo[:, :, t], bank[j][:, 0:KB * L].rearrange("p (k t) -> p k t", k=KB),
                                          f32(h_hi[:, :, t]), ALU.subtract).then_inc(h_lo_ok, 1)

                def group(i, last):
                    ev = [G * i + j + 1 for j in range(G)]

                    def score_max(j):
                        dve.wait_ge(sc_mm, ev[j])
                        dve.reduce_max(ssum[:, j, :], bank[j][:, :].rearrange("p (h k) -> p h k", h=KB), AX).then_inc(smx_raw, 1)
                        dve.wait_ge(smx_raw, ev[j])
                        dve.tensor_scalar(smx[:, j, :], ssum[:, j, :], -ATT_SCALE, None, ALU.mult).then_inc(smx_ok, 1)

                    def inv_sum(j):
                        dve.wait_ge(exp_ok, ev[j])
                        dve.reciprocal(sinv[:, j, :], ssum[:, j, :]).then_inc(sinv_ok, 1)

                    def probs_low(j):
                        dve.wait_ge(w_hi_ok, ev[j])
                        for half in range(KB):
                            n = slice(half * D, (half + 1) * D)
                            w = dve.scalar_tensor_tensor(op_lo[j][:, n], tmp[j][:, n], sinv[:, j, half:half + 1], f32(op_hi[j][:, n]),
                                                         ALU.mult, ALU.subtract)
                        w.then_inc(w_lo_ok, 1)

                    def x1_sum(j):
                        dve.wait_ge(ao_mm, ev[j])
                        dve.tensor_tensor(x1[:, j, :], bank[j][0:L, 0:D], res[:, j, :], ALU.add).then_inc(x1_ok, 1)

                    def x1_stats(j):
                        dve.wait_ge(x1_ok, ev[j])
                        dve.bn_stats(st2[:, j, :], x1[:, j, :]).then_inc(st2_ok, 1)

                    def x1_moments(j):
                        dve.wait_ge(st2_ok, ev[j])
                        dve.tensor_copy(held[0:L, 1 + j:2 + j], mhalf[:, 0:1])
                        dve.bn_aggr(mv2[:, j, :], st2[:, j, :]).then_inc(mv2_ok, 1)

                    def c_rows(j):
                        dve.wait_ge(r2_ok, ev[j])
                        dve.wait_ge(mv2_ok, ev[j])
                        dve.tensor_scalar(c[:, j, :], x1[:, j, :], mv2[:, j, 0:1], r2[:, j:j + 1], ALU.subtract, ALU.mult).then_inc(c_ok, 1)

                    for j in range(G):
                        dve.wait_ge(qk_mm, ev[j])
                        dve.tensor_tensor(tmp[j][0:L, :], bank[j][0:L, :], qk_bias[:, :], ALU.add).then_inc(qk_f_ok, 1)
                    score_max(0)
                    inv_sum(0)
                    score_max(1)
                    score_max(2)
                    probs_low(0)
                    inv_sum(1)
                    score_max(3)
                    inv_sum(2)
                    probs_low(1)
                    inv_sum(3)
                    probs_low(2)
                    probs_low(3)
                    for half in range(KB):
                        dve.wait_ge(v_hi_ok, KB * i + half + 1)
                        dve.scalar_tensor_tensor(v_lo[:, half, :], v_bank[half][:, 0:TOK], v_bias[:, half:half + 1],
                                                 f32(v_hi[:, half, :]), ALU.add, ALU.subtract).then_inc(v_lo_ok, 1)
                    for j in range(G):
                        dve.wait_ge(g_hi_ok, ev[j])
                        dve.tensor_tensor(op_lo[j][:, :], bank[j][:, :], f32(op_hi[j][:, :]), ALU.subtract).then_inc(g_lo_ok, 1)
                    dve.wait_ge(res_ok, G * (i + 1))
                    dve.wait_ge(x2_st, 16 * (i + 1))
                    x1_sum(0)
                    x1_sum(1)
                    x1_stats(0)
                    x1_stats(1)
                    x1_moments(0)
                    x1_sum(2)
                    x1_moments(1)
                    x1_stats(2)
                    x1_sum(3)
                    c_rows(0)
                    x1_moments(2)
                    x1_stats(3)
                    c_rows(1)
                    x1_moments(3)
                    c_rows(2)
                    c_rows(3)
                    for j in range(G):
                        dve.wait_ge(c_hi_ok, ev[j])
                        dve.tensor_tensor(c_lo[:, j, :, :], bank[j][:, 0:KB * L].rearrange("p (k t) -> p k t", k=KB),
                                          f32(c_hi[:, j, :, :]), ALU.subtract).then_inc(c_lo_ok, 1)
                    for j in range(G):
                        if j:
                            dve.wait_ge(rdot_ok, ev[j - 1])
                        else:
                            dve.wait_ge(c_ok, ev[G - 1])
                        dve.scalar_tensor_tensor(cwc[:, :], c[:, j, :], 1.0, wc_wide[:, :], ALU.mult, ALU.mult,
                                                 accum_out=rdot[:, j:j + 1]).then_inc(rdot_ok, 1)
                        dve.wait_ge(cw_hi_ok, ev[j])
                        dve.tensor_tensor(cw_lo[:, j, :, :], ctw[:, j, :, :], f32(cw_hi[:, j, :, :]), ALU.subtract).then_inc(cw_lo_ok, 1)
                    for j in range(G):
                        dve.wait_ge(s_mm, ev[j])
                        dve.reduce_max(smx2[:, j:j + 1], bank[j][0:L, 0:S], AX, negate=True).then_inc(smx2_ok, 1)
                    for j in range(G):
                        dve.wait_ge(smx2_ok, ev[j])
                        dve.scalar_tensor_tensor(m4[:, j:j + 1], rdot[:, j:j + 1], b_sum[:, 0:1], smx2[:, j:j + 1], ALU.add,
                                                 ALU.subtract).then_inc(m4_ok, 1)
                        dve.wait_ge(exp2_ok, ev[j])
                        dve.reciprocal(sinv2[:, j:j + 1], ssum2[:, j:j + 1]).then_inc(sinv2_ok, 1)
                    for j in range(G):
                        if j == 1:
                            dve.wait_ge(t_m, i + 1)
                            dve.reduce_max(mneg[:, :], m_bank[0:G, 0:L], AX, negate=True).then_inc(mneg_ok, 1)
                        dve.wait_ge(a_hi_ok, ev[j])
                        dve.tensor_tensor(op_lo[j][0:SB, 0:NSB * L], bank[j][0:SB, 0:NSB * L], f32(op_hi[j][0:SB, 0:NSB * L]),
                                          ALU.subtract).then_inc(a_lo_ok, 1)
                    dve.wait_ge(mexp_ok, i + 1)
                    dve.reciprocal(minv[:, :], msum[:, :]).then_inc(minv_ok, 1)
                    dve.wait_ge(minv_ok, i + 1)
                    dve.tensor_scalar(mrow[:, :], mexp[:, :], minv[:, 0:1], None, ALU.mult).then_inc(mrow_ok, 1)
                    for j in range(G):
                        dve.wait_ge(c2q_ok, ev[j])
                        dve.tensor_tensor(tmp[j][0:L, D:2 * D], tmp[j][0:L, 0:D], c[:, j, :], ALU.mult).then_inc(x3_ok, 1)
                        if j == 0 and not last:
                            ln1_moments(i + 1)
                        if j == 1:
                            dve.wait_ge(t_b, i + 1)
                            dve.tensor_copy(b4[:, :], m_bank[0:L, P:P + G]).then_inc(b4_ok, 1)
                            dve.wait_ge(b4_ok, i + 1)
                            dve.tensor_tensor(bm[:, :, :], diag[:, :, :], b4[:, :].unsqueeze(2).to_broadcast([L, G, G]),
                                              ALU.mult).then_inc(bm_ok, 1)
                    for j in range(G):
                        dve.wait_ge(x_hi_ok, ev[j])
                        dve.tensor_tensor(op_lo[j][:, 0:2 * KB * L], bank[j][:, 0:2 * KB * L], f32(op_hi[j][:, 0:2 * KB * L]),
                                          ALU.subtract).then_inc(x_lo_ok, 1)
                        if j == 1:
                            dve.wait_ge(q2c_mm, i + 1)
                            dve.tensor_copy(q2c_row[:, :], m_bank[0:G, D:2 * D]).then_inc(q2cr_ok, 1)
                    dve.wait_ge(t_q, i + 1)
                    dve.tensor_copy(q2c[:, :, :], m_bank[:, 0:KB * G].rearrange("p (k g) -> p k g", k=KB)).then_inc(q2c_ok, 1)
                    dve.wait_ge(q2c_ok, i + 1)
                    for k in range(KB):
                        w = dve.tensor_tensor(x4[:, :, k, :], ct[:, :, k, :], q2c[:, k, :].unsqueeze(2).to_broadcast([P, G, L]), ALU.mult)
                    w.then_inc(x4_ok, 1)
                    if not last:
                        normalise_h(i + 1)
                    dve.wait_ge(x4_hi_ok, i + 1)
                    dve.tensor_tensor(x4_lo[:, :, :, :], x4[:, :, :, :], f32(x4_hi[:, :, :, :]), ALU.subtract).then_inc(x4_lo_ok, 1)
                    if not last:
                        h_low(i + 1)
                    dve.wait_ge(x1b_ok, G * (i + 1))
                    for q in range(PAIRS):
                        dve.wait_ge(z_mm, PAIRS * i + q + 1)
                        dve.tensor_tensor(x1[:, 2 * q:2 * q + 2, :], z_bank[q][0:L, :].rearrange("p (g d) -> p g d", g=2),
                                          x1[:, 2 * q:2 * q + 2, :], ALU.add).then_inc(x2_ok, 1)

                dve.memset(mhalf[:, :], -0.5).then_inc(consts, 1)
                dve.memset(eps[:, :], LN_EPS).then_inc(consts, 1)
                dve.memset(one[:, :], 1.0).then_inc(consts, 1)
                dve.memset(mone[:, :], -1.0).then_inc(consts, 1)
                dve.memset(held[:, 0:1], 0.0).then_inc(x2_st, 16)
                dve.wait_ge(x2_st, 16)
                dve.memset(held[:, 0:1], 0.0).then_inc(x2_ok, PAIRS)
                dve.wait_ge(x2_ok, PAIRS)
                dve.memset(f32(ctxt_hi[:, :, :, S:SP_]), 0.0).then_inc(consts, 1)
                dve.memset(f32(ctxt_lo[:, :, :, S:SP_]), 0.0).then_inc(consts, 1)
                dve.wait_ge(consts, 6)
                ln1_moments(0)
                dve.wait_ge(w_in, 16 * (NSETUP))
                dve.tensor_copy(nb_wide[:, :, :], nb[:, :].unsqueeze(2).to_broadcast([P, KB, L])).then_inc(wide, 1)
                normalise_h(0)
                for k in range(KB):
                    dve.tensor_scalar(wqkv_hi[:, k, :], wqkv_f[:, k, :], nw[:, k:k + 1], None, ALU.mult).then_inc(w_split, 1)
                dve.tensor_copy(wp_hi[:, :, :], wp_f[:, :, :]).then_inc(w_split, 1)
                dve.tensor_copy(wl_hi[:, :, :], wl_f[:, :, :]).then_inc(w_split, 1)
                dve.wait_ge(w_split, KB + 2)
                for k in range(KB):
                    dve.scalar_tensor_tensor(wqkv_lo[:, k, :], wqkv_f[:, k, :], nw[:, k:k + 1], f32(wqkv_hi[:, k, :]), ALU.mult,
                                             ALU.subtract).then_inc(w_split, 1)
                dve.tensor_tensor(wp_lo[:, :, :], wp_f[:, :, :], f32(wp_hi[:, :, :]), ALU.subtract).then_inc(w_split, 1)
                dve.tensor_tensor(wl_lo[:, :, :], wl_f[:, :, :], f32(wl_hi[:, :, :]), ALU.subtract).then_inc(w_split, 1)
                dve.reduce_sum(b_sum[:, :], b3[:, :], AX).then_inc(b_sum_ok, 1)
                dve.wait_ge(b_sum_ok, 1)
                dve.wait_ge(bias_mm, 1)
                dve.tensor_tensor(qk_bias[:, :], m_bank[0:L, :], qk_bias0[:, :], ALU.add).then_inc(bias_ok, 1)
                dve.tensor_tensor(v_bias[:, :], v_bank[0][:, 0:KB], v_bias0[:, :], ALU.add).then_inc(bias_ok, 1)
                dve.wait_ge(bias_ok, 2)
                h_low(0)
                with dve.Fori(0, NGRP - 1) as i:
                    group(i, False)
                group(NGRP - 1, True)

        with ExitStack() as c2:
            def sb(name, shape, dt=F32):
                return c2.enter_context(nc.sbuf_tensor(name, shape, dt))

            def sem(name):
                return c2.enter_context(nc.semaphore(name))

            T = FFN_TILES
            g_bank, u_bank, y_bank, h_bank = bank[0:2], bank[2:4], bank[4:6], bank[6:8]
            ORDER = [NEXP] + list(range(NEXP))
            AHEAD = 2

            wgu_f = sb("wgu_f", [P, NE, 2, KB, I])
            wd_f = sb("wd_f", [P, NE, D])
            wgu_hi, wgu_lo = sb("wgu_hi", [P, NE, 2, KB, I], F32R), sb("wgu_lo", [P, NE, 2, KB, I], F32R)
            wd_hi, wd_lo = sb("wd_hi", [P, NE, D], F32R), sb("wd_lo", [P, NE, D], F32R)
            gate_f = sb("gate_f", [P, KB, NEXP])
            gate = sb("gate", [P, KB, 2 * NEXP], F32R)
            corr_w = sb("corr_w", [P, NEXP])
            tri8, tri4 = sb("tri8", [P, 8, 8]), sb("tri4", [P, 4, 4])
            mhalf2, eps2 = sb("mhalf2", [P, T]), sb("eps2", [P, T])

            x2n = sb("x2n", [P, T, D])
            x2t = [sb(f"x2t{p}", [P, T, D]) for p in range(2)]
            st3, mv3, r3a, r3 = sb("st3", [P, T, 6]), sb("mv3", [P, T, 2]), sb("r3a", [P, T]), sb("r3", [P, T])
            h3 = sb("h3", [P, T, D])
            h3_hi = [sb(f"h3_hi{p}", [P, KB, FFN_TOKENS], F32R) for p in range(2)]
            h3_lo = [sb(f"h3_lo{p}", [P, KB, FFN_TOKENS], F32R) for p in range(2)]
            lgt = sb("lgt", [2 * NEXP, FFN_TOKENS])
            lg2 = sb("lg2", [P, T, 2 * NEXP])
            lg, den, score, scorec, choice, wsel, cw = (sb(n, [P, T, NEXP]) for n in ("lg", "den", "score", "scorec", "choice", "wsel", "cw"))
            gsum, grank, gmask = (sb(n, [P, T, 4]) for n in ("gsum", "grank", "gmask"))
            g_gt, g_eq = sb("g_gt", [P, T, 4, 4]), sb("g_eq", [P, T, 4, 4])
            e_gt, e_eq = sb("e_gt", [P, T, 8, 8]), sb("e_eq", [P, T, 8, 8])
            erank, wsum, winv = sb("erank", [P, T, NEXP]), sb("wsum", [P, T]), sb("winv", [P, T])
            cwt = sb("cwt", [NEXP, FFN_TOKENS])
            cw_wide = [sb(f"cw_wide{p}", [P, NEXP, FFN_TOKENS]) for p in range(2)]
            sg = [sb(f"sg{b}", [P, FFN_TOKENS]) for b in range(2)]
            af = [sb(f"af{b}", [P, FFN_TOKENS]) for b in range(2)]
            a_hi = [sb(f"a_hi{b}", [P, FFN_TOKENS], F32R) for b in range(AHEAD + 1)]
            a_lo = [sb(f"a_lo{b}", [P, FFN_TOKENS], F32R) for b in range(AHEAD + 1)]

            wk_in = sem("routing_constants_in")
            wx_in = [sem(f"expert{e}_in") for e in range(NE)]
            x2n_in, x2_in = sem("norm_x2_in"), [sem(f"x2_{p}_in") for p in range(2)]
            out_st = sem("out_stored")
            w_hi_ok, w_lo_ok, gate_hi_ok, gate_ok, half_ok = sem("expert_hi"), sem("expert_lo"), sem("gate_hi"), sem("gate_ready"), sem("mhalf_set")
            st3_ok, mv3_ok, r3a_ok, r3_ok, h3_ok = sem("ln3_stats"), sem("ln3_moments"), sem("ln3_var_eps"), sem("ln3_rstd"), sem("h3_ready")
            t_h3, h3_hi_ok, h3_lo_ok = sem("h3_transposed"), sem("h3_hi_ready"), sem("h3_lo_ready")
            lg_mm, lgt_ok, t_lg, lg2_ok, lg_ok, eneg_ok = sem("logits_product"), sem("logits_copied"), sem("logits_transposed"), sem("logits_halves"), sem("logits_ready"), sem("logits_exp")
            route = sem("routing_step")
            t_cw, cwt_ok, cw_st, cw_in = sem("cw_transposed"), sem("cw_copied"), sem("cw_stored"), sem("cw_in")
            gu_mm, sg_ok, sgw_ok, af_ok, a_hi_ok, a_lo_ok = sem("gate_up_product"), sem("silu_ready"), sem("silu_weighted"), sem("act_ready"), sem("act_hi"), sem("act_lo")
            y_mm, out_ok = sem("down_product"), sem("out_ready")

            x2_g = x2_dram.rearrange("(t p) d -> p t d", p=P)
            out_g = out.rearrange("b l d -> (b l) d").rearrange("(t p) d -> p t d", p=P)
            ROUTE_STEPS = 23

            block = c2.enter_context(nc.Block())

            @block.sync
            def _(sp):
                def load_norm(g):
                    sp.dma_start(x2n[:, :, :], x2_g[:, bass.ds(T * g, T), :]).then_inc(x2n_in, 16)

                def load_x2(g, p):
                    sp.dma_start(x2t[p][:, :, :], x2_g[:, bass.ds(T * g, T), :]).then_inc(x2_in[p], 16)

                def spread_cw(g, p):
                    sp.wait_ge(cwt_ok, g + 1)
                    sp.dma_start(cw_dram[p], cwt[:, :]).then_inc(cw_st, 16)
                    sp.wait_ge(cw_st, 16 * (g + 1))
                    sp.dma_start(cw_wide[p][:, :, :], cw_dram[p].partition_broadcast(P)).then_inc(cw_in, 16)

                def store(g, p):
                    sp.wait_ge(out_ok, 2 * (g + 1))
                    sp.wait_ge(wk_in, 64)
                    sp.dma_start(out_g[:, bass.ds(T * g, T), :], x2t[p][:, :, :]).then_inc(out_st, 16)

                load_norm(0)
                sp.dma_start(corr_w[:, :], corr.partition_broadcast(P)).then_inc(wk_in, 16)
                sp.dma_start(tri8[:, :, :], tri8_in.partition_broadcast(P)).then_inc(wk_in, 16)
                sp.dma_start(tri4[:, :, :], tri4_in.partition_broadcast(P)).then_inc(wk_in, 16)
                sp.dma_start(gate_f[:, :, :], gate_t.rearrange("(k p) n -> p k n", p=P)).then_inc(wk_in, 16)
                for e in ORDER:
                    for half, (w, ws) in enumerate(((wg, wg_s), (wu, wu_s))):
                        src = ws if e == NEXP else w[e]
                        sp.dma_start(wgu_f[:, e, half, :, :], src.rearrange("(k p) n -> p k n", p=P)).then_inc(wx_in[e], 16)
                    sp.dma_start(wd_f[:, e, :], wd_s if e == NEXP else wd[e]).then_inc(wx_in[e], 16)
                load_x2(0, 0)
                sp.wait_ge(h3_ok, T)
                load_norm(1)
                spread_cw(0, 0)

                def group(g, p, more):
                    if not is_first(g):
                        store(g - 1, 1 - p)
                        sp.wait_ge(out_st, 16 * g)
                        sp.wait_ge(wk_in, 64)
                    load_x2(g + 1, 1 - p)
                    if more:
                        sp.wait_ge(h3_ok, T * (g + 2))
                        sp.wait_ge(wk_in, 64)
                        load_norm(g + 2)
                    spread_cw(g + 1, 1 - p)

                group(0, 0, True)
                with sp.Fori(0, NG2 // 2 - 1) as it:
                    group(2 * it + 1, 1, True)
                    group(2 * it + 2, 0, True)
                group(NG2 - 2, 1, False)
                store(NG2 - 2, 1)
                store(NG2 - 1, 0)
                sp.wait_ge(out_st, 16 * NG2)

            @block.tensor
            def _(pe):
                def turn_h3(g):
                    pe.wait_ge(h3_ok, T * (g + 1))
                    for k in range(KB):
                        for t in range(T):
                            last = pe.transpose(h_bank[k][:, t * P:(t + 1) * P], h3[:, t, k * P:(k + 1) * P], ident[:, :])
                        last.then_inc(t_h3, 1)

                def logits(g, p):
                    pe.wait_ge(h3_lo_ok, KB * (g + 1))
                    for k in range(KB):
                        pe.matmul(h_bank[0][0:2 * NEXP, :], gate[:, k, :], h3_lo[p][:, k, :], start=(k == 0), stop=False)
                        last = pe.matmul(h_bank[0][0:2 * NEXP, :], gate[:, k, :], h3_hi[p][:, k, :], start=False, stop=(k == KB - 1))
                    last.then_inc(lg_mm, 1)

                def turn_logits(g):
                    for t in range(T):
                        last = pe.transpose(h_bank[1][:, t * 2 * NEXP:(t + 1) * 2 * NEXP], lgt[:, t * P:(t + 1) * P],
                                            ident[0:2 * NEXP, 0:2 * NEXP])
                    last.then_inc(t_lg, 1)

                def turn_cw(g):
                    pe.wait_ge(route, ROUTE_STEPS * (g + 1))
                    for t in range(T):
                        last = pe.transpose(h_bank[0][0:NEXP, t * P:(t + 1) * P], cw[:, t, :], ident[:, :])
                    last.then_inc(t_cw, 1)

                def gate_up(g, p, n):
                    e, b = ORDER[n], (p + n) % 2
                    if n >= 2 or not is_first(g):
                        pe.wait_ge(af_ok, NE * g + n - 1)
                    if is_first(g):
                        pe.wait_ge(w_lo_ok, n + 1)
                    for half, dst in enumerate((g_bank[b], u_bank[b])):
                        for k in range(KB):
                            last = mm3(pe, dst[:, :], wgu_hi[:, e, half, k, :], wgu_lo[:, e, half, k, :], h3_hi[p][:, k, :],
                                       h3_lo[p][:, k, :], k == 0, k == KB - 1)
                        last.then_inc(gu_mm, 1)

                def down(g, n):
                    e, b = ORDER[n], n % (AHEAD + 1)
                    pe.wait_ge(a_lo_ok, NE * g + n + 1)
                    if n == 0 and not is_first(g):
                        pe.wait_ge(out_ok, 2 * g)
                    for t in range(T):
                        s = slice(t * P, (t + 1) * P)
                        last = mm3(pe, y_bank[t // 2][:, (t % 2) * D:(t % 2 + 1) * D], a_hi[b][:, s], a_lo[b][:, s], wd_hi[:, e, :],
                                   wd_lo[:, e, :], n == 0 and t % 2 == 0, n == NE - 1, skip_group_check=True)
                    if n == NE - 1:
                        last.then_inc(y_mm, 1)

                def group(g, p, last):
                    for n in range(NE):
                        gate_up(g, p, n)
                        if n == 0 and is_first(g):
                            turn_cw(0)
                        if not last:
                            if n == 1:
                                turn_h3(g + 1)
                            if n == 3:
                                pe.wait_ge(lgt_ok, g + 2)
                            if n == 7:
                                turn_cw(g + 1)
                        if n >= AHEAD:
                            down(g, n - AHEAD)
                        elif not is_first(g):
                            down(g - 1, NE + n - AHEAD)
                        if n == 2 and not last:
                            logits(g + 1, 1 - p)
                        if n == 3 and not last:
                            turn_logits(g + 1)

                turn_h3(0)
                pe.wait_ge(gate_ok, 1)
                logits(0, 0)
                pe.wait_ge(lgt_ok, 1)
                turn_logits(0)
                group(0, 0, False)
                with pe.Fori(0, NG2 // 2 - 1) as it:
                    group(2 * it + 1, 1, False)
                    group(2 * it + 2, 0, False)
                group(NG2 - 2, 1, False)
                group(NG2 - 1, 0, True)
                for n in range(NE - AHEAD, NE):
                    down(NG2 - 1, n)

            @block.scalar
            def _(act):
                def h3_high(g, p):
                    for k in range(KB):
                        act.wait_ge(t_h3, KB * g + k + 1)
                        act.activation(h3_hi[p][:, k, :], h_bank[k][:, :], ACT.Copy).then_inc(h3_hi_ok, 1)

                def copy_logits(g):
                    act.wait_ge(lg_mm, g + 1)
                    act.activation(lgt[:, :], h_bank[0][0:2 * NEXP, :], ACT.Copy).then_inc(lgt_ok, 1)

                def exp_logits(g):
                    act.wait_ge(lg_ok, g + 1)
                    act.activation(den[:, :, :], lg[:, :, :], ACT.Exp, scale=-1.0).then_inc(eneg_ok, 1)

                def copy_cw(g):
                    act.wait_ge(t_cw, g + 1)
                    if not is_first(g):
                        act.wait_ge(cw_st, 16 * g)
                    act.activation(cwt[:, :], h_bank[0][0:NEXP, :], ACT.Copy).then_inc(cwt_ok, 1)

                def split_high(n):
                    e = ORDER[n]
                    act.wait_ge(wx_in[e], 48)
                    act.activation(wgu_hi[:, e, :, :, :], wgu_f[:, e, :, :, :], ACT.Copy)
                    act.activation(wd_hi[:, e, :], wd_f[:, e, :], ACT.Copy).then_inc(w_hi_ok, 1)

                def expert(g, p, n):
                    b = (p + n) % 2
                    act.wait_ge(gu_mm, 2 * (NE * g + n) + 1)
                    act.activation(sg[b][:, :], g_bank[b][:, :], ACT.Silu).then_inc(sg_ok, 1)

                def act_high(g, p, n):
                    act.wait_ge(af_ok, NE * g + n + 1)
                    act.activation(a_hi[n % (AHEAD + 1)][:, :], af[(p + n) % 2][:, :], ACT.Copy).then_inc(a_hi_ok, 1)

                def group(g, p, last):
                    for n in range(NE):
                        expert(g, p, n)
                        if is_first(g):
                            if n == 0:
                                copy_cw(0)
                            if n + 3 < NE:
                                split_high(n + 3)
                        if not last:
                            if n == 1:
                                h3_high(g + 1, 1 - p)
                            if n == 7:
                                copy_cw(g + 1)
                        act_high(g, p, n)
                        if not last:
                            if n == 2:
                                copy_logits(g + 1)
                            if n == 3:
                                exp_logits(g + 1)

                split_high(0)
                h3_high(0, 0)
                split_high(1)
                copy_logits(0)
                exp_logits(0)
                split_high(2)
                group(0, 0, False)
                with act.Fori(0, NG2 // 2 - 1) as it:
                    group(2 * it + 1, 1, False)
                    group(2 * it + 2, 0, False)
                group(NG2 - 2, 1, False)
                group(NG2 - 1, 0, True)

            @block.gpsimd
            def _(pool):
                def rstd(g):
                    pool.wait_ge(mv3_ok, T * (g + 1))
                    if not is_first(g):
                        pool.wait_ge(h3_ok, T * g)
                    pool.tensor_tensor(r3a[:, :], mv3[:, :, 1], eps2[:, :], ALU.add).then_inc(r3a_ok, 1)
                    pool.wait_ge(r3a_ok, g + 1)
                    pool.tensor_tensor(r3[:, :], r3a[:, :], mhalf2[:, :], ALU.pow).then_inc(r3_ok, 1)

                def expert(g, p, n):
                    b = (p + n) % 2
                    pool.wait_ge(sg_ok, NE * g + n + 1)
                    if n == 1:
                        pool.wait_ge(cw_in, 16 * (g + 1))
                    pool.tensor_tensor(sg[b][:, :], sg[b][:, :], cw_wide[p][:, ORDER[n], :], ALU.mult).then_inc(sgw_ok, 1)

                def group(g, p, last):
                    if not last:
                        rstd(g + 1)
                    for n in range(1, NE):
                        expert(g, p, n)

                pool.wait_ge(half_ok, 2)
                rstd(0)
                with pool.Fori(0, NG2 // 2) as it:
                    group(2 * it, 0, False)
                    group(2 * it + 1, 1, False)
                group(NG2 - 1, 0, True)

            @block.vector
            def _(dve):
                def moments(g):
                    dve.wait_ge(x2n_in, 16 * (g + 1))
                    if not is_first(g):
                        dve.wait_ge(r3_ok, g)
                    for t in range(T):
                        dve.bn_stats(st3[:, t, :], x2n[:, t, :]).then_inc(st3_ok, 1)
                    dve.wait_ge(st3_ok, T * (g + 1))
                    dve.tensor_copy(held[:, 0:1], mhalf2[:, 0:1])
                    for t in range(T):
                        dve.bn_aggr(mv3[:, t, :], st3[:, t, :]).then_inc(mv3_ok, 1)

                def normalise(g):
                    dve.wait_ge(r3_ok, g + 1)
                    dve.wait_ge(mv3_ok, T * (g + 1))
                    if not is_first(g):
                        dve.wait_ge(t_h3, KB * g)
                    for t in range(T):
                        dve.tensor_scalar(h3[:, t, :], x2n[:, t, :], mv3[:, t, 0:1], r3[:, t:t + 1], ALU.subtract,
                                          ALU.mult).then_inc(h3_ok, 1)

                def h3_low(g, p):
                    for k in range(KB):
                        dve.wait_ge(h3_hi_ok, KB * g + k + 1)
                        dve.tensor_tensor(h3_lo[p][:, k, :], h_bank[k][:, :], f32(h3_hi[p][:, k, :]), ALU.subtract).then_inc(h3_lo_ok, 1)

                def sum_logits(g):
                    dve.wait_ge(t_lg, g + 1)
                    dve.tensor_copy(lg2[:, :, :], h_bank[1][:, 0:T * 2 * NEXP].rearrange("p (t n) -> p t n", t=T)).then_inc(lg2_ok, 1)
                    dve.wait_ge(lg2_ok, g + 1)
                    dve.tensor_tensor(lg[:, :, :], lg2[:, :, 0:NEXP], lg2[:, :, NEXP:2 * NEXP], ALU.add).then_inc(lg_ok, 1)

                halves = scorec[:, :, :].rearrange("p t (a b) -> p t a b", b=2)

                def stepper(g, done):
                    def step(ins):
                        nonlocal done
                        done += 1
                        ins.then_inc(route, 1)
                        dve.wait_ge(route, ROUTE_STEPS * g + done)
                    return step

                def pairs(a, n, axis):
                    return a.unsqueeze(axis).to_broadcast([P, T, n, n])

                def route_groups(g):
                    step = stepper(g, 0)
                    dve.wait_ge(eneg_ok, g + 1)
                    if not is_first(g):
                        dve.wait_ge(t_cw, g)
                    step(dve.tensor_scalar(den[:, :, :], den[:, :, :], 1.0, None, ALU.add))
                    step(dve.reciprocal(score[:, :, :], den[:, :, :]))
                    step(dve.tensor_tensor(scorec[:, :, :], score[:, :, :], corr_w[:, :].unsqueeze(1).to_broadcast([P, T, NEXP]), ALU.add))
                    step(dve.tensor_tensor(gsum[:, :, :], halves[:, :, :, 0], halves[:, :, :, 1], ALU.add))
                    mine, other = pairs(gsum[:, :, :], 4, 3), pairs(gsum[:, :, :], 4, 2)
                    step(dve.tensor_tensor(g_gt[:, :, :, :], other, mine, ALU.is_gt))
                    step(dve.tensor_tensor(g_eq[:, :, :, :], other, mine, ALU.is_equal))
                    step(dve.tensor_tensor(g_eq[:, :, :, :], g_eq[:, :, :, :], tri4[:, :, :].unsqueeze(1).to_broadcast([P, T, 4, 4]), ALU.mult))
                    step(dve.tensor_tensor(g_gt[:, :, :, :], g_gt[:, :, :, :], g_eq[:, :, :, :], ALU.add))
                    step(dve.reduce_sum(grank[:, :, :], g_gt[:, :, :, :], AX))
                    step(dve.tensor_scalar(gmask[:, :, :], grank[:, :, :], 2.0, None, ALU.is_lt))
                    step(dve.tensor_tensor(choice[:, :, :].rearrange("p t (a b) -> p t a b", b=2), halves,
                                           gmask[:, :, :].unsqueeze(3).to_broadcast([P, T, 4, 2]), ALU.mult))

                def route_experts(g):
                    step = stepper(g, 11)
                    mine, other = pairs(choice[:, :, :], 8, 3), pairs(choice[:, :, :], 8, 2)
                    step(dve.tensor_tensor(e_gt[:, :, :, :], other, mine, ALU.is_gt))
                    step(dve.tensor_tensor(e_eq[:, :, :, :], other, mine, ALU.is_equal))
                    step(dve.tensor_tensor(e_eq[:, :, :, :], e_eq[:, :, :, :], tri8[:, :, :].unsqueeze(1).to_broadcast([P, T, 8, 8]), ALU.mult))
                    step(dve.tensor_tensor(e_gt[:, :, :, :], e_gt[:, :, :, :], e_eq[:, :, :, :], ALU.add))
                    step(dve.reduce_sum(erank[:, :, :], e_gt[:, :, :, :], AX))
                    step(dve.tensor_scalar(erank[:, :, :], erank[:, :, :], 4.0, None, ALU.is_lt))
                    step(dve.tensor_tensor(wsel[:, :, :], score[:, :, :], erank[:, :, :], ALU.mult))
                    step(dve.reduce_sum(wsum[:, :], wsel[:, :, :], AX))
                    step(dve.tensor_scalar(wsum[:, :], wsum[:, :], ROUTE_TINY, None, ALU.add))
                    step(dve.reciprocal(winv[:, :], wsum[:, :]))
                    step(dve.tensor_tensor(wsel[:, :, :], wsel[:, :, :], winv[:, :].unsqueeze(2).to_broadcast([P, T, NEXP]), ALU.mult))
                    step(dve.tensor_scalar(cw[:, :, :], wsel[:, :, :], EXPERT_SCALE, None, ALU.mult))

                def product(g, p, n):
                    b = (p + n) % 2
                    dve.wait_ge(gu_mm, 2 * (NE * g + n) + 2)
                    if n == 0:
                        dve.wait_ge(sg_ok, NE * g + 1)
                    else:
                        dve.wait_ge(sgw_ok, NEXP * g + n)
                    dve.tensor_tensor(af[b][:, :], u_bank[b][:, :], sg[b][:, :], ALU.mult).then_inc(af_ok, 1)

                def act_low(g, p, n):
                    b = n % (AHEAD + 1)
                    dve.wait_ge(a_hi_ok, NE * g + n + 1)
                    dve.tensor_tensor(a_lo[b][:, :], af[(p + n) % 2][:, :], f32(a_hi[b][:, :]), ALU.subtract).then_inc(a_lo_ok, 1)

                def finish(g, p, nth):
                    dve.wait_ge(y_mm, g + 1)
                    dve.wait_ge(x2_in[p], 16 * nth)
                    for q in range(2):
                        x2q = x2t[p][:, 2 * q:2 * q + 2, :]
                        dve.tensor_tensor(x2q, y_bank[q][:, :].rearrange("p (t d) -> p t d", t=2), x2q, ALU.add).then_inc(out_ok, 1)

                def split_low(n):
                    e = ORDER[n]
                    dve.wait_ge(w_hi_ok, n + 1)
                    dve.tensor_tensor(wgu_lo[:, e, :, :, :], wgu_f[:, e, :, :, :], f32(wgu_hi[:, e, :, :, :]), ALU.subtract)
                    dve.tensor_tensor(wd_lo[:, e, :], wd_f[:, e, :], f32(wd_hi[:, e, :]), ALU.subtract).then_inc(w_lo_ok, 1)

                def group(g, p, nth, last):
                    if not last:
                        moments(g + 1)
                    for n in range(NE):
                        if is_first(g) and n + 2 < NE:
                            split_low(n + 2)
                        product(g, p, n)
                        if n == 1 and not is_first(g):
                            finish(g - 1, 1 - p, nth)
                        if not last:
                            if n == 1:
                                h3_low(g + 1, 1 - p)
                            if n == 4:
                                route_groups(g + 1)
                        act_low(g, p, n)
                        if n == 0 and not last:
                            normalise(g + 1)
                        if n == 3 and not last:
                            sum_logits(g + 1)
                        if n == 5 and not last:
                            route_experts(g + 1)

                dve.memset(mhalf2[:, :], -0.5).then_inc(half_ok, 1)
                dve.memset(eps2[:, :], LN_EPS).then_inc(half_ok, 1)
                dve.wait_ge(half_ok, 2)
                moments(0)
                dve.wait_ge(wk_in, 64)
                dve.tensor_copy(gate[:, :, 0:NEXP], gate_f[:, :, :]).then_inc(gate_hi_ok, 1)
                dve.wait_ge(gate_hi_ok, 1)
                dve.tensor_tensor(gate[:, :, NEXP:2 * NEXP], gate_f[:, :, :], f32(gate[:, :, 0:NEXP]), ALU.subtract).then_inc(gate_ok, 1)
                normalise(0)
                split_low(0)
                h3_low(0, 0)
                sum_logits(0)
                route_groups(0)
                route_experts(0)
                split_low(1)
                group(0, 0, None, False)
                with dve.Fori(0, NG2 // 2 - 1) as it:
                    group(2 * it + 1, 1, it + 1, False)
                    group(2 * it + 2, 0, it + 1, False)
                group(NG2 - 2, 1, NG2 // 2, False)
                group(NG2 - 1, 0, NG2 // 2, True)
                finish(NG2 - 1, 0, NG2 // 2 + 1)


def kernel(**inputs):
    import concourse.bacc as bacc
    from concourse.bass_utils import run_bass_kernel_spmd

    a = {k: np.asarray(v) for k, v in inputs.items()}
    D = a["x"].shape[2]
    att, xat, ffn = (lambda n, p=p: a[f"L0_{p}_{n}"] for p in ("attn", "xattn", "ffn"))

    def columns(v):
        return v.reshape(-1, P).T

    arrays = {
        "x": a["x"], "ctx": a["ctx_1024"], "ctx_t": a["ctx_1024"].transpose(0, 2, 1),
        "norm_w": columns(att("norm_w")), "norm_b": columns(att("norm_b")), "qkv_wt": att("qkv_w").T,
        "qk_b": att("qkv_b")[:2 * D], "v_b": columns(att("qkv_b")[2 * D:]),
        "proj_wt": att("proj_w").T, "proj_b": att("proj_b"),
        "w_cq": columns(xat("w_cq")), "b_cq": xat("b_cq").reshape(1), "w_c": xat("w_c"), "b_c": xat("b_c").reshape(1),
        "w_q": columns(xat("w_q")), "b_q": xat("b_q").reshape(1), "wl_t": xat("W_l").T, "b_l": xat("b_l"),
        "gate_t": ffn("gate_w").T, "corr": ffn("correction_bias"), "wg": ffn("Wg"), "wu": ffn("Wu"), "wd": ffn("Wd"),
        "wg_s": ffn("Wg_s"), "wu_s": ffn("Wu_s"), "wd_s": ffn("Wd_s"),
        "ident_in": np.eye(P, dtype=np.float32), "tri8_in": np.tri(8, 8, -1, dtype=np.float32),
        "tri4_in": np.tri(4, 4, -1, dtype=np.float32), "diag_in": np.eye(STREAMS, dtype=np.float32),
    }
    nc = bacc.Bacc("TRN2", target_bir_lowering=False, num_devices=1)
    arrays = {k: np.ascontiguousarray(v) for k, v in arrays.items()}
    aps = {k: nc.dram_tensor(f"in_{k}", v.shape, mybir.dt.from_np(v.dtype), kind="ExternalInput").ap() for k, v in arrays.items()}
    out = nc.dram_tensor("out_dram", a["x"].shape, F32, kind="ExternalOutput").ap()
    decoder_layer(nc, **aps, out=out)
    r = run_bass_kernel_spmd(nc, [{f"in_{k}": v for k, v in arrays.items()}], core_ids=[0])
    return r.results[0]["out_dram"]
```

```python
from contextlib import ExitStack

import numpy as np

import concourse.bass as bass
from concourse import mybir

F32 = mybir.dt.float32
F32R = mybir.dt.float32r
ALU = mybir.AluOpType
ACT = mybir.ActivationFunctionType
AX = mybir.AxisListType.X

P = 128
STREAMS = 4
LN_EPS = 1e-5
NEXP = 8
EXPERT_SCALE = 2.5
ROUTE_TINY = 1e-20
FFN_TOKENS = 512
FFN_TILES = FFN_TOKENS // P


def is_first(g):
    return isinstance(g, int) and g == 0


def f32(ap):
    return ap.bitcast(F32)


def decoder_layer(nc, x, ctx, ctx_t, norm_w, norm_b, qkv_wt, qk_b, v_b, proj_wt, proj_b, w_cq, b_cq, w_c, b_c,
                  w_q, b_q, wl_t, b_l, gate_t, corr, wg, wu, wd, wg_s, wu_s, wd_s, ident_in, tri8_in,
                  tri4_in, diag_in, out):
    B, L, D = x.shape
    S = ctx.shape[1]
    KB = D // P
    I = wg.shape[2]
    G = STREAMS
    NGRP = B // G
    SB = 125
    NSB = S // SB
    SP_ = S + S % 2
    TOK = G * L
    PAIRS = G // 2
    ATT_SCALE = float(1.0 / np.sqrt(L))
    NT = B * L
    NG2 = NT // FFN_TOKENS
    NE = NEXP + 1
    assert D == 256 and I == P and NSB * SB == S and NG2 * FFN_TOKENS == NT and NG2 % 2 == 1

    x2_dram = nc.dram_tensor("x2_scratch", (NT, D), F32, kind="Internal").ap()
    cw_dram = nc.dram_tensor("cw_scratch", (2, NEXP, FFN_TOKENS), F32, kind="Internal").ap()

    def mm3(pe, dst, a_hi, a_lo, b_hi, b_lo, first, last, **kw):
        pe.matmul(dst, a_lo, b_hi, start=first, stop=False, **kw)
        pe.matmul(dst, a_hi, b_lo, start=False, stop=False, **kw)
        return pe.matmul(dst, a_hi, b_hi, start=False, stop=last, **kw)

    outer = ExitStack()
    with outer:
        bank = [outer.enter_context(nc.psum_tensor(f"bank{n}", [P, 512], F32)) for n in range(8)]
        ident = outer.enter_context(nc.sbuf_tensor("ident", [P, P], F32))
        held = outer.enter_context(nc.sbuf_tensor("held", [P, 1 + STREAMS], F32))
        x2_st = outer.enter_context(nc.semaphore("x2_stored"))

        def osb(name, shape, dt=F32):
            return outer.enter_context(nc.sbuf_tensor(name, shape, dt))

        def osem(name):
            return outer.enter_context(nc.semaphore(name))

        T = FFN_TILES
        assert T == G and FFN_TOKENS >= TOK and KB * TOK >= 2 * KB * I + D
        h_bank = bank[6:8]
        x2b = osb("x2b", [L, G, D])
        h3 = osb("h3", [P, T, D])
        x2n = osb("x2n", [P, T, D])
        h3_hi0, h3_lo0 = osb("h3_hi0", [P, KB, FFN_TOKENS], F32R), osb("h3_lo0", [P, KB, FFN_TOKENS], F32R)
        shared_hi, shared_lo = osb("shared_hi", [P, KB * TOK], F32R), osb("shared_lo", [P, KB * TOK], F32R)
        mhalf2, eps2 = osb("mhalf2", [P, T]), osb("eps2", [P, T])
        gate_f = osb("gate_f", [P, KB, NEXP])
        gate = osb("gate", [P, KB, 2 * NEXP], F32R)
        corr_w = osb("corr_w", [P, NEXP])
        tri8, tri4 = osb("tri8", [P, 8, 8]), osb("tri4", [P, 4, 4])
        lgt = osb("lgt", [2 * NEXP, FFN_TOKENS])
        st3, mv3, r3a, r3 = osb("st3", [P, T, 6]), osb("mv3", [P, T, 2]), osb("r3a", [P, T]), osb("r3", [P, T])
        x2n_in, half_ok = osem("norm_x2_in"), osem("mhalf_set")
        st3_ok, mv3_ok, r3a_ok, r3_ok, h3_ok = osem("ln3_stats"), osem("ln3_moments"), osem("ln3_var_eps"), osem("ln3_rstd"), osem("h3_ready")
        t_h3, h3_hi_ok, h3_lo_ok = osem("h3_transposed"), osem("h3_hi_ready"), osem("h3_lo_ready")
        shared_in, shared_hi_ok, shared_lo_ok = osem("shared_expert_in"), osem("shared_expert_hi"), osem("shared_expert_lo")
        gate_in, gate_hi_ok, gate_ok = osem("gate_in"), osem("gate_hi"), osem("gate_ready")
        wk_in = osem("routing_constants_in")
        lg_mm, lgt_ok = osem("logits_product"), osem("logits_copied")
        x2_g = x2_dram.rearrange("(t p) d -> p t d", p=P)
        GU = 2 * KB * I

        def gate_up_weights(w):
            return w[:, 0:GU].rearrange("p (h k n) -> p h k n", h=2, k=KB)

        def load_norm(sp, g):
            sp.dma_start(x2n[:, :, :], x2_g[:, bass.ds(T * g, T), :]).then_inc(x2n_in, 16)


        def turn_h3(pe, g):
            pe.wait_ge(h3_ok, T * (g + 1))
            for k in range(KB):
                for t in range(T):
                    last = pe.transpose(h_bank[k][:, t * P:(t + 1) * P], h3[:, t, k * P:(k + 1) * P], ident[:, :])
                last.then_inc(t_h3, 1)

        def h3_high(act, g, h3_hi):
            for k in range(KB):
                act.wait_ge(t_h3, KB * g + k + 1)
                act.activation(h3_hi[:, k, :], h_bank[k][:, :], ACT.Copy).then_inc(h3_hi_ok, 1)

        def rstd3(pool, g):
            pool.wait_ge(mv3_ok, T * (g + 1))
            if not is_first(g):
                pool.wait_ge(h3_ok, T * g)
            pool.tensor_tensor(r3a[:, :], mv3[:, :, 1], eps2[:, :], ALU.add).then_inc(r3a_ok, 1)
            pool.wait_ge(r3a_ok, g + 1)
            pool.tensor_tensor(r3[:, :], r3a[:, :], mhalf2[:, :], ALU.pow).then_inc(r3_ok, 1)

        def moments3(dve, g):
            dve.wait_ge(x2n_in, 16 * (g + 1))
            if not is_first(g):
                dve.wait_ge(r3_ok, g)
            for t in range(T):
                dve.bn_stats(st3[:, t, :], x2n[:, t, :]).then_inc(st3_ok, 1)
            dve.wait_ge(st3_ok, T * (g + 1))
            dve.tensor_copy(held[:, 0:1], mhalf2[:, 0:1])
            for t in range(T):
                dve.bn_aggr(mv3[:, t, :], st3[:, t, :]).then_inc(mv3_ok, 1)

        def normalise3(dve, g):
            dve.wait_ge(r3_ok, g + 1)
            dve.wait_ge(mv3_ok, T * (g + 1))
            if not is_first(g):
                dve.wait_ge(t_h3, KB * g)
            for t in range(T):
                dve.tensor_scalar(h3[:, t, :], x2n[:, t, :], mv3[:, t, 0:1], r3[:, t:t + 1], ALU.subtract,
                                  ALU.mult).then_inc(h3_ok, 1)

        def h3_low(dve, g, h3_hi, h3_lo):
            for k in range(KB):
                dve.wait_ge(h3_hi_ok, KB * g + k + 1)
                dve.tensor_tensor(h3_lo[:, k, :], h_bank[k][:, :], f32(h3_hi[:, k, :]), ALU.subtract).then_inc(h3_lo_ok, 1)

        def logits(pe, g, h3_hi, h3_lo):
            pe.wait_ge(h3_lo_ok, KB * (g + 1))
            for k in range(KB):
                pe.matmul(h_bank[0][0:2 * NEXP, :], gate[:, k, :], h3_lo[:, k, :], start=(k == 0), stop=False)
                last = pe.matmul(h_bank[0][0:2 * NEXP, :], gate[:, k, :], h3_hi[:, k, :], start=False, stop=(k == KB - 1))
            last.then_inc(lg_mm, 1)

        def copy_logits(act, g):
            act.wait_ge(lg_mm, g + 1)
            act.activation(lgt[:, :], h_bank[0][0:2 * NEXP, :], ACT.Copy).then_inc(lgt_ok, 1)

        with ExitStack() as c1:
            def sb(name, shape, dt=F32):
                return c1.enter_context(nc.sbuf_tensor(name, shape, dt))

            def sem(name):
                return c1.enter_context(nc.semaphore(name))

            v_bank = bank[6:8]
            z_bank = bank[4:6]
            m_bank = bank[6]

            ctxf = sb("ctxf", [P, G, NSB, D])
            tmp_all = sb("tmp", [P, G, 512])
            assert 2 * NSB == 3 * KB
            wqkv_f = ctxf[:, 2:4, :, :].rearrange("p g b d -> p (g b d)").rearrange("p (k n) -> p k n", k=KB)
            wl_f = tmp_all[:, :, :].rearrange("p g (k n) -> p (g k) n", n=D)
            wqkv_hi, wqkv_lo = sb("wqkv_hi", [P, KB, 3 * D], F32R), sb("wqkv_lo", [P, KB, 3 * D], F32R)
            wp_hi, wp_lo = sb("wp_hi", [P, KB, D], F32R), sb("wp_lo", [P, KB, D], F32R)
            wl_hi, wl_lo = sb("wl_hi", [P, 4 * KB, D], F32R), sb("wl_lo", [P, 4 * KB, D], F32R)
            nw, nb, nwq = sb("nw", [P, KB]), sb("nb", [P, KB]), sb("nwq", [P, KB])
            nb_wide = sb("nb_wide", [P, KB, L])
            qk_bias, qk_bias0 = sb("qk_bias", [L, 2 * D]), sb("qk_bias0", [L, 2 * D])
            v_bias, v_bias0 = sb("v_bias", [P, KB]), sb("v_bias0", [P, KB])
            pb_wide, bl_wide, wc_wide = sb("pb_wide", [L, D]), sb("bl_wide", [L, D]), sb("wc_wide", [L, D])
            wcq, wq = sb("wcq", [P, KB]), sb("wq", [P, KB])
            b3, b_sum = sb("b3", [L, 3]), sb("b_sum", [L, 1])
            diag = sb("diag", [L, G, G])
            mhalf, eps, one, mone, pheld = (sb(n, [L, G]) for n in ("mhalf", "eps", "one", "mone", "pheld"))

            xt = sb("xt", [L, G, D])
            st1, mv1 = sb("st1", [L, G, 6]), sb("mv1", [L, G, 2])
            ln1 = sb("ln1", [L, 10, G])
            hh, res = h3[0:L, :, :], x2n[0:L, :, :]
            h_hi, h_lo = h3_hi0[:, :, 0:TOK], h3_lo0[:, :, 0:TOK]
            v_hi, v_lo = (v[:, :].rearrange("p (k t) -> p k t", k=KB) for v in (shared_hi, shared_lo))
            op_hi = [sb(f"op_hi{j}", [P, 512], F32R) for j in range(G)]
            op_lo = [sb(f"op_lo{j}", [P, 512], F32R) for j in range(G)]
            tmp = [tmp_all[:, j, :] for j in range(G)]
            smx, ssum, sinv = sb("smx", [P, G, 2]), sb("ssum", [P, G, 2]), sb("sinv", [P, G, 2])
            st2, mv2, r2a, r2 = sb("st2", [L, G, 6]), sb("mv2", [L, G, 2]), sb("r2a", [L, G]), sb("r2", [L, G])
            x1 = sb("x1", [L, G, D])
            c = sb("c", [L, G, D])
            cwc, rdot = sb("cwc", [L, D]), sb("rdot", [L, G])
            ct = sb("ct", [P, G, KB, L])
            wp_f = ct[:, :, :, :].rearrange("p g k t -> p (g k t)")[:, 0:KB * D].rearrange("p (k n) -> p k n", k=KB)
            c_hi, c_lo = sb("c_hi", [P, G, KB, L], F32R), sb("c_lo", [P, G, KB, L], F32R)
            ctw = sb("ctw", [P, G, KB, L])
            cw_hi, cw_lo = sb("cw_hi", [P, G, KB, L], F32R), sb("cw_lo", [P, G, KB, L], F32R)
            ctxtf = sb("ctxtf", [P, G, KB, S])
            ctx_hi, ctx_lo = sb("ctx_hi", [SB, G, NSB, D], F32R), sb("ctx_lo", [SB, G, NSB, D], F32R)
            ctxt_hi, ctxt_lo = sb("ctxt_hi", [P, G, KB, SP_], F32R), sb("ctxt_lo", [P, G, KB, SP_], F32R)
            smx2, ssum2, sinv2 = sb("smx2", [L, G]), sb("ssum2", [L, G]), sb("sinv2", [L, G])
            m4 = sb("m4", [L, G])
            mneg, msum, minv = sb("mneg", [G, 1]), sb("msum", [G, 1]), sb("minv", [G, 1])
            mexp, mrow = sb("mexp", [G, L]), sb("mrow", [G, L])
            b4 = sb("b4", [L, G])
            shared_f = ctxf[:, 0, :, :].rearrange("p b d -> p (b d)")
            assert GU + D == NSB * D
            bm = sb("bm", [L, G, G])
            q2c_row, q2c = sb("q2c_row", [G, D]), sb("q2c", [P, KB, G])
            x4 = ctw
            x4_hi, x4_lo = cw_hi, cw_lo

            w_in, wpl_in, late_in, x_in = sem("qkv_weights_in"), sem("proj_and_l_weights_in"), sem("constants_in"), sem("x_in")
            cx_in = [sem(f"context{j}_in") for j in range(G)]
            wide = sem("nb_widened")
            nwq_ok, qk_bias_ok = sem("q_norm_scale"), sem("qk_bias_sum")
            w_split, w2_hi_ok, w2_split = sem("qkv_weights_split"), sem("other_weights_hi"), sem("other_weights_split")
            bias_mm, bias_ok = sem("bias_product"), sem("bias_ready")
            consts = sem("constants_set")
            st1_ok, mv1_ok, ln1_step = sem("ln1_stats"), sem("ln1_moments"), sem("ln1_scalars")
            hh_ok, res0_ok, res_ok = sem("hh_ready"), sem("residual_scaled"), sem("residual_ready")
            t_h, h_hi_ok, h_lo_ok = sem("h_transposed"), sem("h_hi_ready"), sem("h_lo_ready")
            qk_mm, qk_f_ok, qk_hi_ok, qk_lo_ok = sem("qk_product"), sem("qk_biased"), sem("qk_hi_ready"), sem("qk_lo_ready")
            v_mm, v_hi_ok, v_lo_ok = sem("v_product"), sem("v_hi_ready"), sem("v_lo_ready")
            sc_mm, smx_ok, exp_ok, sinv_ok = sem("scores_product"), sem("scores_max"), sem("scores_exp"), sem("scores_inv_sum")
            w_hi_ok, w_lo_ok = sem("probs_hi_ready"), sem("probs_lo_ready")
            g_mm, g_hi_ok, g_lo_ok = sem("probs_proj_product"), sem("probs_proj_hi"), sem("probs_proj_lo")
            ao_mm, x1_ok, st2_ok, mv2_ok = sem("attention_out"), sem("x1_ready"), sem("ln2_stats"), sem("ln2_moments")
            r2a_ok, r2_ok, c_ok, x1b_ok = sem("ln2_var_eps"), sem("ln2_rstd"), sem("c_ready"), sem("x1_biased")
            rdot_ok = sem("row_term_ready")
            t_c, ct_ok, c_hi_ok, c_lo_ok = sem("c_transposed"), sem("ct_ready"), sem("c_hi_ready"), sem("c_lo_ready")
            ctw_ok, cw_hi_ok, cw_lo_ok = sem("c_weighted"), sem("cw_hi_ready"), sem("cw_lo_ready")
            cx_hi_ok, cx_lo_ok = sem("context_hi_ready"), sem("context_lo_ready")
            s_mm, smx2_ok, exp2_ok, sinv2_ok = sem("similarity"), sem("sim_max"), sem("sim_exp"), sem("sim_inv_sum")
            m4_ok = sem("row_max_ready")
            t_a, a_hi_ok, a_lo_ok = sem("a_transposed"), sem("a_hi_ready"), sem("a_lo_ready")
            c2q_mm, c2q_ok, x3_ok = sem("c2q_product"), sem("c2q_copied"), sem("c_c2q_ready")
            t_x, x_hi_ok, x_lo_ok = sem("x23_transposed"), sem("x23_hi_ready"), sem("x23_lo_ready")
            t_m, mneg_ok, mexp_ok, minv_ok, mrow_ok = sem("m_transposed"), sem("m_max"), sem("m_exp"), sem("m_inv_sum"), sem("b_att_rows")
            t_b, b4_ok, bm_ok, q2c_mm, q2cr_ok = sem("b_att_transposed"), sem("b_att_columns"), sem("b_att_masked"), sem("q2c_product"), sem("q2c_rows")
            t_q, q2c_ok, x4_ok, x4_hi_ok, x4_lo_ok = sem("q2c_transposed"), sem("q2c_ready"), sem("x4_ready"), sem("x4_hi_ready"), sem("x4_lo_ready")
            z_mm, x2_ok = sem("z_product"), sem("x2_ready")
            b_sum_ok = sem("b_sum_ready")

            QKV_LOADS, LATE_LOADS = 6, 9
            QKV_SPLITS = 2 * 2 * KB
            qkv_parts = [(slice(0, D), nwq), (slice(D, 3 * D), nw)]
            x_tiles = x.rearrange("b t d -> t b d")
            x2_tiles = x2_dram.rearrange("(b t) d -> t b d", t=L)
            LN1_STEPS = 10

            block = c1.enter_context(nc.Block())

            @block.sync
            def _(sp):
                sp.dma_start(xt[:, :, :], x_tiles[:, 0:G, :]).then_inc(x_in, 16)
                sp.dma_start(ident[:, :], ident_in).then_inc(w_in, 16)
                sp.dma_start(nw[:, :], norm_w).then_inc(w_in, 16)
                sp.dma_start(nb[:, :], norm_b).then_inc(w_in, 16)
                sp.dma_start(wqkv_f[:, :, :], qkv_wt.rearrange("(k p) n -> p k n", p=P)).then_inc(w_in, 16)
                sp.dma_start(qk_bias0[:, :], qk_b.partition_broadcast(L)).then_inc(w_in, 16)
                sp.dma_start(v_bias0[:, :], v_b).then_inc(w_in, 16)
                def load_context(batch, j):
                    sp.dma_start(ctxtf[:, j, :, :], ctx_t[bass.ds(batch + j, 1)].rearrange("o (k p) s -> p (o k) s", p=P)).then_inc(cx_in[j], 16)
                    sp.dma_start(ctxf[0:SB, j, :, :], ctx[bass.ds(batch + j, 1)].rearrange("o (k p) d -> p (o k) d", p=SB)).then_inc(cx_in[j], 16)

                load_context(0, 0)
                load_context(0, 1)
                sp.dma_start(wp_f[:, :, :], proj_wt.rearrange("(k p) n -> p k n", p=P)).then_inc(wpl_in, 16)
                sp.dma_start(wl_f[:, :, :], wl_t.rearrange("(k p) n -> p k n", p=P)).then_inc(wpl_in, 16)
                sp.dma_start(pb_wide[:, :], proj_b.partition_broadcast(L)).then_inc(late_in, 16)
                sp.dma_start(bl_wide[:, :], b_l.partition_broadcast(L)).then_inc(late_in, 16)
                sp.dma_start(wc_wide[:, :], w_c.partition_broadcast(L)).then_inc(late_in, 16)
                sp.dma_start(wcq[:, :], w_cq).then_inc(late_in, 16)
                sp.dma_start(wq[:, :], w_q).then_inc(late_in, 16)
                sp.dma_start(diag[:, :, :], diag_in.partition_broadcast(L)).then_inc(late_in, 16)
                for n, b in enumerate((b_cq, b_c, b_q)):
                    sp.dma_start(b3[:, n:n + 1], b.partition_broadcast(L)).then_inc(late_in, 16)

                def group(i, last):
                    batch = sp.snap(G * i)
                    if not last:
                        sp.wait_ge(hh_ok, G * (i + 1))
                        sp.wait_ge(res0_ok, G * (i + 1))
                        sp.wait_ge(w_in, 16)
                        sp.dma_start(xt[:, :, :], x_tiles[:, bass.ds(batch + G, G), :]).then_inc(x_in, 16)
                        for j in range(G):
                            sp.wait_ge(cx_lo_ok, G * i + j + 1)
                            sp.wait_ge(w_in, 16)
                            load_context(batch + G, j)
                    if not is_first(i):
                        sp.wait_ge(x2_ok, PAIRS * (i + 1))
                        sp.wait_ge(w_in, 16)
                        sp.dma_start(x2_tiles[:, bass.ds(batch - G, G), :], x2b[:, :, :]).then_inc(x2_st, 16)
                    if last:
                        sp.wait_ge(x2_ok, PAIRS * (i + 2))
                        sp.wait_ge(w_in, 16)
                        sp.dma_start(x2_tiles[:, bass.ds(batch, G), :], x2b[:, :, :]).then_inc(x2_st, 16)

                sp.dma_start(gate_f[:, :, :], gate_t.rearrange("(k p) n -> p k n", p=P)).then_inc(gate_in, 16)
                sp.dma_start(corr_w[:, :], corr.partition_broadcast(P)).then_inc(wk_in, 16)
                sp.dma_start(tri8[:, :, :], tri8_in.partition_broadcast(P)).then_inc(wk_in, 16)
                sp.dma_start(tri4[:, :, :], tri4_in.partition_broadcast(P)).then_inc(wk_in, 16)
                sp.wait_ge(w_split, QKV_SPLITS)
                sp.wait_ge(bias_mm, 1)
                for j in range(2, G):
                    load_context(0, j)
                group(0, False)
                with sp.Fori(1, NGRP - 1) as i:
                    group(i, False)
                sp.wait_ge(cx_lo_ok, G * (NGRP - 1) + 1)
                for half, w in enumerate((wg_s, wu_s)):
                    sp.dma_start(gate_up_weights(shared_f)[:, half, :, :], w.rearrange("(k p) n -> p k n", p=P)).then_inc(shared_in, 16)
                sp.dma_start(shared_f[:, GU:GU + D], wd_s).then_inc(shared_in, 16)
                sp.wait_ge(x1_ok, G * NGRP)
                sp.wait_ge(x2_st, 16 * (NGRP - 1))
                load_norm(sp, 0)
                group(NGRP - 1, True)

            @block.tensor
            def _(pe):
                def turn_h(g):
                    for j in range(G):
                        pe.wait_ge(hh_ok, G * g + j + 1)
                        for k in range(KB):
                            t = pe.transpose(bank[j][:, k * L:(k + 1) * L], hh[:, j, k * P:(k + 1) * P], ident[0:L, 0:L])
                        t.then_inc(t_h, 1)

                turn_h(0)
                pe.wait_ge(wide, 1)
                for k in range(KB):
                    pe.matmul(m_bank[0:L, :], nb_wide[:, k, :], wqkv_f[:, k, 0:2 * D], start=(k == 0), stop=(k == KB - 1))
                for half in range(KB):
                    for k in range(KB):
                        last = pe.matmul(v_bank[1][:, half:half + 1], wqkv_f[:, k, 2 * D + half * P:2 * D + (half + 1) * P],
                                         nb[:, k:k + 1], start=(k == 0), stop=(k == KB - 1))
                last.then_inc(bias_mm, 1)

                def z_of(j):
                    return z_bank[j // 2][0:L, (j % 2) * D:(j % 2 + 1) * D]

                def z_q2c(g, q):
                    if q == 0:
                        pe.wait_ge(x4_lo_ok, g + 1)
                    for j in (2 * q, 2 * q + 1):
                        for k in range(KB):
                            last = mm3(pe, z_of(j), x4_hi[:, j, k, :], x4_lo[:, j, k, :], wl_hi[:, 3 * KB + k, :],
                                       wl_lo[:, 3 * KB + k, :], False, k == KB - 1, skip_group_check=True)
                    last.then_inc(z_mm, 1)

                def group(i, last_group):
                    ev = [G * i + j + 1 for j in range(G)]

                    def qk_product(j):
                        pe.wait_ge(h_lo_ok, ev[j])
                        for k in range(KB):
                            t = slice(j * L, (j + 1) * L)
                            last = mm3(pe, bank[j][0:L, :], h_hi[:, k, t], h_lo[:, k, t], wqkv_hi[:, k, 0:2 * D],
                                       wqkv_lo[:, k, 0:2 * D], k == 0, k == KB - 1)
                        last.then_inc(qk_mm, 1)

                    def scores(j):
                        pe.wait_ge(qk_lo_ok, ev[j])
                        for half in range(KB):
                            q = slice(half * P, (half + 1) * P)
                            last = mm3(pe, bank[j][:, half * D:(half + 1) * D], op_hi[j][0:L, q], op_lo[j][0:L, q],
                                       op_hi[j][0:L, D:2 * D], op_lo[j][0:L, D:2 * D], True, True)
                        last.then_inc(sc_mm, 1)

                    def v_product(half):
                        pe.wait_ge(h_lo_ok, ev[G - 1])
                        n = slice(2 * D + half * P, 2 * D + (half + 1) * P)
                        for k in range(KB):
                            last = mm3(pe, v_bank[half][:, 0:TOK], wqkv_hi[:, k, n], wqkv_lo[:, k, n], h_hi[:, k, :], h_lo[:, k, :],
                                       k == 0, k == KB - 1)
                        last.then_inc(v_mm, 1)

                    def probs_proj(j):
                        if j == 0:
                            pe.wait_ge(w2_split, 2)
                        pe.wait_ge(w_lo_ok, ev[j])
                        for half in range(KB):
                            for q in range(KB):
                                n = slice(q * D + half * P, q * D + (half + 1) * P)
                                last = mm3(pe, bank[j][:, half * D:(half + 1) * D], op_hi[j][:, n], op_lo[j][:, n],
                                           wp_hi[:, q, :], wp_lo[:, q, :], q == 0, q == KB - 1)
                        last.then_inc(g_mm, 1)

                    def attention_out(j):
                        if j == 0:
                            pe.wait_ge(v_lo_ok, KB * (i + 1))
                        pe.wait_ge(g_lo_ok, ev[j])
                        t = slice(j * L, (j + 1) * L)
                        for k in range(KB):
                            n = slice(k * D, (k + 1) * D)
                            last = mm3(pe, bank[j][0:L, 0:D], v_hi[:, k, t], v_lo[:, k, t], op_hi[j][:, n], op_lo[j][:, n],
                                       k == 0, k == KB - 1)
                        last.then_inc(ao_mm, 1)

                    def turn_c(j):
                        pe.wait_ge(c_ok, ev[j])
                        for k in range(KB):
                            last = pe.transpose(bank[j][:, k * L:(k + 1) * L], c[:, j, k * P:(k + 1) * P], ident[0:L, 0:L])
                        last.then_inc(t_c, 1)

                    def z_c(j):
                        pe.wait_ge(c_lo_ok, ev[j])
                        if j % 2 == 0:
                            pe.wait_ge(x2_ok, PAIRS * i + j // 2 + 1)
                        for k in range(KB):
                            mm3(pe, z_of(j), c_hi[:, j, k, :], c_lo[:, j, k, :], wl_hi[:, k, :], wl_lo[:, k, :],
                                k == 0 and j % 2 == 0, False, skip_group_check=True)

                    def similarity(j):
                        pe.wait_ge(cw_lo_ok, ev[j])
                        pe.wait_ge(c_lo_ok, ev[j])
                        pe.wait_ge(cx_lo_ok, ev[j])
                        for k in range(KB):
                            last = mm3(pe, bank[j][0:L, 0:SP_], cw_hi[:, j, k, :], cw_lo[:, j, k, :], ctxt_hi[:, j, k, :],
                                       ctxt_lo[:, j, k, :], k == 0, k == KB - 1)
                        last.then_inc(s_mm, 1)

                    qk_product(0)
                    qk_product(1)
                    qk_product(2)
                    qk_product(3)
                    scores(0)
                    scores(1)
                    scores(2)
                    scores(3)
                    v_product(0)
                    probs_proj(0)
                    v_product(1)
                    probs_proj(1)
                    probs_proj(2)
                    probs_proj(3)
                    attention_out(0)
                    attention_out(1)
                    attention_out(2)
                    attention_out(3)
                    if not is_first(i):
                        z_q2c(i - 1, 0)
                        z_q2c(i - 1, 1)
                    turn_c(0)
                    turn_c(1)
                    turn_c(2)
                    turn_c(3)
                    z_c(0)
                    z_c(1)
                    similarity(0)
                    similarity(1)
                    similarity(2)
                    similarity(3)
                    z_c(2)
                    z_c(3)
                    for j in range(G):
                        pe.wait_ge(exp2_ok, ev[j])
                        for b in range(NSB):
                            last = pe.transpose(bank[j][0:SB, b * L:(b + 1) * L], tmp[j][0:L, b * SB:(b + 1) * SB], ident[0:L, 0:L])
                        last.then_inc(t_a, 1)
                    pe.wait_ge(m4_ok, G * (i + 1))
                    pe.transpose(m_bank[0:G, 0:L], m4[:, :], ident[0:L, 0:L]).then_inc(t_m, 1)
                    for j in range(G):
                        pe.wait_ge(a_lo_ok, ev[j])
                        for b in range(NSB):
                            t = slice(b * L, (b + 1) * L)
                            last = mm3(pe, bank[j][0:L, 0:D], op_hi[j][0:SB, t], op_lo[j][0:SB, t], ctx_hi[:, j, b, :],
                                       ctx_lo[:, j, b, :], b == 0, b == NSB - 1)
                        last.then_inc(c2q_mm, 1)
                    for j in range(2):
                        if j == 0:
                            pe.wait_ge(mrow_ok, i + 1)
                        pe.wait_ge(x3_ok, ev[j])
                        for k in range(2 * KB):
                            last = pe.transpose(bank[j][:, k * L:(k + 1) * L], tmp[j][0:L, k * P:(k + 1) * P], ident[0:L, 0:L])
                        last.then_inc(t_x, 1)
                        if j == 0:
                            pe.transpose(m_bank[0:L, P:P + G], mrow[:, :], ident[0:G, 0:G]).then_inc(t_b, 1)
                    pe.wait_ge(bm_ok, i + 1)
                    for j in range(G):
                        last = pe.matmul(m_bank[0:G, D:2 * D], bm[:, j, :], c[:, j, :], start=(j == 0), stop=(j == G - 1))
                    last.then_inc(q2c_mm, 1)
                    for j in range(2, G):
                        pe.wait_ge(x3_ok, ev[j])
                        for k in range(2 * KB):
                            last = pe.transpose(bank[j][:, k * L:(k + 1) * L], tmp[j][0:L, k * P:(k + 1) * P], ident[0:L, 0:L])
                        last.then_inc(t_x, 1)
                    def z_c2q(j):
                        pe.wait_ge(x_lo_ok, ev[j])
                        if j == 0:
                            pe.wait_ge(q2cr_ok, i + 1)
                        for k in range(2 * KB):
                            t = slice(k * L, (k + 1) * L)
                            mm3(pe, z_of(j), op_hi[j][:, t], op_lo[j][:, t], wl_hi[:, KB + k, :], wl_lo[:, KB + k, :], False, False,
                                skip_group_check=True)
                            if j == 0 and k == 0:
                                for h in range(KB):
                                    last = pe.transpose(m_bank[:, h * G:(h + 1) * G], q2c_row[:, h * P:(h + 1) * P], ident[0:G, 0:G])
                                last.then_inc(t_q, 1)

                    z_c2q(0)
                    z_c2q(1)
                    z_c2q(2)
                    if not last_group:
                        pe.wait_ge(x_lo_ok, ev[G - 1])
                        turn_h(i + 1)
                    z_c2q(3)
                    if last_group:
                        turn_h3(pe, 0)
                        z_q2c(i, 0)
                        z_q2c(i, 1)
                    if last_group:
                        pe.wait_ge(gate_ok, 1)
                        logits(pe, 0, h3_hi0, h3_lo0)

                pe.wait_ge(bias_ok, 2)
                pe.wait_ge(w_split, QKV_SPLITS)
                group(0, False)
                with pe.Fori(1, NGRP - 1) as i:
                    group(i, False)
                group(NGRP - 1, True)

            @block.scalar
            def _(act):
                def residual(g):
                    act.wait_ge(x_in, 16 * (g + 1))
                    act.wait_ge(ln1_step, LN1_STEPS * (g + 1))
                    if not is_first(g):
                        act.wait_ge(x1_ok, G * g)
                    for j in range(G):
                        act.activation(res[:, j, :], xt[:, j, :], ACT.Identity, bias=ln1[:, 9, j:j + 1],
                                       scale=ln1[:, 7, j:j + 1]).then_inc(res0_ok, 1)

                def context_hi(i, j):
                    act.wait_ge(cx_in[j], 32 * (i + 1))
                    act.activation(ctxt_hi[:, j, :, 0:S], ctxtf[:, j, :, :], ACT.Copy)
                    act.activation(ctx_hi[:, j, :, :], ctxf[0:SB, j, :, :], ACT.Copy).then_inc(cx_hi_ok, 1)

                def x4_high(g):
                    act.wait_ge(x4_ok, g + 1)
                    act.activation(x4_hi[:, :, :, :], x4[:, :, :, :], ACT.Copy).then_inc(x4_hi_ok, 1)

                def h_high(g):
                    for j in range(G):
                        act.wait_ge(t_h, G * g + j + 1)
                        act.activation(h_hi[:, :, j * L:(j + 1) * L], bank[j][:, 0:KB * L].rearrange("p (k t) -> p k t", k=KB),
                                       ACT.Copy).then_inc(h_hi_ok, 1)

                def group(i, last):
                    ev = [G * i + j + 1 for j in range(G)]

                    def qk_high(j):
                        act.wait_ge(qk_f_ok, ev[j])
                        act.activation(op_hi[j][0:L, :], tmp[j][0:L, :], ACT.Copy).then_inc(qk_hi_ok, 1)

                    def exps(j):
                        act.wait_ge(smx_ok, ev[j])
                        for half in range(KB):
                            n = slice(half * D, (half + 1) * D)
                            e = act.activation(tmp[j][:, n], bank[j][:, n], ACT.Exp, bias=smx[:, j, half:half + 1],
                                               accum_out=ssum[:, j, half:half + 1])
                        e.then_inc(exp_ok, 1)

                    def probs_high(j):
                        act.wait_ge(sinv_ok, ev[j])
                        for half in range(KB):
                            n = slice(half * D, (half + 1) * D)
                            w = act.activation(op_hi[j][:, n], tmp[j][:, n], ACT.Copy, scale=sinv[:, j, half:half + 1])
                        w.then_inc(w_hi_ok, 1)

                    def v_high(half):
                        act.wait_ge(v_mm, KB * i + half + 1)
                        act.activation(v_hi[:, half, :], v_bank[half][:, 0:TOK], ACT.Identity,
                                       bias=v_bias[:, half:half + 1]).then_inc(v_hi_ok, 1)

                    def probs_proj_high(j):
                        act.wait_ge(g_mm, ev[j])
                        act.activation(op_hi[j][:, :], bank[j][:, :], ACT.Copy).then_inc(g_hi_ok, 1)

                    def c_high(j):
                        act.wait_ge(t_c, ev[j])
                        tc = bank[j][:, 0:KB * L].rearrange("p (k t) -> p k t", k=KB)
                        act.activation(ct[:, j, :, :], tc, ACT.Copy).then_inc(ct_ok, 1)
                        act.activation(c_hi[:, j, :, :], tc, ACT.Copy).then_inc(c_hi_ok, 1)

                    def c_weighted_high(j):
                        act.wait_ge(ctw_ok, ev[j])
                        act.activation(cw_hi[:, j, :, :], ctw[:, j, :, :], ACT.Copy).then_inc(cw_hi_ok, 1)

                    if not is_first(i):
                        x4_high(i - 1)
                    qk_high(0)
                    qk_high(1)
                    context_hi(i, 3)
                    qk_high(2)
                    qk_high(3)
                    exps(0)
                    probs_high(0)
                    exps(1)
                    exps(2)
                    probs_high(1)
                    exps(3)
                    probs_high(2)
                    probs_high(3)
                    v_high(0)
                    v_high(1)
                    probs_proj_high(0)
                    probs_proj_high(1)
                    probs_proj_high(2)
                    probs_proj_high(3)
                    c_high(0)
                    c_high(1)
                    c_high(2)
                    c_high(3)
                    c_weighted_high(0)
                    c_weighted_high(1)
                    c_weighted_high(2)
                    c_weighted_high(3)
                    for j in range(G):
                        act.wait_ge(smx2_ok, ev[j])
                        act.activation(tmp[j][0:L, 0:S], bank[j][0:L, 0:S], ACT.Exp, bias=smx2[:, j:j + 1],
                                       accum_out=ssum2[:, j:j + 1]).then_inc(exp2_ok, 1)
                    for j in range(G):
                        act.wait_ge(t_a, ev[j])
                        act.activation(op_hi[j][0:SB, 0:NSB * L], bank[j][0:SB, 0:NSB * L], ACT.Copy).then_inc(a_hi_ok, 1)
                    act.wait_ge(mneg_ok, i + 1)
                    act.activation(mexp[:, :], m_bank[0:G, 0:L], ACT.Exp, bias=mneg[:, :], accum_out=msum[:, :]).then_inc(mexp_ok, 1)
                    for j in range(G):
                        act.wait_ge(c2q_mm, ev[j])
                        act.wait_ge(sinv2_ok, ev[j])
                        act.activation(tmp[j][0:L, 0:D], bank[j][0:L, 0:D], ACT.Copy, scale=sinv2[:, j:j + 1]).then_inc(c2q_ok, 1)
                    for j in range(G):
                        act.wait_ge(t_x, ev[j])
                        act.activation(op_hi[j][:, 0:2 * KB * L], bank[j][:, 0:2 * KB * L], ACT.Copy).then_inc(x_hi_ok, 1)
                        if j % 2 and not last:
                            context_hi(i + 1, j // 2)
                        if j == 1 and last:
                            act.wait_ge(shared_in, 48)
                            act.activation(shared_hi[:, 0:GU + D], shared_f[:, :], ACT.Copy).then_inc(shared_hi_ok, 1)
                    if last:
                        x4_high(i)
                        h3_high(act, 0, h3_hi0)
                        copy_logits(act, 0)
                    else:
                        h_high(i + 1)
                        context_hi(i + 1, 2)
                        residual(i + 1)

                act.wait_ge(nwq_ok, 1)
                for k in range(KB):
                    for n, scale in qkv_parts:
                        act.activation(wqkv_hi[:, k, n], wqkv_f[:, k, n], ACT.Copy, scale=scale[:, k:k + 1]).then_inc(w_split, 1)
                context_hi(0, 0)
                h_high(0)
                context_hi(0, 1)
                residual(0)
                act.wait_ge(wpl_in, 32)
                act.activation(wp_hi[:, :, :], wp_f[:, :, :], ACT.Copy)
                act.activation(wl_hi[:, :, :], wl_f[:, :, :], ACT.Copy).then_inc(w2_hi_ok, 1)
                context_hi(0, 2)
                group(0, False)
                with act.Fori(1, NGRP - 1) as i:
                    group(i, False)
                group(NGRP - 1, True)

            @block.gpsimd
            def _(pool):
                def ln1_scalars(g):
                    pool.wait_ge(mv1_ok, G * (g + 1))
                    if not is_first(g):
                        pool.wait_ge(res0_ok, G * g)
                        pool.wait_ge(hh_ok, G * g)
                    mean, var = mv1[:, :, 0], mv1[:, :, 1]
                    row = [ln1[:, n, :] for n in range(10)]
                    done = [0]

                    def step(ins):
                        done[0] += 1
                        ins.then_inc(ln1_step, 1)
                        if done[0] < LN1_STEPS:
                            pool.wait_ge(ln1_step, LN1_STEPS * g + done[0])

                    step(pool.tensor_tensor(row[0], var, eps[:, :], ALU.add))
                    step(pool.tensor_tensor(row[1], row[0], mhalf[:, :], ALU.pow))
                    step(pool.tensor_tensor(row[2], var, row[1], ALU.mult))
                    step(pool.tensor_tensor(row[3], row[2], row[1], ALU.mult))
                    step(pool.tensor_tensor(row[4], row[3], eps[:, :], ALU.add))
                    step(pool.tensor_tensor(row[5], row[4], mhalf[:, :], ALU.pow))
                    step(pool.tensor_tensor(row[6], row[5], row[1], ALU.mult))
                    step(pool.tensor_tensor(row[7], row[1], one[:, :], ALU.add))
                    step(pool.tensor_tensor(row[8], mean, row[1], ALU.mult))
                    step(pool.tensor_tensor(row[9], row[8], mone[:, :], ALU.mult))

                def residual_bias(g):
                    for j in range(G):
                        pool.wait_ge(res0_ok, G * g + j + 1)
                        pool.tensor_tensor(res[:, j, :], res[:, j, :], pb_wide[:, :], ALU.add).then_inc(res_ok, 1)

                def context_lo(i, j):
                    pool.wait_ge(cx_hi_ok, G * i + j + 1)
                    pool.tensor_tensor(ctxt_lo[:, j, :, 0:S], ctxtf[:, j, :, :], f32(ctxt_hi[:, j, :, 0:S]), ALU.subtract)
                    pool.tensor_tensor(ctx_lo[:, j, :, :], ctxf[0:SB, j, :, :], f32(ctx_hi[:, j, :, :]), ALU.subtract).then_inc(cx_lo_ok, 1)

                def group(i, last):
                    ev = [G * i + j + 1 for j in range(G)]
                    for j in range(G):
                        pool.wait_ge(qk_hi_ok, ev[j])
                        pool.tensor_tensor(op_lo[j][0:L, :], tmp[j][0:L, :], f32(op_hi[j][0:L, :]), ALU.subtract).then_inc(qk_lo_ok, 1)
                    context_lo(i, 2)
                    residual_bias(i)
                    context_lo(i, 3)

                    def rstd2(j):
                        pool.wait_ge(mv2_ok, ev[j])
                        pool.tensor_tensor(r2a[:, j:j + 1], mv2[:, j, 1:2], eps[:, j:j + 1], ALU.add).then_inc(r2a_ok, 1)
                        pool.wait_ge(r2a_ok, ev[j])
                        pool.tensor_tensor(r2[:, j:j + 1], r2a[:, j:j + 1], mhalf[:, j:j + 1], ALU.pow).then_inc(r2_ok, 1)

                    def c_weighted(j):
                        pool.wait_ge(ct_ok, ev[j])
                        pool.tensor_tensor(pheld[:, j:j + 1], one[:, 0:1], one[:, 0:1], ALU.add)
                        for k in range(KB):
                            w = pool.tensor_scalar(ctw[:, j, k, :], ct[:, j, k, :], wcq[:, k:k + 1], wq[:, k:k + 1], ALU.mult, ALU.add)
                        w.then_inc(ctw_ok, 1)

                    rstd2(0)
                    rstd2(1)
                    rstd2(2)
                    rstd2(3)
                    c_weighted(0)
                    c_weighted(1)
                    c_weighted(2)
                    c_weighted(3)
                    for j in range(G):
                        pool.wait_ge(c_ok, ev[j])
                        if j == 0:
                            pool.wait_ge(x2_st, 16 * (i + 1))
                        pool.tensor_tensor(x2b[:, j, :], x1[:, j, :], bl_wide[:, :], ALU.add).then_inc(x1b_ok, 1)
                    if not last:
                        ln1_scalars(i + 1)
                        context_lo(i + 1, 0)
                        context_lo(i + 1, 1)
                    else:
                        rstd3(pool, 0)

                pool.wait_ge(consts, 6)
                ln1_scalars(0)
                pool.wait_ge(late_in, 16 * LATE_LOADS)
                context_lo(0, 0)
                context_lo(0, 1)
                group(0, False)
                with pool.Fori(1, NGRP - 1) as i:
                    group(i, False)
                group(NGRP - 1, True)

            @block.vector
            def _(dve):
                def ln1_moments(g):
                    dve.wait_ge(x_in, 16 * (g + 1))
                    if not is_first(g):
                        dve.wait_ge(ln1_step, LN1_STEPS * g)
                    for j in range(G):
                        dve.bn_stats(st1[:, j, :], xt[:, j, :]).then_inc(st1_ok, 1)
                    dve.wait_ge(st1_ok, G * (g + 1))
                    dve.tensor_copy(held[0:L, 0:1], mhalf[:, 0:1])
                    for j in range(G):
                        dve.bn_aggr(mv1[:, j, :], st1[:, j, :]).then_inc(mv1_ok, 1)

                def normalise_h(g):
                    dve.wait_ge(ln1_step, LN1_STEPS * (g + 1))
                    if not is_first(g):
                        dve.wait_ge(t_h, G * g)
                    for j in range(G):
                        dve.tensor_scalar(hh[:, j, :], xt[:, j, :], mv1[:, j, 0:1], ln1[:, 6, j:j + 1], ALU.subtract,
                                          ALU.mult).then_inc(hh_ok, 1)

                def x4_low(g):
                    dve.wait_ge(x4_hi_ok, g + 1)
                    dve.tensor_tensor(x4_lo[:, :, :, :], x4[:, :, :, :], f32(x4_hi[:, :, :, :]), ALU.subtract).then_inc(x4_lo_ok, 1)

                def x2_sum(g, q):
                    dve.wait_ge(x1b_ok, G * (g + 1))
                    dve.wait_ge(z_mm, PAIRS * g + q + 1)
                    dve.tensor_tensor(x2b[:, 2 * q:2 * q + 2, :], z_bank[q][0:L, :].rearrange("p (g d) -> p g d", g=2),
                                      x2b[:, 2 * q:2 * q + 2, :], ALU.add).then_inc(x2_ok, 1)

                def h_low(g):
                    for j in range(G):
                        dve.wait_ge(h_hi_ok, G * g + j + 1)
                        t = slice(j * L, (j + 1) * L)
                        dve.tensor_tensor(h_lo[:, :, t], bank[j][:, 0:KB * L].rearrange("p (k t) -> p k t", k=KB),
                                          f32(h_hi[:, :, t]), ALU.subtract).then_inc(h_lo_ok, 1)

                def group(i, last):
                    ev = [G * i + j + 1 for j in range(G)]

                    def score_max(j):
                        dve.wait_ge(sc_mm, ev[j])
                        dve.reduce_max(smx[:, j, :], bank[j][:, :].rearrange("p (h k) -> p h k", h=KB), AX, negate=True).then_inc(smx_ok, 1)

                    def inv_sum(j):
                        dve.wait_ge(exp_ok, ev[j])
                        dve.reciprocal(sinv[:, j, :], ssum[:, j, :]).then_inc(sinv_ok, 1)

                    def probs_low(j):
                        dve.wait_ge(w_hi_ok, ev[j])
                        for half in range(KB):
                            n = slice(half * D, (half + 1) * D)
                            w = dve.scalar_tensor_tensor(op_lo[j][:, n], tmp[j][:, n], sinv[:, j, half:half + 1], f32(op_hi[j][:, n]),
                                                         ALU.mult, ALU.subtract)
                        w.then_inc(w_lo_ok, 1)

                    def x1_sum(j):
                        dve.wait_ge(ao_mm, ev[j])
                        dve.tensor_tensor(x1[:, j, :], bank[j][0:L, 0:D], res[:, j, :], ALU.add).then_inc(x1_ok, 1)

                    def x1_stats(j):
                        dve.wait_ge(x1_ok, ev[j])
                        dve.bn_stats(st2[:, j, :], x1[:, j, :]).then_inc(st2_ok, 1)

                    def x1_moments(j):
                        dve.wait_ge(st2_ok, ev[j])
                        dve.tensor_copy(held[0:L, 1 + j:2 + j], mhalf[:, 0:1])
                        dve.bn_aggr(mv2[:, j, :], st2[:, j, :]).then_inc(mv2_ok, 1)

                    def c_rows(j):
                        dve.wait_ge(r2_ok, ev[j])
                        dve.wait_ge(mv2_ok, ev[j])
                        dve.tensor_scalar(c[:, j, :], x1[:, j, :], mv2[:, j, 0:1], r2[:, j:j + 1], ALU.subtract, ALU.mult).then_inc(c_ok, 1)

                    def v_low(half):
                        dve.wait_ge(v_hi_ok, KB * i + half + 1)
                        dve.scalar_tensor_tensor(v_lo[:, half, :], v_bank[half][:, 0:TOK], v_bias[:, half:half + 1],
                                                 f32(v_hi[:, half, :]), ALU.add, ALU.subtract).then_inc(v_lo_ok, 1)

                    def probs_proj_low(j):
                        dve.wait_ge(g_hi_ok, ev[j])
                        dve.tensor_tensor(op_lo[j][:, :], bank[j][:, :], f32(op_hi[j][:, :]), ALU.subtract).then_inc(g_lo_ok, 1)

                    def c_low(j):
                        dve.wait_ge(c_hi_ok, ev[j])
                        dve.tensor_tensor(c_lo[:, j, :, :], bank[j][:, 0:KB * L].rearrange("p (k t) -> p k t", k=KB),
                                          f32(c_hi[:, j, :, :]), ALU.subtract).then_inc(c_lo_ok, 1)

                    def c_weighted_low(j):
                        dve.wait_ge(cw_hi_ok, ev[j])
                        dve.tensor_tensor(cw_lo[:, j, :, :], ctw[:, j, :, :], f32(cw_hi[:, j, :, :]), ALU.subtract).then_inc(cw_lo_ok, 1)

                    def qk_biased(j):
                        dve.wait_ge(qk_mm, ev[j])
                        dve.tensor_tensor(tmp[j][0:L, :], bank[j][0:L, :], qk_bias[:, :], ALU.add).then_inc(qk_f_ok, 1)

                    qk_biased(0)
                    qk_biased(1)
                    qk_biased(2)
                    qk_biased(3)
                    score_max(0)
                    if not is_first(i):
                        x4_low(i - 1)
                    inv_sum(0)
                    score_max(1)
                    score_max(2)
                    probs_low(0)
                    inv_sum(1)
                    score_max(3)
                    inv_sum(2)
                    probs_low(1)
                    inv_sum(3)
                    probs_low(2)
                    v_low(0)
                    probs_low(3)
                    v_low(1)
                    probs_proj_low(0)
                    probs_proj_low(1)
                    probs_proj_low(2)
                    probs_proj_low(3)
                    dve.wait_ge(res_ok, G * (i + 1))
                    x1_sum(0)
                    x1_sum(1)
                    x1_stats(0)
                    x1_stats(1)
                    x1_moments(0)
                    x1_sum(2)
                    x1_moments(1)
                    x1_sum(3)
                    x1_stats(2)
                    c_rows(0)
                    x1_moments(2)
                    x1_stats(3)
                    c_rows(1)
                    x1_moments(3)
                    c_low(0)
                    c_rows(2)
                    c_rows(3)
                    if not is_first(i):
                        x2_sum(i - 1, 0)
                    c_low(1)
                    c_low(2)
                    c_low(3)
                    c_weighted_low(0)
                    c_weighted_low(1)
                    c_weighted_low(2)
                    if not is_first(i):
                        x2_sum(i - 1, 1)
                    c_weighted_low(3)
                    for j in range(G):
                        dve.wait_ge(s_mm, ev[j])
                        dve.reduce_max(smx2[:, j:j + 1], bank[j][0:L, 0:S], AX, negate=True).then_inc(smx2_ok, 1)
                        dve.wait_ge(c_ok, ev[j])
                        if j:
                            dve.wait_ge(rdot_ok, ev[j - 1])
                        dve.scalar_tensor_tensor(cwc[:, :], c[:, j, :], 1.0, wc_wide[:, :], ALU.mult, ALU.mult,
                                                 accum_out=rdot[:, j:j + 1]).then_inc(rdot_ok, 1)
                    for j in range(G):
                        dve.wait_ge(smx2_ok, ev[j])
                        dve.wait_ge(rdot_ok, ev[j])
                        dve.scalar_tensor_tensor(m4[:, j:j + 1], rdot[:, j:j + 1], b_sum[:, 0:1], smx2[:, j:j + 1], ALU.add,
                                                 ALU.subtract).then_inc(m4_ok, 1)
                        dve.wait_ge(exp2_ok, ev[j])
                        dve.reciprocal(sinv2[:, j:j + 1], ssum2[:, j:j + 1]).then_inc(sinv2_ok, 1)
                    for j in range(G):
                        if j == 1:
                            dve.wait_ge(t_m, i + 1)
                            dve.reduce_max(mneg[:, :], m_bank[0:G, 0:L], AX, negate=True).then_inc(mneg_ok, 1)
                        dve.wait_ge(a_hi_ok, ev[j])
                        dve.tensor_tensor(op_lo[j][0:SB, 0:NSB * L], bank[j][0:SB, 0:NSB * L], f32(op_hi[j][0:SB, 0:NSB * L]),
                                          ALU.subtract).then_inc(a_lo_ok, 1)
                    dve.wait_ge(mexp_ok, i + 1)
                    dve.reciprocal(minv[:, :], msum[:, :]).then_inc(minv_ok, 1)
                    dve.wait_ge(minv_ok, i + 1)
                    dve.tensor_scalar(mrow[:, :], mexp[:, :], minv[:, 0:1], None, ALU.mult).then_inc(mrow_ok, 1)
                    for j in range(G):
                        dve.wait_ge(c2q_ok, ev[j])
                        dve.tensor_tensor(tmp[j][0:L, D:2 * D], tmp[j][0:L, 0:D], c[:, j, :], ALU.mult).then_inc(x3_ok, 1)
                        if j == 0 and last:
                            moments3(dve, 0)
                        elif j == 0:
                            ln1_moments(i + 1)
                        if j == 1:
                            dve.wait_ge(t_b, i + 1)
                            dve.tensor_copy(b4[:, :], m_bank[0:L, P:P + G]).then_inc(b4_ok, 1)
                            dve.wait_ge(b4_ok, i + 1)
                            dve.tensor_tensor(bm[:, :, :], diag[:, :, :], b4[:, :].unsqueeze(2).to_broadcast([L, G, G]),
                                              ALU.mult).then_inc(bm_ok, 1)
                    for j in range(G):
                        dve.wait_ge(x_hi_ok, ev[j])
                        dve.tensor_tensor(op_lo[j][:, 0:2 * KB * L], bank[j][:, 0:2 * KB * L], f32(op_hi[j][:, 0:2 * KB * L]),
                                          ALU.subtract).then_inc(x_lo_ok, 1)
                        if j == 1:
                            dve.wait_ge(q2c_mm, i + 1)
                            dve.tensor_copy(q2c_row[:, :], m_bank[0:G, D:2 * D]).then_inc(q2cr_ok, 1)
                    if not last:
                        normalise_h(i + 1)
                    dve.wait_ge(t_q, i + 1)
                    dve.tensor_copy(q2c[:, :, :], m_bank[:, 0:KB * G].rearrange("p (k g) -> p k g", k=KB)).then_inc(q2c_ok, 1)
                    if not last:
                        h_low(i + 1)
                    dve.wait_ge(q2c_ok, i + 1)
                    for k in range(KB):
                        w = dve.tensor_tensor(x4[:, :, k, :], ct[:, :, k, :], q2c[:, k, :].unsqueeze(2).to_broadcast([P, G, L]), ALU.mult)
                    w.then_inc(x4_ok, 1)
                    if last:
                        normalise3(dve, 0)
                        x4_low(i)
                        h3_low(dve, 0, h3_hi0, h3_lo0)
                        dve.wait_ge(shared_hi_ok, 1)
                        dve.tensor_tensor(shared_lo[:, 0:GU + D], shared_f[:, :], f32(shared_hi[:, 0:GU + D]), ALU.subtract).then_inc(shared_lo_ok, 1)
                        x2_sum(i, 0)
                        x2_sum(i, 1)

                dve.memset(mhalf[:, :], -0.5).then_inc(consts, 1)
                dve.memset(eps[:, :], LN_EPS).then_inc(consts, 1)
                dve.memset(one[:, :], 1.0).then_inc(consts, 1)
                dve.memset(mone[:, :], -1.0).then_inc(consts, 1)
                dve.memset(mhalf2[:, :], -0.5).then_inc(half_ok, 1)
                dve.memset(eps2[:, :], LN_EPS).then_inc(half_ok, 1)
                dve.memset(held[:, 0:1], 0.0).then_inc(x2_st, 16)
                dve.wait_ge(x2_st, 16)
                dve.memset(held[:, 0:1], 0.0).then_inc(x2_ok, PAIRS)
                dve.wait_ge(x2_ok, PAIRS)
                dve.memset(f32(ctxt_hi[:, :, :, S:SP_]), 0.0).then_inc(consts, 1)
                dve.memset(f32(ctxt_lo[:, :, :, S:SP_]), 0.0).then_inc(consts, 1)
                dve.wait_ge(consts, 6)
                ln1_moments(0)
                dve.wait_ge(w_in, 16 * QKV_LOADS)
                dve.tensor_copy(nb_wide[:, :, :], nb[:, :].unsqueeze(2).to_broadcast([P, KB, L])).then_inc(wide, 1)
                dve.tensor_scalar(nwq[:, :], nw[:, :], ATT_SCALE, None, ALU.mult).then_inc(nwq_ok, 1)
                dve.wait_ge(nwq_ok, 1)
                normalise_h(0)
                dve.wait_ge(w_split, QKV_SPLITS // 2)
                for k in range(KB):
                    for n, scale in qkv_parts:
                        dve.scalar_tensor_tensor(wqkv_lo[:, k, n], wqkv_f[:, k, n], scale[:, k:k + 1], f32(wqkv_hi[:, k, n]),
                                                 ALU.mult, ALU.subtract).then_inc(w_split, 1)
                dve.wait_ge(bias_mm, 1)
                dve.tensor_tensor(qk_bias[:, :], m_bank[0:L, :], qk_bias0[:, :], ALU.add).then_inc(qk_bias_ok, 1)
                dve.tensor_tensor(v_bias[:, :], v_bank[1][:, 0:KB], v_bias0[:, :], ALU.add).then_inc(bias_ok, 1)
                dve.wait_ge(qk_bias_ok, 1)
                dve.tensor_scalar(qk_bias[:, 0:D], qk_bias[:, 0:D], ATT_SCALE, None, ALU.mult).then_inc(bias_ok, 1)
                h_low(0)
                dve.wait_ge(bias_ok, 2)
                dve.wait_ge(w2_hi_ok, 1)
                dve.tensor_tensor(wp_lo[:, :, :], wp_f[:, :, :], f32(wp_hi[:, :, :]), ALU.subtract).then_inc(w2_split, 1)
                dve.tensor_tensor(wl_lo[:, :, :], wl_f[:, :, :], f32(wl_hi[:, :, :]), ALU.subtract).then_inc(w2_split, 1)
                dve.wait_ge(late_in, 16 * LATE_LOADS)
                dve.reduce_sum(b_sum[:, :], b3[:, :], AX).then_inc(b_sum_ok, 1)
                dve.wait_ge(b_sum_ok, 1)
                dve.wait_ge(gate_in, 16)
                dve.tensor_copy(gate[:, :, 0:NEXP], gate_f[:, :, :]).then_inc(gate_hi_ok, 1)
                dve.wait_ge(gate_hi_ok, 1)
                dve.tensor_tensor(gate[:, :, NEXP:2 * NEXP], gate_f[:, :, :], f32(gate[:, :, 0:NEXP]), ALU.subtract).then_inc(gate_ok, 1)
                group(0, False)
                with dve.Fori(1, NGRP - 1) as i:
                    group(i, False)
                group(NGRP - 1, True)

        with ExitStack() as c2:
            def sb(name, shape, dt=F32):
                return c2.enter_context(nc.sbuf_tensor(name, shape, dt))

            def sem(name):
                return c2.enter_context(nc.semaphore(name))

            g_bank, u_bank, y_bank = bank[0:2], bank[2:4], bank[4:6]
            ORDER = [NEXP] + list(range(NEXP))
            AHEAD = 2

            w_f = [sb(f"w_f{e}", [P, GU + D]) for e in range(NEXP)]
            w_hi = [sb(f"w_hi{e}", [P, GU + D], F32R) for e in range(NEXP)] + [shared_hi]
            w_lo = [sb(f"w_lo{e}", [P, GU + D], F32R) for e in range(NEXP)] + [shared_lo]

            x2t = [sb(f"x2t{p}", [P, T, D]) for p in range(2)]
            h3_hi = [h3_hi0, sb("h3_hi1", [P, KB, FFN_TOKENS], F32R)]
            h3_lo = [h3_lo0, sb("h3_lo1", [P, KB, FFN_TOKENS], F32R)]
            lg2 = sb("lg2", [P, T, 2 * NEXP])
            lg, den, score, scorec, choice, wsel, cw = (sb(n, [P, T, NEXP]) for n in ("lg", "den", "score", "scorec", "choice", "wsel", "cw"))
            gsum, grank, gmask = (sb(n, [P, T, 4]) for n in ("gsum", "grank", "gmask"))
            g_gt, g_eq = sb("g_gt", [P, T, 4, 4]), sb("g_eq", [P, T, 4, 4])
            e_gt, e_eq = sb("e_gt", [P, T, 8, 8]), sb("e_eq", [P, T, 8, 8])
            erank, wsum, winv = sb("erank", [P, T, NEXP]), sb("wsum", [P, T]), sb("winv", [P, T])
            cwt = sb("cwt", [NEXP, FFN_TOKENS])
            cw_wide = [sb(f"cw_wide{p}", [P, NEXP, FFN_TOKENS]) for p in range(2)]
            sg = [sb(f"sg{b}", [P, FFN_TOKENS]) for b in range(2)]
            af = [sb(f"af{b}", [P, FFN_TOKENS]) for b in range(2)]
            a_hi = [sb(f"a_hi{b}", [P, FFN_TOKENS], F32R) for b in range(AHEAD + 1)]
            a_lo = [sb(f"a_lo{b}", [P, FFN_TOKENS], F32R) for b in range(AHEAD + 1)]

            wx_in = [sem(f"expert{e}_in") for e in range(NEXP)]
            x2_in = [sem(f"x2_{p}_in") for p in range(2)]
            out_st = sem("out_stored")
            w_hi_ok, w_lo_ok = sem("expert_hi"), sem("expert_lo")
            t_lg, lg2_ok, lg_ok, eneg_ok = sem("logits_transposed"), sem("logits_halves"), sem("logits_ready"), sem("logits_exp")
            route = sem("routing_step")
            t_cw, cwt_ok, cw_st, cw_in = sem("cw_transposed"), sem("cw_copied"), sem("cw_stored"), sem("cw_in")
            gu_mm, sg_ok, sgw_ok, af_ok, a_hi_ok, a_lo_ok = sem("gate_up_product"), sem("silu_ready"), sem("silu_weighted"), sem("act_ready"), sem("act_hi"), sem("act_lo")
            y_mm, out_ok = sem("down_product"), sem("out_ready")

            out_g = out.rearrange("b l d -> (b l) d").rearrange("(t p) d -> p t d", p=P)
            ROUTE_STEPS = 23

            block = c2.enter_context(nc.Block())

            @block.sync
            def _(sp):
                def load_x2(g, p):
                    sp.dma_start(x2t[p][:, :, :], x2_g[:, bass.ds(T * g, T), :]).then_inc(x2_in[p], 16)

                def spread_cw(g, p):
                    sp.wait_ge(cwt_ok, g + 1)
                    sp.dma_start(cw_dram[p], cwt[:, :]).then_inc(cw_st, 16)
                    sp.wait_ge(cw_st, 16 * (g + 1))
                    sp.dma_start(cw_wide[p][:, :, :], cw_dram[p].partition_broadcast(P)).then_inc(cw_in, 16)

                def store(g, p):
                    sp.wait_ge(out_ok, 2 * (g + 1))
                    sp.wait_ge(wk_in, 48)
                    sp.dma_start(out_g[:, bass.ds(T * g, T), :], x2t[p][:, :, :]).then_inc(out_st, 16)

                load_norm(sp, 1)
                for e in range(NEXP):
                    for half, w in enumerate((wg, wu)):
                        sp.dma_start(gate_up_weights(w_f[e])[:, half, :, :], w[e].rearrange("(k p) n -> p k n", p=P)).then_inc(wx_in[e], 16)
                    sp.dma_start(w_f[e][:, GU:GU + D], wd[e]).then_inc(wx_in[e], 16)
                sp.wait_ge(x2_st, 16 * (NGRP + 1))
                load_x2(0, 0)
                spread_cw(0, 0)

                def group(g, p, more):
                    if not is_first(g):
                        store(g - 1, 1 - p)
                        sp.wait_ge(out_st, 16 * g)
                        sp.wait_ge(wk_in, 48)
                    load_x2(g + 1, 1 - p)
                    if more:
                        sp.wait_ge(h3_ok, T * (g + 2))
                        sp.wait_ge(wk_in, 48)
                        load_norm(sp, g + 2)
                    spread_cw(g + 1, 1 - p)

                group(0, 0, True)
                with sp.Fori(0, NG2 // 2 - 1) as it:
                    group(2 * it + 1, 1, True)
                    group(2 * it + 2, 0, True)
                group(NG2 - 2, 1, False)
                store(NG2 - 2, 1)
                store(NG2 - 1, 0)
                sp.wait_ge(out_st, 16 * NG2)

            @block.tensor
            def _(pe):
                def turn_logits(g):
                    for t in range(T):
                        last = pe.transpose(h_bank[1][:, t * 2 * NEXP:(t + 1) * 2 * NEXP], lgt[:, t * P:(t + 1) * P],
                                            ident[0:2 * NEXP, 0:2 * NEXP])
                    last.then_inc(t_lg, 1)

                def turn_cw(g):
                    pe.wait_ge(route, ROUTE_STEPS * (g + 1))
                    for t in range(T):
                        last = pe.transpose(h_bank[0][0:NEXP, t * P:(t + 1) * P], cw[:, t, :], ident[:, :])
                    last.then_inc(t_cw, 1)

                def gate_up(g, p, n):
                    e, b = ORDER[n], (p + n) % 2
                    if n >= 2 or not is_first(g):
                        pe.wait_ge(af_ok, NE * g + n - 1)
                    if is_first(g) and n:
                        pe.wait_ge(w_lo_ok, n)
                    for half, dst in enumerate((g_bank[b], u_bank[b])):
                        for k in range(KB):
                            last = mm3(pe, dst[:, :], gate_up_weights(w_hi[e])[:, half, k, :], gate_up_weights(w_lo[e])[:, half, k, :], h3_hi[p][:, k, :],
                                       h3_lo[p][:, k, :], k == 0, k == KB - 1)
                        last.then_inc(gu_mm, 1)

                def down(g, n):
                    e, b = ORDER[n], n % (AHEAD + 1)
                    pe.wait_ge(a_lo_ok, NE * g + n + 1)
                    if n == 0 and not is_first(g):
                        pe.wait_ge(out_ok, 2 * g)
                    for t in range(T):
                        s = slice(t * P, (t + 1) * P)
                        last = mm3(pe, y_bank[t // 2][:, (t % 2) * D:(t % 2 + 1) * D], a_hi[b][:, s], a_lo[b][:, s], w_hi[e][:, GU:GU + D],
                                   w_lo[e][:, GU:GU + D], n == 0 and t % 2 == 0, n == NE - 1, skip_group_check=True)
                    if n == NE - 1:
                        last.then_inc(y_mm, 1)

                def group(g, p, last):
                    for n in range(NE):
                        gate_up(g, p, n)
                        if n == 1 and is_first(g):
                            turn_cw(0)
                            pe.wait_ge(cwt_ok, 1)
                        if not last:
                            if n == 3:
                                pe.wait_ge(lgt_ok, g + 2)
                        if n >= AHEAD:
                            down(g, n - AHEAD)
                        elif not is_first(g):
                            down(g - 1, NE + n - AHEAD)
                        if n == 1 and not last:
                            turn_h3(pe, g + 1)
                        if n == 6 and not last:
                            turn_cw(g + 1)
                        if n == 2 and not last:
                            logits(pe, g + 1, h3_hi[1 - p], h3_lo[1 - p])
                        if n == 3 and not last:
                            turn_logits(g + 1)

                turn_logits(0)
                group(0, 0, False)
                with pe.Fori(0, NG2 // 2 - 1) as it:
                    group(2 * it + 1, 1, False)
                    group(2 * it + 2, 0, False)
                group(NG2 - 2, 1, False)
                group(NG2 - 1, 0, True)
                for n in range(NE - AHEAD, NE):
                    down(NG2 - 1, n)

            @block.scalar
            def _(act):
                def exp_logits(g):
                    act.wait_ge(lg_ok, g + 1)
                    act.activation(den[:, :, :], lg[:, :, :], ACT.Exp, scale=-1.0).then_inc(eneg_ok, 1)

                def copy_cw(g):
                    act.wait_ge(t_cw, g + 1)
                    if not is_first(g):
                        act.wait_ge(cw_st, 16 * g)
                    act.activation(cwt[:, :], h_bank[0][0:NEXP, :], ACT.Copy).then_inc(cwt_ok, 1)

                def split_high(n):
                    e = ORDER[n]
                    act.wait_ge(wx_in[e], 48)
                    act.activation(w_hi[e][:, :], w_f[e][:, :], ACT.Copy).then_inc(w_hi_ok, 1)

                def expert(g, p, n):
                    b = (p + n) % 2
                    act.wait_ge(gu_mm, 2 * (NE * g + n) + 1)
                    act.activation(sg[b][:, :], g_bank[b][:, :], ACT.Silu).then_inc(sg_ok, 1)

                def act_high(g, p, n):
                    act.wait_ge(af_ok, NE * g + n + 1)
                    act.activation(a_hi[n % (AHEAD + 1)][:, :], af[(p + n) % 2][:, :], ACT.Copy).then_inc(a_hi_ok, 1)

                def group(g, p, last):
                    for n in range(NE):
                        expert(g, p, n)
                        if is_first(g):
                            if n == 0:
                                copy_cw(0)
                            if n + 3 < NE:
                                split_high(n + 3)
                        if not last:
                            if n == 1:
                                h3_high(act, g + 1, h3_hi[1 - p])
                            if n == 6:
                                copy_cw(g + 1)
                        act_high(g, p, n)
                        if not last:
                            if n == 2:
                                copy_logits(act, g + 1)
                            if n == 3:
                                exp_logits(g + 1)

                exp_logits(0)
                split_high(1)
                split_high(2)
                group(0, 0, False)
                with act.Fori(0, NG2 // 2 - 1) as it:
                    group(2 * it + 1, 1, False)
                    group(2 * it + 2, 0, False)
                group(NG2 - 2, 1, False)
                group(NG2 - 1, 0, True)

            @block.gpsimd
            def _(pool):
                def expert(g, p, n):
                    b = (p + n) % 2
                    pool.wait_ge(sg_ok, NE * g + n + 1)
                    if n == 1:
                        pool.wait_ge(cw_in, 16 * (g + 1))
                    pool.tensor_tensor(sg[b][:, :], sg[b][:, :], cw_wide[p][:, ORDER[n], :], ALU.mult).then_inc(sgw_ok, 1)

                def group(g, p, last):
                    if not last:
                        rstd3(pool, g + 1)
                    for n in range(1, NE):
                        expert(g, p, n)

                with pool.Fori(0, NG2 // 2) as it:
                    group(2 * it, 0, False)
                    group(2 * it + 1, 1, False)
                group(NG2 - 1, 0, True)

            @block.vector
            def _(dve):
                def sum_logits(g):
                    dve.wait_ge(t_lg, g + 1)
                    dve.tensor_copy(lg2[:, :, :], h_bank[1][:, 0:T * 2 * NEXP].rearrange("p (t n) -> p t n", t=T)).then_inc(lg2_ok, 1)
                    dve.wait_ge(lg2_ok, g + 1)
                    dve.tensor_tensor(lg[:, :, :], lg2[:, :, 0:NEXP], lg2[:, :, NEXP:2 * NEXP], ALU.add).then_inc(lg_ok, 1)

                halves = scorec[:, :, :].rearrange("p t (a b) -> p t a b", b=2)

                def stepper(g, done):
                    def step(ins):
                        nonlocal done
                        done += 1
                        ins.then_inc(route, 1)
                        dve.wait_ge(route, ROUTE_STEPS * g + done)
                    return step

                def pairs(a, n, axis):
                    return a.unsqueeze(axis).to_broadcast([P, T, n, n])

                def route_groups(g):
                    step = stepper(g, 0)
                    dve.wait_ge(eneg_ok, g + 1)
                    if not is_first(g):
                        dve.wait_ge(t_cw, g)
                    step(dve.tensor_scalar(den[:, :, :], den[:, :, :], 1.0, None, ALU.add))
                    step(dve.reciprocal(score[:, :, :], den[:, :, :]))
                    step(dve.tensor_tensor(scorec[:, :, :], score[:, :, :], corr_w[:, :].unsqueeze(1).to_broadcast([P, T, NEXP]), ALU.add))
                    step(dve.tensor_tensor(gsum[:, :, :], halves[:, :, :, 0], halves[:, :, :, 1], ALU.add))
                    mine, other = pairs(gsum[:, :, :], 4, 3), pairs(gsum[:, :, :], 4, 2)
                    step(dve.tensor_tensor(g_gt[:, :, :, :], other, mine, ALU.is_gt))
                    step(dve.tensor_tensor(g_eq[:, :, :, :], other, mine, ALU.is_equal))
                    step(dve.tensor_tensor(g_eq[:, :, :, :], g_eq[:, :, :, :], tri4[:, :, :].unsqueeze(1).to_broadcast([P, T, 4, 4]), ALU.mult))
                    step(dve.tensor_tensor(g_gt[:, :, :, :], g_gt[:, :, :, :], g_eq[:, :, :, :], ALU.add))
                    step(dve.reduce_sum(grank[:, :, :], g_gt[:, :, :, :], AX))
                    step(dve.tensor_scalar(gmask[:, :, :], grank[:, :, :], 2.0, None, ALU.is_lt))
                    step(dve.tensor_tensor(choice[:, :, :].rearrange("p t (a b) -> p t a b", b=2), halves,
                                           gmask[:, :, :].unsqueeze(3).to_broadcast([P, T, 4, 2]), ALU.mult))

                def route_experts(g):
                    step = stepper(g, 11)
                    mine, other = pairs(choice[:, :, :], 8, 3), pairs(choice[:, :, :], 8, 2)
                    step(dve.tensor_tensor(e_gt[:, :, :, :], other, mine, ALU.is_gt))
                    step(dve.tensor_tensor(e_eq[:, :, :, :], other, mine, ALU.is_equal))
                    step(dve.tensor_tensor(e_eq[:, :, :, :], e_eq[:, :, :, :], tri8[:, :, :].unsqueeze(1).to_broadcast([P, T, 8, 8]), ALU.mult))
                    step(dve.tensor_tensor(e_gt[:, :, :, :], e_gt[:, :, :, :], e_eq[:, :, :, :], ALU.add))
                    step(dve.reduce_sum(erank[:, :, :], e_gt[:, :, :, :], AX))
                    step(dve.tensor_scalar(erank[:, :, :], erank[:, :, :], 4.0, None, ALU.is_lt))
                    step(dve.tensor_tensor(wsel[:, :, :], score[:, :, :], erank[:, :, :], ALU.mult))
                    step(dve.reduce_sum(wsum[:, :], wsel[:, :, :], AX))
                    step(dve.tensor_scalar(wsum[:, :], wsum[:, :], ROUTE_TINY, None, ALU.add))
                    step(dve.reciprocal(winv[:, :], wsum[:, :]))
                    step(dve.tensor_tensor(wsel[:, :, :], wsel[:, :, :], winv[:, :].unsqueeze(2).to_broadcast([P, T, NEXP]), ALU.mult))
                    step(dve.tensor_scalar(cw[:, :, :], wsel[:, :, :], EXPERT_SCALE, None, ALU.mult))

                def product(g, p, n):
                    b = (p + n) % 2
                    dve.wait_ge(gu_mm, 2 * (NE * g + n) + 2)
                    if n == 0:
                        dve.wait_ge(sg_ok, NE * g + 1)
                    else:
                        dve.wait_ge(sgw_ok, NEXP * g + n)
                    dve.tensor_tensor(af[b][:, :], u_bank[b][:, :], sg[b][:, :], ALU.mult).then_inc(af_ok, 1)

                def act_low(g, p, n):
                    b = n % (AHEAD + 1)
                    dve.wait_ge(a_hi_ok, NE * g + n + 1)
                    dve.tensor_tensor(a_lo[b][:, :], af[(p + n) % 2][:, :], f32(a_hi[b][:, :]), ALU.subtract).then_inc(a_lo_ok, 1)

                def finish(g, p, nth):
                    dve.wait_ge(y_mm, g + 1)
                    dve.wait_ge(x2_in[p], 16 * nth)
                    for q in range(2):
                        x2q = x2t[p][:, 2 * q:2 * q + 2, :]
                        dve.tensor_tensor(x2q, y_bank[q][:, :].rearrange("p (t d) -> p t d", t=2), x2q, ALU.add).then_inc(out_ok, 1)

                def split_low(n):
                    e = ORDER[n]
                    dve.wait_ge(w_hi_ok, n)
                    dve.tensor_tensor(w_lo[e][:, :], w_f[e][:, :], f32(w_hi[e][:, :]), ALU.subtract).then_inc(w_lo_ok, 1)

                def group(g, p, nth, last):
                    if not last:
                        moments3(dve, g + 1)
                    for n in range(NE):
                        if is_first(g) and n + 2 < NE:
                            split_low(n + 2)
                        product(g, p, n)
                        if n == 1 and not is_first(g):
                            finish(g - 1, 1 - p, nth)
                        if not last:
                            if n == 1:
                                h3_low(dve, g + 1, h3_hi[1 - p], h3_lo[1 - p])
                            if n == 0:
                                normalise3(dve, g + 1)
                        act_low(g, p, n)
                        if n == 3 and not last:
                            sum_logits(g + 1)
                            route_groups(g + 1)
                        if n == 4 and not last:
                            route_experts(g + 1)

                dve.wait_ge(wk_in, 48)
                sum_logits(0)
                route_groups(0)
                split_low(1)
                route_experts(0)
                group(0, 0, None, False)
                with dve.Fori(0, NG2 // 2 - 1) as it:
                    group(2 * it + 1, 1, it + 1, False)
                    group(2 * it + 2, 0, it + 1, False)
                group(NG2 - 2, 1, NG2 // 2, False)
                group(NG2 - 1, 0, NG2 // 2, True)
                finish(NG2 - 1, 0, NG2 // 2 + 1)


def kernel(**inputs):
    import concourse.bacc as bacc
    from concourse.bass_utils import run_bass_kernel_spmd

    a = {k: np.asarray(v) for k, v in inputs.items()}
    D = a["x"].shape[2]
    att, xat, ffn = (lambda n, p=p: a[f"L0_{p}_{n}"] for p in ("attn", "xattn", "ffn"))

    def columns(v):
        return v.reshape(-1, P).T

    arrays = {
        "x": a["x"], "ctx": a["ctx_1024"], "ctx_t": a["ctx_1024"].transpose(0, 2, 1),
        "norm_w": columns(att("norm_w")), "norm_b": columns(att("norm_b")), "qkv_wt": att("qkv_w").T,
        "qk_b": att("qkv_b")[:2 * D], "v_b": columns(att("qkv_b")[2 * D:]),
        "proj_wt": att("proj_w").T, "proj_b": att("proj_b"),
        "w_cq": columns(xat("w_cq")), "b_cq": xat("b_cq").reshape(1), "w_c": xat("w_c"), "b_c": xat("b_c").reshape(1),
        "w_q": columns(xat("w_q")), "b_q": xat("b_q").reshape(1), "wl_t": xat("W_l").T, "b_l": xat("b_l"),
        "gate_t": ffn("gate_w").T, "corr": ffn("correction_bias"), "wg": ffn("Wg"), "wu": ffn("Wu"), "wd": ffn("Wd"),
        "wg_s": ffn("Wg_s"), "wu_s": ffn("Wu_s"), "wd_s": ffn("Wd_s"),
        "ident_in": np.eye(P, dtype=np.float32), "tri8_in": np.tri(8, 8, -1, dtype=np.float32),
        "tri4_in": np.tri(4, 4, -1, dtype=np.float32), "diag_in": np.eye(STREAMS, dtype=np.float32),
    }
    nc = bacc.Bacc("TRN2", target_bir_lowering=False, num_devices=1)
    arrays = {k: np.ascontiguousarray(v) for k, v in arrays.items()}
    aps = {k: nc.dram_tensor(f"in_{k}", v.shape, mybir.dt.from_np(v.dtype), kind="ExternalInput").ap() for k, v in arrays.items()}
    out = nc.dram_tensor("out_dram", a["x"].shape, F32, kind="ExternalOutput").ap()
    decoder_layer(nc, **aps, out=out)
    r = run_bass_kernel_spmd(nc, [{f"in_{k}": v for k, v in arrays.items()}], core_ids=[0])
    return r.results[0]["out_dram"]
```
